# Optimizing a Trainium2 kernel written in Bass

```python
import numpy as np
import jax
import jax.numpy as jnp

def _softmax(x, axis=-1):
    return jax.nn.softmax(x, axis=axis)

def _gelu(x):
    return jax.nn.gelu(x, approximate=True)

def _silu(x):
    return jax.nn.silu(x)

def _sigmoid(x):
    return jax.nn.sigmoid(x)

def _layernorm(x, axis=-1, eps=1e-05):
    m = jnp.mean(x, axis=axis, keepdims=True)
    v = jnp.var(x, axis=axis, keepdims=True)
    return (x - m) / jnp.sqrt(v + eps)

def _scatter_add(tgt, idx, src, axis=0):
    return tgt.at[idx].add(src)

def _segment_sum(src, seg, n):
    return jax.ops.segment_sum(src, seg, n)
kernel_name = 'mk_seq_postln_d2_jaxref_r4_cda25b'

def setup_inputs(seed: int=0):
    np.random.seed(seed)
    _w = jnp.asarray

    def _L0_attn_setup():
        import jax, jax.numpy as jnp
        import numpy as np
        import math
        D_MODEL = 256
        N_HEADS = 16
        HEAD_DIM = D_MODEL // N_HEADS
        CTX_LEN = 256
        POOL_OUT = 64

        def _heads(x):
            B, S, _ = x.shape
            return x.reshape(B, S, N_HEADS, HEAD_DIM)

        def _cross_attn(seq, ctx, Wq, Wk, Wv, Wo):
            B, S, _ = seq.shape
            Q = _heads(seq @ Wq)
            K = _heads(ctx @ Wk)
            V = _heads(ctx @ Wv)
            scale = 1.0 / math.sqrt(HEAD_DIM)
            scores = jnp.einsum('bqhd,bkhd->bhqk', Q, K) * scale
            probs = jax.nn.softmax(scores, axis=-1)
            out = jnp.einsum('bhqk,bkhd->bqhd', probs, V).reshape(B, S, D_MODEL)
            return out @ Wo

        def _causal_self_attn(x, Wq, Wk, Wv, Wo):
            B, S, _ = x.shape
            Q = _heads(x @ Wq)
            K = _heads(x @ Wk)
            V = _heads(x @ Wv)
            scale = 1.0 / math.sqrt(HEAD_DIM)
            scores = jnp.einsum('bqhd,bkhd->bhqk', Q, K) * scale
            causal = jnp.tril(jnp.ones((S, S), dtype=bool))
            scores = jnp.where(causal[None, None], scores, -jnp.inf)
            probs = jax.nn.softmax(scores, axis=-1)
            out = jnp.einsum('bhqk,bkhd->bqhd', probs, V).reshape(B, S, D_MODEL)
            return out @ Wo
        key = jax.random.key(seed)
        ks = jax.random.split(key, 8)
        s = 1.0 / math.sqrt(D_MODEL)
        return {'hidden_states': jax.random.normal(ks[0], (2, 4096, D_MODEL), dtype=jnp.float32), 'Wq': jax.random.normal(ks[1], (D_MODEL, D_MODEL), dtype=jnp.float32) * s, 'Wk': jax.random.normal(ks[2], (D_MODEL, D_MODEL), dtype=jnp.float32) * s, 'Wv': jax.random.normal(ks[3], (D_MODEL, D_MODEL), dtype=jnp.float32) * s, 'Wo': jax.random.normal(ks[4], (D_MODEL, D_MODEL), dtype=jnp.float32) * s, 'W1': jax.random.normal(ks[5], (D_MODEL, D_MODEL // 2), dtype=jnp.float32) * s, 'b1': jnp.zeros((D_MODEL // 2,), dtype=jnp.float32), 'W2': jax.random.normal(ks[6], (D_MODEL // 2, D_MODEL), dtype=jnp.float32) * (1.0 / math.sqrt(D_MODEL // 2)), 'b2': jnp.zeros((D_MODEL,), dtype=jnp.float32)}
    _L0_attn_in = _L0_attn_setup()

    def _L0_ffn_setup():
        import jax, jax.numpy as jnp
        import numpy as np
        B, S, D, H, E = (8, 1024, 256, 512, 8)
        key = jax.random.key(seed)
        ks = jax.random.split(key, 7)
        scale = 0.02
        return {'x': jax.random.normal(ks[0], (B, S, D), dtype=jnp.float32), 'W1': jax.random.normal(ks[1], (E, D, H), dtype=jnp.float32) * scale, 'b1': jnp.zeros((E, H), dtype=jnp.float32), 'W2': jax.random.normal(ks[2], (E, H, D), dtype=jnp.float32) * scale, 'b2': jnp.zeros((E, D), dtype=jnp.float32), 'Wg': jax.random.normal(ks[3], (D, E), dtype=jnp.float32) * scale, 'bg': jnp.zeros((E,), dtype=jnp.float32)}
    _L0_ffn_in = _L0_ffn_setup()

    def _L1_attn_setup():
        import jax, jax.numpy as jnp
        import numpy as np
        INF = 1000000000.0
        D = 256
        key = jax.random.key(seed)
        k_enc, k_r = jax.random.split(key)
        encoding = jax.random.normal(k_enc, (8, 512, D), dtype=jnp.float32)
        R = jax.random.normal(k_r, (D, D), dtype=jnp.float32) / D
        return {'encoding': encoding, 'R': R}
    _L1_attn_in = _L1_attn_setup()

    def _L1_ffn_setup():
        import jax, jax.numpy as jnp
        import numpy as np
        import math
        BETA = 0.9
        THRESHOLD = 1.0
        NUM_STEPS = 5
        ALPHA = 2.0

        @jax.custom_vjp
        def spike_fn(u):
            return (u > 0).astype(u.dtype)

        def _spike_fwd(u):
            return (spike_fn(u), u)

        def _spike_bwd(u, g):
            s = jnp.pi / 2.0 * ALPHA * u
            return (g * (ALPHA / 2.0) / (1.0 + s * s),)
        spike_fn.defvjp(_spike_fwd, _spike_bwd)
        key = jax.random.key(seed)
        k1, k2, k3 = jax.random.split(key, 3)
        n_embd = 256
        x = jax.random.normal(k1, (4, 512, n_embd), dtype=jnp.float32)
        W_fc = jax.random.normal(k2, (4 * n_embd, n_embd), dtype=jnp.float32) / math.sqrt(n_embd)
        W_proj = jax.random.normal(k3, (n_embd, 4 * n_embd), dtype=jnp.float32) / math.sqrt(4 * n_embd)
        return {'x': x, 'W_fc': W_fc, 'W_proj': W_proj}
    _L1_ffn_in = _L1_ffn_setup()
    _d = {'L0_attn_hidden_states': _L0_attn_in['hidden_states'], 'L0_attn_Wq': _L0_attn_in['Wq'], 'L0_attn_Wk': _L0_attn_in['Wk'], 'L0_attn_Wv': _L0_attn_in['Wv'], 'L0_attn_Wo': _L0_attn_in['Wo'], 'L0_attn_W1': _L0_attn_in['W1'], 'L0_attn_b1': _L0_attn_in['b1'], 'L0_attn_W2': _L0_attn_in['W2'], 'L0_attn_b2': _L0_attn_in['b2'], 'L0_ffn_W1': _L0_ffn_in['W1'], 'L0_ffn_b1': _L0_ffn_in['b1'], 'L0_ffn_W2': _L0_ffn_in['W2'], 'L0_ffn_b2': _L0_ffn_in['b2'], 'L0_ffn_Wg': _L0_ffn_in['Wg'], 'L0_ffn_bg': _L0_ffn_in['bg'], 'L1_attn_R': _L1_attn_in['R'], 'L1_ffn_W_fc': _L1_ffn_in['W_fc'], 'L1_ffn_W_proj': _L1_ffn_in['W_proj']}
    _x0 = _d['L0_attn_hidden_states']
    _d['L0_attn_hidden_states'] = jax.random.normal(jax.random.fold_in(jax.random.key(seed), 1), (4, 2048, 256), dtype=_x0.dtype)
    del _x0
    return _d

def reference(L0_attn_hidden_states, L0_attn_Wq, L0_attn_Wk, L0_attn_Wv, L0_attn_Wo, L0_attn_W1, L0_attn_b1, L0_attn_W2, L0_attn_b2, L0_ffn_W1, L0_ffn_b1, L0_ffn_W2, L0_ffn_b2, L0_ffn_Wg, L0_ffn_bg, L1_attn_R, L1_ffn_W_fc, L1_ffn_W_proj):

    def _L0_attn_ref(hidden_states, Wq, Wk, Wv, Wo, W1, b1, W2, b2):
        import jax, jax.numpy as jnp
        import numpy as np
        import math
        D_MODEL = 256
        N_HEADS = 16
        HEAD_DIM = D_MODEL // N_HEADS
        CTX_LEN = 256
        POOL_OUT = 64

        def _heads(x):
            B, S, _ = x.shape
            return x.reshape(B, S, N_HEADS, HEAD_DIM)

        def _cross_attn(seq, ctx, Wq, Wk, Wv, Wo):
            B, S, _ = seq.shape
            Q = _heads(seq @ Wq)
            K = _heads(ctx @ Wk)
            V = _heads(ctx @ Wv)
            scale = 1.0 / math.sqrt(HEAD_DIM)
            scores = jnp.einsum('bqhd,bkhd->bhqk', Q, K) * scale
            probs = jax.nn.softmax(scores, axis=-1)
            out = jnp.einsum('bhqk,bkhd->bqhd', probs, V).reshape(B, S, D_MODEL)
            return out @ Wo

        def _causal_self_attn(x, Wq, Wk, Wv, Wo):
            B, S, _ = x.shape
            Q = _heads(x @ Wq)
            K = _heads(x @ Wk)
            V = _heads(x @ Wv)
            scale = 1.0 / math.sqrt(HEAD_DIM)
            scores = jnp.einsum('bqhd,bkhd->bhqk', Q, K) * scale
            causal = jnp.tril(jnp.ones((S, S), dtype=bool))
            scores = jnp.where(causal[None, None], scores, -jnp.inf)
            probs = jax.nn.softmax(scores, axis=-1)
            out = jnp.einsum('bhqk,bkhd->bqhd', probs, V).reshape(B, S, D_MODEL)
            return out @ Wo
        B, S, D = hidden_states.shape
        initial = hidden_states[:, :CTX_LEN]
        remaining = hidden_states[:, CTX_LEN:]
        comp = jax.nn.relu(initial @ W1 + b1) @ W2 + b2
        comp = comp.reshape(B, POOL_OUT, CTX_LEN // POOL_OUT, D).mean(axis=2)
        remaining_out = _cross_attn(remaining, comp, Wq, Wk, Wv, Wo)
        initial_out = _causal_self_attn(initial, Wq, Wk, Wv, Wo)
        return jnp.concatenate([initial_out, remaining_out], axis=1)

    def _L0_ffn_ref(x, W1, b1, W2, b2, Wg, bg):
        import jax, jax.numpy as jnp
        import numpy as np
        B, S, D, H, E = (8, 1024, 256, 512, 8)
        logits = jnp.einsum('bsd,de->bse', x, Wg) + bg
        probs = jax.nn.softmax(logits, axis=-1)
        top1 = jnp.argmax(probs, axis=-1)
        out = jnp.zeros_like(x)
        for e in range(E):
            coef = jnp.where(top1 == e, probs[..., e], 0.0)[..., None]
            h = jax.nn.gelu(jnp.einsum('bsd,dh->bsh', x, W1[e]) + b1[e], approximate=False)
            y = jnp.einsum('bsh,hd->bsd', h, W2[e]) + b2[e]
            out = out + coef * y
        return out

    def _L1_attn_ref(encoding, R):
        import jax, jax.numpy as jnp
        import numpy as np
        INF = 1000000000.0
        D = 256
        b, n, d = encoding.shape
        encR = jnp.einsum('bnd,de->bne', encoding, R)
        scores = jnp.einsum('bnd,bmd->bnm', encR, encoding)
        mask = jnp.where(jnp.tril(jnp.ones((n, n), dtype=bool)), 0.0, -INF).astype(scores.dtype)
        A = jax.nn.softmax(scores + mask, axis=2)
        return jnp.einsum('bnm,bmd->bnd', A, encoding)

    def _L1_ffn_ref(x, W_fc, W_proj):
        import jax, jax.numpy as jnp
        import numpy as np
        import math
        BETA = 0.9
        THRESHOLD = 1.0
        NUM_STEPS = 5
        ALPHA = 2.0

        @jax.custom_vjp
        def spike_fn(u):
            return (u > 0).astype(u.dtype)

        def _spike_fwd(u):
            return (spike_fn(u), u)

        def _spike_bwd(u, g):
            s = jnp.pi / 2.0 * ALPHA * u
            return (g * (ALPHA / 2.0) / (1.0 + s * s),)
        spike_fn.defvjp(_spike_fwd, _spike_bwd)
        h = jnp.square(jax.nn.relu(jnp.einsum('bsd,fd->bsf', x, W_fc)))
        y = jnp.einsum('bsf,df->bsd', h, W_proj)

        def step(mem, _):
            reset = jax.lax.stop_gradient(spike_fn(mem - THRESHOLD))
            mem_new = BETA * mem + y - reset * THRESHOLD
            spk = spike_fn(mem_new - THRESHOLD)
            return (mem_new, spk)
        mem0 = jnp.zeros_like(y)
        _, spks = jax.lax.scan(step, mem0, None, length=NUM_STEPS)
        return jnp.sum(spks, axis=0) / NUM_STEPS
    x = L0_attn_hidden_states
    x = _layernorm(x + _L0_attn_ref(x, L0_attn_Wq, L0_attn_Wk, L0_attn_Wv, L0_attn_Wo, L0_attn_W1, L0_attn_b1, L0_attn_W2, L0_attn_b2), axis=-1)
    x = _layernorm(x + _L0_ffn_ref(x, L0_ffn_W1, L0_ffn_b1, L0_ffn_W2, L0_ffn_b2, L0_ffn_Wg, L0_ffn_bg), axis=-1)
    x = _layernorm(x + _L1_attn_ref(x, L1_attn_R), axis=-1)
    x = _layernorm(x + _L1_ffn_ref(x, L1_ffn_W_fc, L1_ffn_W_proj), axis=-1)
    return x

_drawn_inputs = setup_inputs


def setup_inputs(seed=0):
    import zlib

    import numpy as np

    out = dict(_drawn_inputs(seed))
    spreads = {'L0_attn_b1': (0.0, 0.1),
     'L0_attn_b2': (0.0, 0.1),
     'L0_ffn_b1': (0.0, 0.5),
     'L0_ffn_b2': (0.0, 0.1),
     'L0_ffn_bg': (0.0, 0.346)}
    factors = {}
    for name, (base, spread) in spreads.items():
        noise = np.random.default_rng([zlib.crc32(name.encode()), seed]).standard_normal(out[name].shape)
        drawn = base * np.exp(spread * noise) if base else spread * noise
        out[name] = jnp.asarray(drawn.astype(out[name].dtype))
    for name, factor in factors.items():
        out[name] = (out[name] * factor).astype(out[name].dtype)
    return out
```

```python
from contextlib import ExitStack

import numpy as np
import concourse.bass as bass
from concourse import mybir

F32 = mybir.dt.float32
F32R = mybir.dt.float32r
BF16 = mybir.dt.bfloat16
F16 = mybir.dt.float16
I32 = mybir.dt.int32
ALU = mybir.AluOpType
ACT = mybir.ActivationFunctionType
AX = mybir.AxisListType
SUB, ADD, MUL, MAXOP = ALU.subtract, ALU.add, ALU.mult, ALU.max

P = 128
D = 256
KC = D // P
B, S = 4, 2048
T = B * S
TILES = S // P
CTX = 256
POOL = 64
HEADS, HD = 16, 16
VW = HD + 1
EXPERTS, HID = 8, 512
FF = 1024
EPS = 1e-5
HIDDEN_NEG = -1.0e30
MASKED = -1.0e9

CAP = T + P
PAD_ROW = EXPERTS * CAP
ROW = D + 2
ROUTED_TILES = T // P + EXPERTS - 1
OFF_LIST = 2.0 * T


class Signal:

    def __init__(self, nc, name, per, credit=0):
        self.sem, self.per, self.credit = nc.alloc_semaphore(name), per, credit

    def at(self, b, k):
        return b * self.per + (k + self.credit)


def f32(ap):
    return ap.bitcast(F32)


def mm_split(pe, out, lh, ll, rh, rl, first, last):
    pe.matmul(out, lh, rh, start=first, stop=False)
    pe.matmul(out, lh, rl, start=False, stop=False)
    return pe.matmul(out, ll, rh, start=False, stop=last)


INIT_UNITS = 8
UNITS = INIT_UNITS + TILES - 2
BLOCKS = TILES // 2
GROUPS = TILES // 4


def last_unit(t):
    return 4 * t + 3 if t < 2 else t + INIT_UNITS - 2


def tile_of(n):
    if n in (3, 7):
        return n // 4
    return n - INIT_UNITS + 2 if INIT_UNITS <= n < UNITS else None


def block_at(n):
    return (n - 3) // 2 if n >= 5 and n % 2 and (n - 3) // 2 < BLOCKS else None


def group_done(n, lag):
    t = tile_of(n - lag)
    return t // 4 if t is not None and t % 4 == 3 else None


def layer0_attention(nc, dr, c):
    ctx = ExitStack()

    def sb(name, shape, dt):
        return ctx.enter_context(nc.sbuf_tensor(name, shape, dt))

    with ctx:
        raw = [sb(f"a_raw{i}", [P, KC, 256], F32) for i in range(2)]
        xh = [sb(f"a_xh{i}", [P, KC, 256], F32R) for i in range(2)]
        xl = [sb(f"a_xl{i}", [P, KC, 256], F32R) for i in range(2)]
        rows_in = [sb(f"a_rows{i}", [P, 4, D], F32) for i in range(2)]
        qh = [sb(f"a_qh{i}", [P, KC, 256], F32R) for i in range(2)]
        ql = [sb(f"a_ql{i}", [P, KC, 256], F32R) for i in range(2)]
        h1 = sb("a_h1", [P, CTX], F32)
        hsum = sb("a_hsum", [P, POOL], F32)
        hp = sb("a_hp", [P, POOL], F32)
        hph, hpl = sb("a_hph", [P, POOL], F32R), sb("a_hpl", [P, POOL], F32R)
        comp = sb("a_comp", [P, KC, POOL], F32)
        ch, cl = sb("a_ch", [P, KC, 2, POOL], F32R), sb("a_cl", [P, KC, 2, POOL], F32R)
        kih, kil = sb("a_kih", [P, KC, 2, CTX], F32R), sb("a_kil", [P, KC, 2, CTX], F32R)
        kcl = sb("a_kcl", [P, KC, POOL], F32)
        kchr = sb("a_kchr", [P, KC, POOL], F32R)
        kmh, kml = sb("a_kmh", [P, KC, 8, POOL], F32R), sb("a_kml", [P, KC, 8, POOL], F32R)
        vi = [sb(f"a_vi{i}", [P, 2, HEADS, VW], BF16) for i in range(3)]
        vir = [sb(f"a_vir{i}", [P, 2, D], F32) for i in range(2)]
        vc = [sb(f"a_vc{i}", [P, HEADS, VW], BF16) for i in range(3)]
        vcr = [sb(f"a_vcr{i}", [P, D], F32) for i in range(3)]
        mx = [sb(f"a_mx{i}", [P, HEADS], F32) for i in range(2)]
        mts = [sb(f"a_mts{i}", [HEADS, P], F32R) for i in range(2)]
        prob = [sb(f"a_prob{i}", [P, 1024], F32) for i in range(2)]
        pth, ptl = sb("a_pth", [P, 1024], F16), sb("a_ptl", [P, 1024], F16)
        rs = sb("a_rs", [P, HEADS], F32)
        o = [sb(f"a_o{i}", [P, HEADS, HD], F32) for i in range(2)]
        oth, otl = sb("a_oth", [P, KC, P], F32R), sb("a_otl", [P, KC, P], F32R)
        r = [sb(f"a_r{i}", [P, D], F32) for i in range(2)]
        stats, mv = sb("a_stats", [P, 6], F32), [sb(f"a_mv{i}", [P, 2], F32) for i in range(2)]
        ve = sb("a_ve", [P, 1], F32)
        rstd = [sb(f"a_rstd{i}", [P, 1], F32) for i in range(2)]
        rows = [sb(f"a_out{i}", [P, 4, ROW], F32) for i in range(2)]
        x1h = [sb(f"a_x1h{i}", [P, KC, P], F32R) for i in range(2)]
        x1l = [sb(f"a_x1l{i}", [P, KC, P], F32R) for i in range(2)]
        lga = sb("a_lga", [P, EXPERTS], F32)
        lg = sb("a_lg", [P, 4, EXPERTS], F32)
        lmax, mkey = sb("a_lmax", [P, 4], F32), sb("a_mkey", [P, 4], F32)
        ld, lex = sb("a_ld", [P, 4, EXPERTS], F32), sb("a_lex", [P, 4, EXPERTS], F32)
        key = sb("a_key", [P, 4, EXPERTS], F32)
        key2 = sb("a_key2", [P, 4, EXPERTS], F32)
        oh = sb("a_oh", [P, 4, EXPERTS], BF16)
        lsum = sb("a_lsum", [P, 4], F32)
        pf, pf2 = sb("a_pf", [P, 4, EXPERTS], F32), sb("a_pf2", [P, 4, EXPERTS], F32)
        pos = [sb(f"a_pos{i}", [P, 4], I32) for i in range(2)]

        ps_s = [ctx.enter_context(nc.psum_tensor(f"a_ps_s{i}", [P, 1024], F32)) for i in range(2)]
        ps_t = [ctx.enter_context(nc.psum_tensor(f"a_ps_t{i}", [P, 512], F32)) for i in range(2)]
        ps_o = ctx.enter_context(nc.psum_tensor("a_ps_o", [P, 512], F32))
        ps_m = ctx.enter_context(nc.psum_tensor("a_ps_m", [P, 512], F32))
        OUT = ps_o[:, 0:HEADS * VW]
        MT = ps_m[:, 0:128]
        LG = ps_o[:, 400:416]
        PF = ps_o[:, 416:448]
        TOT = ps_o[:, 448:456]
        TURN = ps_m[:, 128:384]
        PROJ = ps_t[0][:, 0:256]
        X1T = ps_t[1][:, 0:256]
        KI, VI = ps_s[0][:, 0:512], ps_s[0][:, 512:1024]
        H1, CM = ps_s[1][:, 0:256], ps_s[1][:, 256:384]
        KCP, VCP = ps_s[1][:, 512:640], ps_s[1][:, 640:896]

        n_ = {}

        def sig(name, per, credit=0):
            n_[name] = Signal(nc, "a_" + name, per, credit)
            return n_[name]

        xt_in = [sig(f"xt_in{i}", 8 * BLOCKS) for i in range(2)]
        rows_got = [sig(f"rows_got{i}", 8 * GROUPS) for i in range(2)]
        xh_done, xl_done = sig("xh_done", BLOCKS), sig("xl_done", BLOCKS, 2)
        h1_ready, h1_done = sig("h1_ready", 1), sig("h1_done", 1)
        hp_sum, hp_done, hph_done, hpl_done = sig("hp_sum", 1), sig("hp_done", 1), sig("hph_done", 1), sig("hpl_done", 1)
        comp_ready, comp_done, ch_done, cl_done = sig("comp_ready", 1), sig("comp_done", 1), sig("ch_done", 1), sig("cl_done", 1)
        ki_ready, kih_done, kil_done = sig("ki_ready", 1), sig("kih_done", 1), sig("kil_done", 1)
        vi_ready, vi_hi, vi_mid = sig("vi_ready", 1), sig("vi_hi", 3), sig("vi_mid", 2)
        kc_ready, kch_done, kcl_done, kmh_done, kml_done = sig("kc_ready", 1), sig("kch_done", 1), sig("kcl_done", 1), sig("kmh_done", 1), sig("kml_done", 1)
        vc_hi, vc_mid = sig("vc_hi", 3), sig("vc_mid", 3)
        q_ready, qh_done, ql_done = sig("q_ready", BLOCKS), sig("qh_done", BLOCKS), sig("ql_done", BLOCKS)
        s_ready, max_done = sig("s_ready", UNITS), sig("max_done", UNITS)
        mt_ready, mts_done = sig("mt_ready", UNITS), sig("mts_done", UNITS)
        sh_ready, exp_done = sig("sh_ready", UNITS), sig("exp_done", UNITS)
        t_ready, pth_done, ptl_done = sig("t_ready", 2 * UNITS), sig("pth_done", 2 * UNITS), sig("ptl_done", 2 * UNITS)
        pv_ready, rs_done, o_done = sig("pv_ready", UNITS), sig("rs_done", UNITS), sig("o_done", UNITS, 1)
        ot_ready, oth_done, otl_done = sig("ot_ready", TILES), sig("oth_done", TILES), sig("otl_done", TILES)
        wo_ready, r_done, st_done, mv_done = sig("wo_ready", TILES), sig("r_done", TILES, 1), sig("st_done", TILES), sig("mv_done", TILES)
        ve_done, rstd_done, x1_done = sig("ve_done", TILES), sig("rstd_done", TILES), sig("x1_done", TILES)
        xt_ready, x1h_done, x1l_done = sig("xt_ready", TILES), sig("x1h_done", TILES), sig("x1l_done", TILES, 1)
        lg_ready, lga_done, lg_done = sig("lg_ready", TILES), sig("lga_done", TILES), sig("lg_done", TILES, 1)
        lm_done, ld_done, ex_done = sig("lm_done", GROUPS), sig("ld_done", GROUPS), sig("ex_done", GROUPS)
        key_done, oh_done = sig("key_done", 3 * GROUPS), sig("oh_done", GROUPS)
        pf_ready, base_read, base_done, pos_done = sig("pf_ready", 1), sig("base_read", GROUPS), sig("base_done", GROUPS), sig("pos_done", GROUPS, 1)
        sel_done, lsum_done, row_done = sig("sel_done", GROUPS), sig("lsum_done", GROUPS), sig("row_done", 2 * GROUPS)
        ids_done = sig("ids_done", 1, 1)
        scattered = [sig(f"scattered{i}", 8 * TILES) for i in range(2)]

        credits = nc.Block()
        with credits as block:
            @block.vector
            def _(dve):
                dve.sem_inc(xl_done.sem, 2)
                dve.sem_inc(o_done.sem, 1)
                dve.sem_inc(r_done.sem, 1)
                dve.sem_inc(x1l_done.sem, 1)
                dve.sem_inc(lg_done.sem, 1)
                dve.sem_inc(pos_done.sem, 1)
                dve.sem_inc(ids_done.sem, 1)
                for i in range(3):
                    dve.memset(vi[i][:, :, :, HD:VW], 1.0 if i == 0 else 0.0)
                    if i:
                        dve.memset(vc[i][:, :, HD:VW], 0.0)
                dve.tensor_copy(vc[0][:, :, HD:VW], c["half"][:, :].rearrange("p (h a) -> p h a", a=1))

        with nc.Block() as block:

            @block.sync
            def _(sp):
                with sp.Fori(0, B) as b:
                    def rows_load(g):
                        if g >= 2:
                            sp.wait_ge(r_done.sem, r_done.at(b, 4 * (g - 1)))
                        else:
                            sp.wait_ge(r_done.sem, r_done.at(b, 0))
                        sp.dma_start(rows_in[g % 2][:, :, :],
                                     dr["x"][bass.ds(b * S + g * 512, 512), :].rearrange("(j p) d -> p j d", p=P)
                                     ).then_inc(rows_got[g % 2].sem, 16)

                    for k in range(BLOCKS):
                        sp.wait_ge(xl_done.sem, xl_done.at(b, k - 1))
                        if k >= 2:
                            sp.wait_ge(xh_done.sem, xh_done.at(b, k - 1))
                        sp.dma_start(raw[k % 2][:, :, :],
                                     dr["xT"][:, :, bass.ds(b * S + k * 256, 256)]).then_inc(xt_in[k % 2].sem, 16)
                        if k % 2 == 0:
                            rows_load(k // 2)

            @block.gpsimd
            def _(pool):
                with pool.Fori(0, B) as b:
                    pool.wait_ge(kcl_done.sem, kcl_done.at(b, 1))
                    pool.tensor_tensor(kml[:, :, :, :],
                                       kcl[:, :, :].unsqueeze(2).broadcast_to([P, KC, 8, POOL]),
                                       c["head"][:, :].unsqueeze(1).unsqueeze(3).broadcast_to([P, KC, 8, POOL]),
                                       MUL).then_inc(kml_done.sem, 1)
                    for n in range(0, UNITS + 5):
                        t = tile_of(n - 2)
                        if t is not None:
                            pool.wait_ge(mv_done.sem, mv_done.at(b, t + 1))
                            pool.tensor_tensor(ve[:, :], mv[t % 2][:, 1:2], c["eps"][:, :], ADD).then_inc(ve_done.sem, 1)
                            pool.wait_ge(ve_done.sem, ve_done.at(b, t + 1))
                            pool.tensor_tensor(rstd[t % 2][:, :], ve[:, :], c["mhalf"][:, :], ALU.pow).then_inc(rstd_done.sem, 1)
                        g = group_done(n, 5)
                        if g is not None:
                            pool.wait_ge(pos_done.sem, pos_done.at(b, g + 1))
                            pool.wait_ge(row_done.sem, row_done.at(b, 2 * g + 2))
                            pool.nop(nofuse=True)
                            for j in range(4):
                                pool.indirect_dma_start(
                                    out=dr["routed"][:, :],
                                    out_offset=bass.IndirectOffsetOnAxis(ap=pos[g % 2][:, j:j + 1], axis=0),
                                    in_=rows[g % 2][:, j, :], in_offset=None).then_inc(scattered[g % 2].sem, 16)
                for i in range(2):
                    pool.wait_ge(scattered[i].sem, 8 * TILES * B)

            @block.scalar
            def _(act):
                with act.Fori(0, B) as b:
                    def split_x(k):
                        act.wait_ge(xt_in[k % 2].sem, xt_in[k % 2].at(b, 16 * (k // 2 + 1)))
                        if k >= 2:
                            act.wait_ge(q_ready.sem, q_ready.at(b, k - 1))
                            act.wait_ge(vi_ready.sem, vi_ready.at(b, 1))
                        act.activation(xh[k % 2][:, :, :], raw[k % 2][:, :, :], ACT.Copy).then_inc(xh_done.sem, 1)

                    def project_q(k):
                        act.wait_ge(q_ready.sem, q_ready.at(b, k + 1))
                        act.activation(qh[k % 2][:, :, :].rearrange("p c q -> p (c q)"), ps_t[1][:, :], ACT.Copy).then_inc(qh_done.sem, 1)

                    split_x(0)
                    act.wait_ge(ki_ready.sem, ki_ready.at(b, 1))
                    for a in range(2):
                        ins = act.activation(kih[:, :, a, :], KI.rearrange("p (c k) -> p c k", c=KC), ACT.Copy, scale=c["pair"][:, a:a + 1])
                    ins.then_inc(kih_done.sem, 1)
                    project_q(0)
                    act.wait_ge(h1_ready.sem, h1_ready.at(b, 1))
                    act.activation(h1[:, :], H1, ACT.Relu, bias=c["b1"][:, :]).then_inc(h1_done.sem, 1)
                    act.wait_ge(vi_ready.sem, vi_ready.at(b, 1))
                    act.activation(vi[0][:, :, :, 0:HD], VI.rearrange("p (k h d) -> p k h d", k=2, h=HEADS), ACT.Copy).then_inc(vi_hi.sem, 1)
                    act.wait_ge(hp_done.sem, hp_done.at(b, 1))
                    act.activation(hph[:, :], hp[:, :], ACT.Copy).then_inc(hph_done.sem, 1)
                    act.wait_ge(comp_ready.sem, comp_ready.at(b, 1))
                    for k in range(KC):
                        ins = act.activation(comp[:, k, :], CM[:, k * POOL:(k + 1) * POOL], ACT.Identity, bias=c["b2"][:, k:k + 1])
                    ins.then_inc(comp_done.sem, 1)
                    act.wait_ge(comp_done.sem, comp_done.at(b, 1))
                    act.activation(ch[:, :, :, :], comp[:, :, :].unsqueeze(2).broadcast_to([P, KC, 2, POOL]), ACT.Copy).then_inc(ch_done.sem, 1)
                    act.wait_ge(kc_ready.sem, kc_ready.at(b, 1))
                    act.activation(kchr[:, :, :].rearrange("p c k -> p (c k)"), KCP, ACT.Copy).then_inc(kch_done.sem, 1)
                    act.wait_ge(vi_mid.sem, vi_mid.at(b, 1))
                    act.activation(vi[1][:, :, :, 0:HD], vir[0][:, :, :].rearrange("p k (h d) -> p k h d", h=HEADS), ACT.Copy).then_inc(vi_hi.sem, 1)
                    act.wait_ge(vi_mid.sem, vi_mid.at(b, 2))
                    act.activation(vi[2][:, :, :, 0:HD], vir[1][:, :, :].rearrange("p k (h d) -> p k h d", h=HEADS), ACT.Copy).then_inc(vi_hi.sem, 1)
                    for i in range(3):
                        act.wait_ge(vc_mid.sem, vc_mid.at(b, i + 1))
                        act.activation(vc[i][:, :, 0:HD], vcr[i][:, :].rearrange("p (h d) -> p h d", h=HEADS), ACT.Copy).then_inc(vc_hi.sem, 1)

                    for n in range(-1, UNITS + 5):
                        if 0 <= n < UNITS:
                            for i in range(2):
                                act.wait_ge(t_ready.sem, t_ready.at(b, 2 * n + i + 1))
                                act.activation(pth[:, 512 * i:512 * i + 512], ps_t[i][:, :], ACT.Copy).then_inc(pth_done.sem, 1)
                        u = n + 1
                        if u < UNITS:
                            heads = 4 if u < INIT_UNITS else HEADS
                            act.wait_ge(mt_ready.sem, mt_ready.at(b, u + 1))
                            act.activation(mts[u % 2][0:heads, :], MT[0:heads, :], ACT.Copy, scale=-1.0).then_inc(mts_done.sem, 1)
                        k = block_at(n)
                        if k is not None:
                            project_q(k)
                        if u < UNITS:
                            act.wait_ge(sh_ready.sem, sh_ready.at(b, u + 1))
                            act.activation(prob[u % 2][:, :], ps_s[u % 2][:, :], ACT.Exp, scale=float(HD) ** -0.5).then_inc(exp_done.sem, 1)
                        t = tile_of(n - 3)
                        if t is not None:
                            act.wait_ge(xt_ready.sem, xt_ready.at(b, t + 1))
                            act.activation(x1h[t % 2][:, :, :].rearrange("p c q -> p (c q)"), X1T, ACT.Copy).then_inc(x1h_done.sem, 1)
                        t = tile_of(n - 1)
                        if t is not None:
                            act.wait_ge(ot_ready.sem, ot_ready.at(b, t + 1))
                            act.activation(oth[:, :, :].rearrange("p c q -> p (c q)"), TURN, ACT.Copy).then_inc(oth_done.sem, 1)
                        k = block_at(n + 2)
                        if k is not None:
                            split_x(k)
                        g = group_done(n, 4)
                        if g is not None:
                            act.wait_ge(ld_done.sem, ld_done.at(b, g + 1))
                            act.activation(lex[:, :, :], ld[:, :, :], ACT.Exp).then_inc(ex_done.sem, 1)

            @block.tensor
            def _(pe):
                wq, wk, wv, wo = c["wq"], c["wk"], c["wv"], c["wo"]
                with pe.Fori(0, B) as b:
                    def x_split(k):
                        pe.wait_ge(xh_done.sem, xh_done.at(b, k + 1))
                        pe.wait_ge(xl_done.sem, xl_done.at(b, k + 1))

                    def project_q(k):
                        x_split(k)
                        for m in range(KC):
                            for kk in range(KC):
                                ins = mm_split(pe, ps_t[1][:, m * 256:(m + 1) * 256],
                                               wq[0][:, kk, m * P:(m + 1) * P], wq[1][:, kk, m * P:(m + 1) * P],
                                               xh[k % 2][:, kk, :], xl[k % 2][:, kk, :], kk == 0, kk == KC - 1)
                        ins.then_inc(q_ready.sem, 1)

                    def scores(u):
                        out = ps_s[u % 2]
                        if u < INIT_UNITS:
                            t, g = u // 4, u % 4
                            q = slice(P * t, P * t + P)
                            for i in range(2):
                                pair = 2 * g + i
                                m, rr = pair // 4, slice(32 * (pair % 4), 32 * (pair % 4) + 32)
                                o_ = out[:, 512 * i:512 * i + 512]
                                kh = kih[rr, m, :, :].rearrange("p a k -> p (a k)")
                                kl = kil[rr, m, :, :].rearrange("p a k -> p (a k)")
                                mm_split(pe, o_, qh[0][rr, m, q], ql[0][rr, m, q], kh, kl, True, False)
                            for i in range(2):
                                ins = pe.matmul(out[:, 512 * i:512 * i + 512], c["ident_r"][:, :], c["causal"][t][:, :],
                                                start=False, stop=True)
                        else:
                            t = u - INIT_UNITS + 2
                            k, q = t // 2, slice(P * (t % 2), P * (t % 2) + P)
                            for m in range(KC):
                                o_ = out[:, 512 * m:512 * m + 512]
                                kh = kmh[:, m, :, :].rearrange("p h k -> p (h k)")
                                kl = kml[:, m, :, :].rearrange("p h k -> p (h k)")
                                ins = mm_split(pe, o_, qh[k % 2][:, m, q], ql[k % 2][:, m, q], kh, kl, True, True)
                        ins.then_inc(s_ready.sem, 1)

                    x_split(0)
                    for m in range(KC):
                        for kk in range(KC):
                            ins = mm_split(pe, KI[:, m * 256:(m + 1) * 256],
                                           wk[0][:, kk, m * P:(m + 1) * P], wk[1][:, kk, m * P:(m + 1) * P],
                                           xh[0][:, kk, :], xl[0][:, kk, :], kk == 0, kk == KC - 1)
                    ins.then_inc(ki_ready.sem, 1)
                    for kk in range(KC):
                        ins = mm_split(pe, H1, c["w1"][0][:, kk, :], c["w1"][1][:, kk, :],
                                       xh[0][:, kk, :], xl[0][:, kk, :], kk == 0, kk == KC - 1)
                    ins.then_inc(h1_ready.sem, 1)
                    project_q(0)
                    for m in range(2):
                        for kk in range(KC):
                            ins = mm_split(pe, VI[:, m * 256:(m + 1) * 256],
                                           xh[0][:, kk, m * P:(m + 1) * P], xl[0][:, kk, m * P:(m + 1) * P],
                                           wv[0][:, kk, :], wv[1][:, kk, :], kk == 0, kk == KC - 1)
                    ins.then_inc(vi_ready.sem, 1)
                    pe.wait_ge(hph_done.sem, hph_done.at(b, 1))
                    pe.wait_ge(hpl_done.sem, hpl_done.at(b, 1))
                    for m in range(KC):
                        ins = mm_split(pe, CM[:, m * POOL:(m + 1) * POOL],
                                       c["w2"][0][:, m * P:(m + 1) * P], c["w2"][1][:, m * P:(m + 1) * P],
                                       hph[:, :], hpl[:, :], True, True)
                    ins.then_inc(comp_ready.sem, 1)
                    pe.wait_ge(ch_done.sem, ch_done.at(b, 1))
                    pe.wait_ge(cl_done.sem, cl_done.at(b, 1))
                    for m in range(KC):
                        for kk in range(KC):
                            ins = mm_split(pe, KCP[:, m * POOL:(m + 1) * POOL],
                                           wk[0][:, kk, m * P:(m + 1) * P], wk[1][:, kk, m * P:(m + 1) * P],
                                           ch[:, kk, 0, :], cl[:, kk, 0, :], kk == 0, kk == KC - 1)
                    for kk in range(KC):
                        ins = mm_split(pe, VCP,
                                       ch[:, kk, :, :].rearrange("p a k -> p (a k)"), cl[:, kk, :, :].rearrange("p a k -> p (a k)"),
                                       wv[0][:, kk, :], wv[1][:, kk, :], kk == 0, kk == KC - 1)
                    ins.then_inc(kc_ready.sem, 1)
                    pe.wait_ge(kih_done.sem, kih_done.at(b, 1))
                    pe.wait_ge(kil_done.sem, kil_done.at(b, 1))
                    pe.wait_ge(vi_hi.sem, vi_hi.at(b, 1))
                    pe.wait_ge(vi_mid.sem, vi_mid.at(b, 1))
                    pe.wait_ge(qh_done.sem, qh_done.at(b, 1))
                    pe.wait_ge(ql_done.sem, ql_done.at(b, 1))

                    for n in range(-2, UNITS + 5):
                        u = n + 1
                        k = block_at(n - 1)
                        if k is not None:
                            pe.wait_ge(qh_done.sem, qh_done.at(b, k + 1))
                            pe.wait_ge(ql_done.sem, ql_done.at(b, k + 1))
                        if 0 <= n < UNITS:
                            pe.wait_ge(exp_done.sem, exp_done.at(b, n + 1))
                            t = tile_of(n - 3)
                            if t is not None:
                                pe.wait_ge(r_done.sem, r_done.at(b, t + 1))
                            for i in range(2):
                                t = tile_of(n - 4)
                                if i and t is not None:
                                    pe.wait_ge(x1h_done.sem, x1h_done.at(b, t + 1))
                                    pe.wait_ge(x1l_done.sem, x1l_done.at(b, t + 1))
                                for j in range(4):
                                    ins = pe.transpose(ps_t[i][:, P * j:P * j + P],
                                                       prob[n % 2][:, 512 * i + P * j:512 * i + P * j + P], c["ident"][:, :])
                                ins.then_inc(t_ready.sem, 1)
                        if n + 2 < UNITS:
                            if n + 2 == 1:
                                pe.wait_ge(kcl_done.sem, kcl_done.at(b, 1))
                                pe.wait_ge(vc_mid.sem, vc_mid.at(b, 1))
                            if n + 2 == INIT_UNITS:
                                pe.wait_ge(kmh_done.sem, kmh_done.at(b, 1))
                                pe.wait_ge(kml_done.sem, kml_done.at(b, 1))
                            scores(n + 2)
                        if 0 <= u < UNITS:
                            heads = 4 if u < INIT_UNITS else HEADS
                            pe.wait_ge(max_done.sem, max_done.at(b, u + 1))
                            t = tile_of(n - 2)
                            if t is not None:
                                pe.wait_ge(oth_done.sem, oth_done.at(b, t + 1))
                                pe.wait_ge(otl_done.sem, otl_done.at(b, t + 1))
                            pe.transpose(MT[0:heads, :], mx[u % 2][:, 0:heads], c["ident"][:, :]).then_inc(mt_ready.sem, 1)
                        k = block_at(n)
                        if k is not None:
                            pe.wait_ge(pth_done.sem, pth_done.at(b, 2 * n + 2))
                            pe.wait_ge(ptl_done.sem, ptl_done.at(b, 2 * n + 2))
                            project_q(k)
                        t = tile_of(n - 2)
                        if t is not None:
                            pe.wait_ge(oth_done.sem, oth_done.at(b, t + 1))
                            pe.wait_ge(otl_done.sem, otl_done.at(b, t + 1))
                            if n < UNITS:
                                pe.wait_ge(pth_done.sem, pth_done.at(b, 2 * n + 1))
                                pe.wait_ge(ptl_done.sem, ptl_done.at(b, 2 * n + 1))
                            else:
                                pe.wait_ge(r_done.sem, r_done.at(b, t))
                            for kk in range(KC):
                                ins = mm_split(pe, PROJ, oth[:, kk, :], otl[:, kk, :], wo[0][:, kk, :], wo[1][:, kk, :],
                                               kk == 0, kk == KC - 1)
                            ins.then_inc(wo_ready.sem, 1)
                        if 0 <= u < UNITS:
                            pe.wait_ge(mts_done.sem, mts_done.at(b, u + 1))
                            heads = 4 if u < INIT_UNITS else HEADS
                            sel = c["sel4"] if u < INIT_UNITS else c["sel16"]
                            for i in range(2):
                                ins = pe.matmul(ps_s[u % 2][:, 512 * i:512 * i + 512], mts[u % 2][0:heads, :],
                                                sel[0:heads, 512 * i:512 * i + 512], start=False, stop=True,
                                                skip_group_check=True)
                            ins.then_inc(sh_ready.sem, 1)
                        if 0 <= n < UNITS:
                            pe.wait_ge(pth_done.sem, pth_done.at(b, 2 * n + 2))
                            pe.wait_ge(ptl_done.sem, ptl_done.at(b, 2 * n + 2))
                            pe.wait_ge(o_done.sem, o_done.at(b, n))
                            t = tile_of(n - 5)
                            if t is not None:
                                pe.wait_ge(lg_done.sem, lg_done.at(b, t + 1))
                            g = group_done(n, 6)
                            if g is not None:
                                pe.wait_ge(base_done.sem, base_done.at(b, g + 1))
                            if n == 0:
                                pe.wait_ge(vi_hi.sem, vi_hi.at(b, 3))
                            if n == INIT_UNITS:
                                pe.wait_ge(vc_hi.sem, vc_hi.at(b, 3))
                            for j in range(8):
                                blk = slice(P * j, P * j + P)
                                if n < INIT_UNITS:
                                    h = 4 * (n % 4) + j // 2
                                    out, val = OUT[:, VW * h:VW * h + VW], [v[:, j % 2, h, :] for v in vi]
                                    first, last = j % 2 == 0, j % 2 == 1
                                else:
                                    out = OUT[:, 2 * VW * j:2 * VW * j + 2 * VW]
                                    val = [v[:, 2 * j:2 * j + 2, :].rearrange("p h d -> p (h d)") for v in vc]
                                    first = last = True
                                pe.matmul(out, pth[:, blk], val[0], start=first, stop=False)
                                pe.matmul(out, pth[:, blk], val[1], start=False, stop=False)
                                pe.matmul(out, pth[:, blk], val[2], start=False, stop=False)
                                pe.matmul(out, ptl[:, blk], val[0], start=False, stop=False)
                                ins = pe.matmul(out, ptl[:, blk], val[1], start=False, stop=last)
                            ins.then_inc(pv_ready.sem, 1)
                        t = tile_of(n - 3)
                        if t is not None:
                            pe.wait_ge(x1_done.sem, x1_done.at(b, t + 1))
                            k = block_at(n)
                            if k is not None:
                                pe.wait_ge(qh_done.sem, qh_done.at(b, k + 1))
                                pe.wait_ge(ql_done.sem, ql_done.at(b, k + 1))
                            if n >= UNITS:
                                pe.wait_ge(x1l_done.sem, x1l_done.at(b, t))
                            for m in range(KC):
                                ins = pe.transpose(X1T[:, m * P:(m + 1) * P],
                                                   rows[(t // 4) % 2][:, t % 4, m * P:(m + 1) * P], c["ident"][:, :])
                            ins.then_inc(xt_ready.sem, 1)
                        t = tile_of(n - 1)
                        if t is not None:
                            pe.wait_ge(o_done.sem, o_done.at(b, last_unit(t) + 1))
                            for m in range(KC):
                                ins = pe.transpose(TURN[:, m * P:(m + 1) * P],
                                                   o[t % 2][:, 8 * m:8 * m + 8, :].rearrange("p h d -> p (h d)"), c["ident"][:, :])
                            ins.then_inc(ot_ready.sem, 1)
                        g = group_done(n, 5)
                        t = tile_of(n - 4)
                        if g is not None or t is not None:
                            pe.wait_ge(o_done.sem, o_done.at(b, min(n, UNITS - 1) + 1))
                        if g is not None:
                            pe.wait_ge(oh_done.sem, oh_done.at(b, g + 1))
                            pe.wait_ge(lg_done.sem, lg_done.at(b, 4 * g + 4))
                            for j in range(4):
                                pe.matmul(PF[:, 8 * j:8 * j + 8], c["before"][:, :], oh[:, j, :], start=True, stop=j == 0)
                                for i in range(j):
                                    pe.matmul(PF[:, 8 * j:8 * j + 8], c["all"][:, :], oh[:, i, :], start=False, stop=i == j - 1)
                            for j in range(4):
                                ins = pe.matmul(TOT, c["all"][:, :], oh[:, j, :], start=j == 0, stop=j == 3)
                            if t is None:
                                ins.then_inc(pf_ready.sem, 1)
                        if t is not None:
                            pe.wait_ge(x1h_done.sem, x1h_done.at(b, t + 1))
                            pe.wait_ge(x1l_done.sem, x1l_done.at(b, t + 1))
                            pe.wait_ge(lg_done.sem, lg_done.at(b, t))
                            for kk in range(KC):
                                pe.matmul(LG, x1h[t % 2][:, kk, :], c["wg"][:, kk, :], start=kk == 0, stop=False)
                                ins = pe.matmul(LG[:, 0:EXPERTS], x1l[t % 2][:, kk, :], c["wg"][:, kk, 0:EXPERTS],
                                                start=False, stop=kk == KC - 1)
                            ins.then_inc(lg_ready.sem, 1)

            @block.vector
            def _(dve):
                with dve.Fori(0, B) as b:
                    def split_x(k):
                        dve.wait_ge(xh_done.sem, xh_done.at(b, k + 1))
                        dve.tensor_tensor(xl[k % 2][:, :, :], raw[k % 2][:, :, :], f32(xh[k % 2][:, :, :]), SUB).then_inc(xl_done.sem, 1)

                    def project_q(k):
                        dve.wait_ge(qh_done.sem, qh_done.at(b, k + 1))
                        dve.tensor_tensor(ql[k % 2][:, :, :].rearrange("p c q -> p (c q)"), ps_t[1][:, :],
                                          f32(qh[k % 2][:, :, :].rearrange("p c q -> p (c q)")), SUB).then_inc(ql_done.sem, 1)

                    split_x(0)
                    dve.wait_ge(kih_done.sem, kih_done.at(b, 1))
                    for a in range(2):
                        ins = dve.scalar_tensor_tensor(out=kil[:, :, a, :], in0=KI.rearrange("p (c k) -> p c k", c=KC),
                                                       scalar=c["pair"][:, a:a + 1], in1=f32(kih[:, :, a, :]), op0=MUL, op1=SUB)
                    ins.then_inc(kil_done.sem, 1)
                    project_q(0)
                    dve.wait_ge(h1_done.sem, h1_done.at(b, 1))
                    dve.tensor_reduce(hsum[:, :], h1[:, :].rearrange("p (k a) -> p k a", a=CTX // POOL), AX.X, ADD).then_inc(hp_sum.sem, 1)
                    dve.wait_ge(hp_sum.sem, hp_sum.at(b, 1))
                    dve.tensor_scalar(hp[:, :], hsum[:, :], float(POOL) / CTX, None, MUL).then_inc(hp_done.sem, 1)
                    dve.wait_ge(hph_done.sem, hph_done.at(b, 1))
                    dve.wait_ge(hp_done.sem, hp_done.at(b, 1))
                    dve.tensor_tensor(hpl[:, :], hp[:, :], f32(hph[:, :]), SUB).then_inc(hpl_done.sem, 1)
                    dve.wait_ge(vi_hi.sem, vi_hi.at(b, 1))
                    dve.tensor_tensor(vir[0][:, :, :].rearrange("p k (h d) -> p (k h) d", h=HEADS),
                                      VI.rearrange("p (k d) -> p k d", d=HD),
                                      vi[0][:, :, :, 0:HD].rearrange("p k h d -> p (k h) d"), SUB).then_inc(vi_mid.sem, 1)
                    dve.wait_ge(ch_done.sem, ch_done.at(b, 1))
                    dve.tensor_tensor(cl[:, :, :, :], comp[:, :, :].unsqueeze(2).broadcast_to([P, KC, 2, POOL]),
                                      f32(ch[:, :, :, :]), SUB).then_inc(cl_done.sem, 1)
                    dve.wait_ge(kch_done.sem, kch_done.at(b, 1))
                    dve.tensor_tensor(kcl[:, :, :].rearrange("p c k -> p (c k)"), KCP,
                                      f32(kchr[:, :, :].rearrange("p c k -> p (c k)")), SUB).then_inc(kcl_done.sem, 1)
                    dve.tensor_tensor(kmh[:, :, :, :], f32(kchr[:, :, :]).unsqueeze(2).broadcast_to([P, KC, 8, POOL]),
                                      c["head"][:, :].unsqueeze(1).unsqueeze(3).broadcast_to([P, KC, 8, POOL]), MUL
                                      ).then_inc(kmh_done.sem, 1)
                    dve.wait_ge(vi_hi.sem, vi_hi.at(b, 2))
                    dve.wait_ge(vi_mid.sem, vi_mid.at(b, 1))
                    dve.tensor_tensor(vir[1][:, :, :].rearrange("p k (h d) -> p (k h) d", h=HEADS),
                                      vir[0][:, :, :].rearrange("p k (h d) -> p (k h) d", h=HEADS),
                                      vi[1][:, :, :, 0:HD].rearrange("p k h d -> p (k h) d"), SUB).then_inc(vi_mid.sem, 1)
                    dve.wait_ge(kcl_done.sem, kcl_done.at(b, 1))
                    dve.tensor_tensor(vcr[0][:, :].rearrange("p (h d) -> p h d", h=HEADS), VCP.rearrange("p (h d) -> p h d", h=HEADS),
                                      c["half"][:, :].unsqueeze(2).broadcast_to([P, HEADS, HD]), MUL).then_inc(vc_mid.sem, 1)
                    for i in range(2):
                        dve.wait_ge(vc_hi.sem, vc_hi.at(b, i + 1))
                        dve.wait_ge(vc_mid.sem, vc_mid.at(b, i + 1))
                        dve.tensor_tensor(vcr[i + 1][:, :].rearrange("p (h d) -> p h d", h=HEADS),
                                          vcr[i][:, :].rearrange("p (h d) -> p h d", h=HEADS), vc[i][:, :, 0:HD], SUB
                                          ).then_inc(vc_mid.sem, 1)

                    for n in range(-2, UNITS + 5):
                        if 0 <= n < UNITS:
                            for i in range(2):
                                dve.wait_ge(pth_done.sem, pth_done.at(b, 2 * n + i + 1))
                                dve.tensor_tensor(ptl[:, 512 * i:512 * i + 512], ps_t[i][:, :], pth[:, 512 * i:512 * i + 512], SUB
                                                  ).then_inc(ptl_done.sem, 1)
                        t = tile_of(n - 3)
                        if t is not None:
                            g = t // 4
                            if t % 4 == 0 and g >= 2:
                                dve.wait_ge(scattered[g % 2].sem, scattered[g % 2].at(b, 64 * (g // 2)))
                            dve.wait_ge(rstd_done.sem, rstd_done.at(b, t + 1))
                            dve.tensor_scalar(rows[g % 2][:, t % 4, 0:D], r[t % 2][:, :], mv[t % 2][:, 0:1], rstd[t % 2][:, :], SUB, MUL
                                              ).then_inc(x1_done.sem, 1)
                        u = n + 2
                        if u < UNITS:
                            heads, keys = (4, CTX) if u < INIT_UNITS else (HEADS, POOL)
                            dve.wait_ge(s_ready.sem, s_ready.at(b, u + 1))
                            dve.tensor_reduce(mx[u % 2][:, 0:heads], ps_s[u % 2][:, :].rearrange("p (h k) -> p h k", k=keys), AX.X, MAXOP
                                              ).then_inc(max_done.sem, 1)
                        k = block_at(n)
                        if k is not None:
                            project_q(k)
                        t = tile_of(n - 2)
                        if t is not None:
                            dve.wait_ge(wo_ready.sem, wo_ready.at(b, t + 1))
                            if t % 4 == 0:
                                dve.wait_ge(rows_got[t // 4 % 2].sem, rows_got[t // 4 % 2].at(b, 16 * (t // 8 + 1)))
                            dve.tensor_tensor(r[t % 2][:, :], PROJ, rows_in[(t // 4) % 2][:, t % 4, :], ADD).then_inc(r_done.sem, 1)
                            dve.wait_ge(r_done.sem, r_done.at(b, t + 1))
                            dve.bn_stats(stats[:, :], r[t % 2][:, :]).then_inc(st_done.sem, 1)
                            dve.wait_ge(st_done.sem, st_done.at(b, t + 1))
                            dve.nop(nofuse=True)
                            dve.bn_aggr(mv[t % 2][:, :], stats[:, :]).then_inc(mv_done.sem, 1)
                        if 0 <= n < UNITS:
                            hs = slice(4 * (n % 4), 4 * (n % 4) + 4) if n < INIT_UNITS else slice(0, HEADS)
                            heads = hs.stop - hs.start
                            out = OUT.rearrange("p (h d) -> p h d", d=VW)
                            dve.wait_ge(pv_ready.sem, pv_ready.at(b, n + 1))
                            dve.wait_ge(o_done.sem, o_done.at(b, n))
                            dve.reciprocal(rs[:, hs], out[:, hs, HD:VW].rearrange("p h a -> p (h a)")).then_inc(rs_done.sem, 1)
                            dve.wait_ge(rs_done.sem, rs_done.at(b, n + 1))
                            tt = n // 4 if n < INIT_UNITS else n - INIT_UNITS + 2
                            if tt >= 2:
                                dve.wait_ge(ot_ready.sem, ot_ready.at(b, tt - 1))
                            dve.tensor_tensor(o[tt % 2][:, hs, :], out[:, hs, 0:HD], rs[:, hs].unsqueeze(2).broadcast_to([P, heads, HD]), MUL
                                              ).then_inc(o_done.sem, 1)
                        t = tile_of(n - 3)
                        if t is not None:
                            dve.wait_ge(x1h_done.sem, x1h_done.at(b, t + 1))
                            dve.tensor_tensor(x1l[t % 2][:, :, :].rearrange("p c q -> p (c q)"), X1T,
                                              f32(x1h[t % 2][:, :, :].rearrange("p c q -> p (c q)")), SUB).then_inc(x1l_done.sem, 1)
                        t = tile_of(n - 1)
                        if t is not None:
                            dve.wait_ge(oth_done.sem, oth_done.at(b, t + 1))
                            dve.tensor_tensor(otl[:, :, :].rearrange("p c q -> p (c q)"), TURN,
                                              f32(oth[:, :, :].rearrange("p c q -> p (c q)")), SUB).then_inc(otl_done.sem, 1)
                        k = block_at(n + 2)
                        if k is not None:
                            split_x(k)
                        t = tile_of(n - 4)
                        if t is not None:
                            dve.wait_ge(lg_ready.sem, lg_ready.at(b, t + 1))
                            dve.tensor_tensor(lga[:, :], LG[:, 0:EXPERTS], c["bg"][:, :], ADD).then_inc(lga_done.sem, 1)
                            dve.wait_ge(lga_done.sem, lga_done.at(b, t + 1))
                            dve.tensor_tensor(lg[:, t % 4, :], LG[:, EXPERTS:2 * EXPERTS], lga[:, :], ADD).then_inc(lg_done.sem, 1)
                        g = group_done(n, 4)
                        if g is not None:
                            full = [P, 4, EXPERTS]
                            dve.wait_ge(lg_done.sem, lg_done.at(b, 4 * g + 4))
                            dve.tensor_reduce(lmax[:, :], lg[:, :, :], AX.X, MAXOP).then_inc(lm_done.sem, 1)
                            dve.wait_ge(lm_done.sem, lm_done.at(b, g + 1))
                            dve.tensor_tensor(ld[:, :, :], lg[:, :, :], lmax[:, :].unsqueeze(2).broadcast_to(full), SUB).then_inc(ld_done.sem, 1)
                            dve.tensor_tensor(key[:, :, :], lg[:, :, :], lmax[:, :].unsqueeze(2).broadcast_to(full), ALU.is_equal
                                              ).then_inc(key_done.sem, 1)
                            dve.wait_ge(key_done.sem, key_done.at(b, 3 * g + 1))
                            dve.tensor_tensor(key2[:, :, :], key[:, :, :], c["order"][:, :].unsqueeze(1).broadcast_to(full), MUL
                                              ).then_inc(key_done.sem, 1)
                            dve.wait_ge(key_done.sem, key_done.at(b, 3 * g + 2))
                            dve.tensor_reduce(mkey[:, :], key2[:, :, :], AX.X, MAXOP).then_inc(key_done.sem, 1)
                            dve.wait_ge(key_done.sem, key_done.at(b, 3 * g + 3))
                            dve.tensor_tensor(oh[:, :, :], key2[:, :, :], mkey[:, :].unsqueeze(2).broadcast_to(full), ALU.is_equal
                                              ).then_inc(oh_done.sem, 1)
                        g = group_done(n, 5)
                        if g is not None:
                            dve.wait_ge(ids_done.sem, ids_done.at(b, 0))
                            if g:
                                dve.wait_ge(base_done.sem, base_done.at(b, g))
                            dve.wait_ge(oh_done.sem, oh_done.at(b, g + 1))
                            if tile_of(n - 4) is None:
                                dve.wait_ge(pf_ready.sem, pf_ready.at(b, 1))
                            dve.tensor_tensor(pf[:, :, :], PF.rearrange("p (j e) -> p j e", j=4),
                                              c["base"][:, :].unsqueeze(1).broadcast_to(full), ADD).then_inc(base_read.sem, 1)
                            dve.wait_ge(base_read.sem, base_read.at(b, g + 1))
                            dve.tensor_tensor(c["base"][:, :], c["base"][:, :], TOT, ADD).then_inc(base_done.sem, 1)
                            dve.tensor_tensor(pf2[:, :, :], pf[:, :, :], oh[:, :, :], MUL).then_inc(sel_done.sem, 1)
                            dve.wait_ge(ex_done.sem, ex_done.at(b, g + 1))
                            dve.tensor_reduce(lsum[:, :], lex[:, :, :], AX.X, ADD).then_inc(lsum_done.sem, 1)
                            dve.wait_ge(sel_done.sem, sel_done.at(b, g + 1))
                            with nc.allow_low_precision(reason="whole numbers below 2**24"):
                                dve.tensor_reduce(pos[g % 2][:, :], pf2[:, :, :], AX.X, ADD).then_inc(pos_done.sem, 1)
                            dve.wait_ge(lsum_done.sem, lsum_done.at(b, g + 1))
                            dve.reciprocal(rows[g % 2][:, :, D:D + 1].rearrange("p j a -> p (j a)"), lsum[:, :]).then_inc(row_done.sem, 1)
                            dve.tensor_copy(rows[g % 2][:, :, D + 1:D + 2].rearrange("p j a -> p (j a)"), c["ids"][:, 4 * g:4 * g + 4]
                                            ).then_inc(row_done.sem, 1)
                    dve.wait_ge(row_done.sem, row_done.at(b, 2 * GROUPS))
                    dve.tensor_scalar(c["ids"][:, :], c["ids"][:, :], float(S), None, ADD).then_inc(ids_done.sem, 1)
                    for i in range(2):
                        dve.wait_ge(scattered[i].sem, scattered[i].at(b, 8 * TILES))


def const_table():
    p = np.arange(P)
    k = {}
    k["ident"] = np.eye(P)
    k["before"] = (p[:, None] < p[None, :]) * 1.0
    for t in range(2):
        hidden = (np.arange(CTX)[None, :] > (p + P * t)[:, None]) * HIDDEN_NEG
        k[f"causal{t}"] = np.concatenate([hidden, hidden], 1)
    k["sel4"] = (p[:, None] == (np.arange(1024) // CTX)[None, :]) * 1.0
    k["sel16"] = (p[:, None] == (np.arange(1024) // POOL)[None, :]) * 1.0
    k["half"] = ((p // 64)[:, None] == (np.arange(HEADS) % 2)[None, :]) * 1.0
    k["head"] = ((p // HD)[:, None] == np.arange(8)[None, :]) * 1.0
    k["pair"] = ((p // HD % 2)[:, None] == np.arange(2)[None, :]) * 1.0
    k["order"] = np.broadcast_to(EXPERTS - np.arange(EXPERTS), (P, EXPERTS))
    k["ids"] = p[:, None] + P * np.arange(TILES)[None, :]
    k["base"] = np.broadcast_to(CAP * np.arange(EXPERTS), (P, EXPERTS))
    k["lane"] = p[:, None]
    k["rowsel"] = (p[:, None] == np.arange(2)[None, :]) * 1.0
    k["ones_row"] = np.ones((P, P))
    k["mhalf"] = np.full((P, 1), -0.5)
    k["eps"] = np.full((P, 1), EPS)
    k["later"] = (p[None, :] > p[:, None]) * MASKED
    k["slots"] = np.broadcast_to(np.arange(TABLE), (P, TABLE))
    k["caps"] = np.broadcast_to(CAP * np.arange(EXPERTS), (P, EXPERTS))
    at, n = {}, 0
    for name, v in k.items():
        at[name] = (n, v.shape[1])
        n += v.shape[1]
    return np.ascontiguousarray(np.concatenate([v.astype(np.float32) for v in k.values()], 1)), at


PLAIN = ("half", "head", "pair", "order", "ids")
SHARED = ("base", "mhalf", "eps", "ident", "lane", "rowsel", "ones_row", "slots", "caps", "later")
TABLE = 80


def setup_layer0(nc, shared, ctx, dr, const_at):
    def keep(name, shape, dt):
        return ctx.enter_context(nc.sbuf_tensor("k_" + name, shape, dt))

    c = {}
    for name in SHARED:
        c[name] = shared.enter_context(nc.sbuf_tensor("g_" + name, [P, const_at[name][1]], F32))
    names = ["wq", "wk", "wv", "wo"]
    for w in names:
        c[w] = [keep(w + x, [P, KC, D], F32R) for x in "hl"]
    c["w1"] = [keep("w1" + x, [P, KC, P], F32R) for x in "hl"]
    c["w2"] = [keep("w2" + x, [P, D], F32R) for x in "hl"]
    c["wg"] = keep("wg", [P, KC, 2 * EXPERTS], F32R)
    c["b1"], c["b2"], c["bg"] = keep("b1", [P, 1], F32), keep("b2", [P, KC], F32), keep("bg", [P, EXPERTS], F32)
    for name in PLAIN:
        c[name] = keep(name, [P, const_at[name][1]], F32)
    c["ident_r"] = keep("ident_r", [P, P], F32R)
    c["causal"] = [keep(f"causal{t}", [P, 2 * CTX], F32R) for t in range(2)]
    c["sel4"], c["sel16"] = keep("sel4", [4, 1024], F32R), keep("sel16", [HEADS, 1024], F32R)
    c["before"], c["all"] = keep("before", [P, P], BF16), keep("all", [P, P], BF16)
    loaded = nc.alloc_semaphore("w_loaded")
    high = nc.alloc_semaphore("w_high")

    with ExitStack() as tmp:
        def stage(name, shape):
            return tmp.enter_context(nc.sbuf_tensor("s_" + name, shape, F32))

        ncol = sum(v[1] for v in const_at.values())
        table = stage("table", [P, ncol])
        raws = [(c[w], stage(w, [P, KC, D]), dr[w].rearrange("(c p) n -> p c n", p=P)) for w in names]
        raws.append((c["w1"], stage("w1", [P, KC, P]), dr["w1"].rearrange("(c p) n -> p c n", p=P)))
        raws.append((c["w2"], stage("w2", [P, D]), dr["w2"]))
        wg = stage("wg", [P, KC, EXPERTS])

        def col(name):
            a, w = const_at[name]
            return table[:, a:a + w]

        with nc.Block() as block:
            @block.sync
            def _(sp):
                sp.dma_start(table[:, :], dr["table"]).then_inc(loaded, 16)
                for _, raw, src in raws:
                    full = raw[:, :, :] if len(raw.shape) == 3 else raw[:, :]
                    sp.dma_start(full, src).then_inc(loaded, 16)
                sp.dma_start(wg[:, :, :], dr["wg"].rearrange("(c p) e -> p c e", p=P)).then_inc(loaded, 16)
                sp.dma_start(c["b1"][:, :], dr["b1"].rearrange("(p a) -> p a", a=1)).then_inc(loaded, 16)
                sp.dma_start(c["b2"][:, :], dr["b2"]).then_inc(loaded, 16)
                sp.dma_start(c["bg"][:, :], dr["bg"].rearrange("(a e) -> a e", a=1).broadcast_to([P, EXPERTS])).then_inc(loaded, 16)

            all_loaded = 16 * (len(raws) + 5)

            @block.scalar
            def _(act):
                act.wait_ge(loaded, all_loaded)
                for pair, raw, _ in raws:
                    ix = (slice(None),) * len(raw.shape)
                    act.activation(pair[0][ix], raw[ix], ACT.Copy).then_inc(high, 1)
                act.activation(c["wg"][:, :, 0:EXPERTS], wg[:, :, :], ACT.Copy).then_inc(high, 1)
                act.activation(c["ident_r"][:, :], col("ident"), ACT.Copy)
                for t in range(2):
                    act.activation(c["causal"][t][:, :], col(f"causal{t}"), ACT.Copy)
                act.activation(c["sel4"][:, :], col("sel4")[0:4, :], ACT.Copy)
                act.activation(c["sel16"][:, :], col("sel16")[0:HEADS, :], ACT.Copy)

            @block.vector
            def _(dve):
                dve.memset(c["all"][:, :], 1.0)
                dve.wait_ge(loaded, all_loaded)
                dve.tensor_copy(c["before"][:, :], col("before"))
                for name in PLAIN + SHARED:
                    dve.tensor_copy(c[name][:, :], col(name))
                for i, (pair, raw, _) in enumerate(raws):
                    ix = (slice(None),) * len(raw.shape)
                    dve.wait_ge(high, i + 1)
                    dve.tensor_tensor(pair[1][ix], raw[ix], f32(pair[0][ix]), SUB)
                dve.wait_ge(high, len(raws) + 1)
                dve.tensor_tensor(c["wg"][:, :, EXPERTS:], wg[:, :, :], f32(c["wg"][:, :, 0:EXPERTS]), SUB)
    return c



HC = HID // P
STEPS = 72
TURN_OF = 4


def setup_experts(nc, ctx, dr, c):
    def keep(name, shape, dt):
        return ctx.enter_context(nc.sbuf_tensor("m_" + name, shape, dt))

    m = {}
    m["w1"] = [keep("w1" + x, [P, EXPERTS * KC * HID], F32R) for x in "hl"]
    m["w2"] = [keep("w2" + x, [P, EXPERTS * HC * D], F32R) for x in "hl"]
    m["b1"] = keep("b1", [2, EXPERTS * HID], F32R)
    m["b2"] = keep("b2", [2, EXPERTS * D], F32R)
    m["ones"] = keep("ones", [2, P], F32R)
    m["table"] = keep("table", [P, 2, TABLE], I32)
    m["ident"], m["mhalf"], m["eps"] = c["ident"], c["mhalf"], c["eps"]
    W = KC * HID
    chunks = [("b1", i) for i in range(EXPERTS * HID // W)] + [("b2", i) for i in range(EXPERTS * D // W)]
    chunks += [("w1", e) for e in range(EXPERTS)] + [("w2", e) for e in range(EXPERTS)]
    with ExitStack() as tmp:
        def stage(name, shape, dt=F32):
            return tmp.enter_context(nc.sbuf_tensor("t_" + name, shape, dt))

        def sem(name):
            return nc.alloc_semaphore("t_" + name)

        raw = [stage(f"raw{i}", [P, W]) for i in range(3)]
        pad = stage("pad", [P, ROW])
        tail = stage("tail", [P, EXPERTS], I32)
        fill, tiles, tiles_x = stage("fill", [P, EXPERTS]), stage("tiles", [P, EXPERTS], I32), stage("tiles_x", [P, EXPERTS])
        tiles_f, ones8, cum = stage("tiles_f", [P, EXPERTS]), stage("ones8", [P, EXPERTS]), stage("cum", [P, EXPERTS])
        ind, ind2 = stage("ind", [P, TABLE, EXPERTS]), stage("ind2", [P, TABLE, EXPERTS])
        e_of, start = stage("e_of", [P, TABLE]), stage("start", [P, TABLE])
        row, row2 = stage("row", [P, TABLE]), stage("row2", [P, TABLE])
        got = [sem(f"got{i}") for i in range(3)]
        high, low = sem("high"), sem("low")
        pads, step, padded = sem("pads"), sem("table_step"), sem("padded")

        with nc.Block() as block:
            @block.sync
            def _(sp):
                for i, (w, e) in enumerate(chunks):
                    if i >= 3:
                        sp.wait_ge(low, i - 2)
                    if w[0] == "b":
                        src = dr["m" + w].rearrange("(a e) n -> a (e n)", a=1)[:, e * W:(e + 1) * W]
                        sp.dma_start(raw[i % 3][0:2, :], src.broadcast_to([2, W])).then_inc(got[i % 3], 16)
                    else:
                        src = dr["m" + w][e].rearrange("(k p) n -> p k n", p=P)
                        sp.dma_start(raw[i % 3][:, :].rearrange("p (k n) -> p k n", k=src.shape[1]), src).then_inc(got[i % 3], 16)

            @block.scalar
            def _(act):
                for i, (w, e) in enumerate(chunks):
                    act.wait_ge(got[i % 3], 16 * (i // 3 + 1))
                    if w[0] == "b":
                        act.activation(m[w][:, e * W:(e + 1) * W], raw[i % 3][0:2, :], ACT.Copy).then_inc(high, 1)
                    else:
                        act.activation(m[w][0][:, e * W:(e + 1) * W], raw[i % 3][:, :], ACT.Copy).then_inc(high, 1)

            @block.gpsimd
            def _(pool):
                pool.wait_ge(pads, 3)
                for e in range(EXPERTS):
                    pool.indirect_dma_start(out=dr["routed"][:, :],
                                            out_offset=bass.IndirectOffsetOnAxis(ap=tail[:, e:e + 1], axis=0),
                                            in_=pad[:, :], in_offset=None).then_inc(padded, 16)
                pool.dma_start(dr["routed"][PAD_ROW:PAD_ROW + P, :], pad[:, :]).then_inc(padded, 16)
                pool.wait_ge(padded, 16 * (EXPERTS + 1))

            @block.vector
            def _(dve):
                count = [0]

                def link(ins):
                    count[0] += 1
                    ins.then_inc(step, 1)
                    dve.wait_ge(step, count[0])

                dve.memset(pad[:, 0:D + 1], 0.0).then_inc(pads, 1)
                dve.memset(pad[:, D + 1:ROW], OFF_LIST).then_inc(pads, 1)
                link(dve.memset(ones8[:, :], 1.0))
                dve.tensor_copy(m["ones"][:, :], c["ones_row"][0:2, :])
                dve.tensor_tensor(tail[:, :], c["base"][:, :], c["lane"][:, :].broadcast_to([P, EXPERTS]), ADD).then_inc(pads, 1)
                link(dve.tensor_tensor(fill[:, :], c["base"][:, :], c["caps"][:, :], SUB))
                link(dve.tensor_scalar(tiles_x[:, :], fill[:, :], 1.0 / P, (P - 1.0) / P - 0.5 + 0.5 / P, MUL, ADD))
                link(dve.tensor_copy(tiles[:, :], tiles_x[:, :]))
                link(dve.tensor_copy(tiles_f[:, :], tiles[:, :]))
                link(dve.tensor_tensor_scan(cum[:, :], ones8[:, :], tiles_f[:, :], 0.0, MUL, ADD))
                full = [P, TABLE, EXPERTS]
                link(dve.tensor_tensor(ind[:, :, :], c["slots"][:, :].unsqueeze(2).broadcast_to(full),
                                       cum[:, :].unsqueeze(1).broadcast_to(full), ALU.is_ge))
                link(dve.tensor_tensor(ind2[:, :, :], ind[:, :, :], tiles_f[:, :].unsqueeze(1).broadcast_to(full), MUL))
                link(dve.tensor_reduce(e_of[:, :], ind[:, :, :], AX.X, ADD))
                link(dve.tensor_reduce(start[:, :], ind2[:, :, :], AX.X, ADD))
                link(dve.tensor_tensor(row[:, :], c["slots"][:, :], start[:, :], SUB))
                link(dve.tensor_scalar(row2[:, :], row[:, :], float(P), None, MUL))
                link(dve.scalar_tensor_tensor(out=row[:, :], in0=e_of[:, :], scalar=float(CAP), in1=row2[:, :], op0=MUL, op1=ADD))
                dve.tensor_scalar(m["table"][:, 0, :], row[:, :], float(PAD_ROW), None, ALU.min)
                dve.tensor_scalar(m["table"][:, 1, :], e_of[:, :], float(EXPERTS - 1), None, ALU.min)
                for i, (w, e) in enumerate(chunks):
                    dve.wait_ge(high, i + 1)
                    at = slice(e * W, (e + 1) * W)
                    if w[0] == "b":
                        part = raw[i % 3][0:2, :]
                        link(dve.tensor_tensor(part, part, f32(m[w][:, at]), SUB))
                        link(dve.tensor_scalar(part, part, c["rowsel"][0:2, 1:2], None, MUL))
                        dve.scalar_tensor_tensor(out=m[w][:, at], in0=f32(m[w][:, at]), scalar=c["rowsel"][0:2, 0:1], in1=part,
                                                 op0=MUL, op1=ADD).then_inc(low, 1)
                    else:
                        dve.tensor_tensor(m[w][1][:, at], raw[i % 3][:, :], f32(m[w][0][:, at]), SUB).then_inc(low, 1)
    return m


def experts(nc, dr, m):
    N = TURN_OF
    TURNS = STEPS // N
    ctx = ExitStack()

    def sb(name, shape, dt):
        return ctx.enter_context(nc.sbuf_tensor("b_" + name, shape, dt))

    with ctx:
        xin = [sb(f"xin{i}", [P, ROW], F32) for i in range(N)]
        xh = [sb(f"xh{i}", [P, KC, P], F32R) for i in range(2)]
        xl = [sb(f"xl{i}", [P, KC, P], F32R) for i in range(2)]
        hid = [sb(f"hid{i}", [P, HID], F32) for i in range(2)]
        hth = [sb(f"hth{i}", [P, HC, P], F32R) for i in range(2)]
        htl = [sb(f"htl{i}", [P, HC, P], F32R) for i in range(2)]
        r = [sb(f"r{i}", [P, D], F32) for i in range(2)]
        stats, ve = sb("stats", [P, 6], F32), sb("ve", [P, 1], F32)
        mv = [sb(f"mv{i}", [P, 2], F32) for i in range(2)]
        rstd = [sb(f"rstd{i}", [P, 1], F32) for i in range(2)]
        x2 = [sb(f"x2{i}", [P, D], F32) for i in range(N)]
        ids = [sb(f"ids{i}", [P, 1], I32) for i in range(N)]
        ps_x = [ctx.enter_context(nc.psum_tensor(f"b_ps_x{i}", [P, 512], F32)) for i in range(1)]
        ps_h = [ctx.enter_context(nc.psum_tensor(f"b_ps_h{i}", [P, HID], F32)) for i in range(2)]
        ps_t = [ctx.enter_context(nc.psum_tensor(f"b_ps_t{i}", [P, HID], F32)) for i in range(2)]
        ps_y = [ctx.enter_context(nc.psum_tensor(f"b_ps_y{i}", [P, 512], F32)) for i in range(2)]

        def sig(name, per=N, credit=0):
            return Signal(nc, "b_" + name, per, credit)

        got = [sig(f"got{i}", 16) for i in range(N)]
        xt_ready, xh_done, xl_done = sig("xt_ready"), sig("xh_done"), sig("xl_done")
        h_ready, gelu_done = sig("h_ready"), sig("gelu_done")
        ht_ready, hth_done, htl_done = sig("ht_ready"), sig("hth_done"), sig("htl_done")
        y_ready, r_done, st_done, mv_done = sig("y_ready"), sig("r_done", N, 4), sig("st_done"), sig("mv_done")
        ve_done, rstd_done = sig("ve_done"), sig("rstd_done")
        x2_done = sig("x2_done")
        sent = [sig(f"sent{i}", 16) for i in range(N)]

        def slot(eng, name, j):
            k = 0 if name == "row" else 1
            return eng.value_load(m["table"][0:1, k, bass.ds(j, 1)], min_val=0, max_val=PAD_ROW if k == 0 else EXPERTS - 1)

        with nc.Block() as block:
            @block.vector
            def _(dve):
                dve.sem_inc(r_done.sem, 4)

        with nc.Block() as block:
            @block.sync
            def _(sp):
                def load(it, a, j):
                    sp.wait_ge(r_done.sem, r_done.at(it, a - N + 1))
                    row = slot(sp, "row", j)
                    sp.dma_start(xin[a % N][:, :], dr["routed"][bass.ds(row, P), :]).then_inc(got[a % N].sem, 16)

                for a in range(3):
                    load(0, a, a)
                with sp.Fori(0, TURNS) as it:
                    for a in range(3, 3 + N):
                        load(it, a, it * N + a)
                for a in range(3):
                    sp.wait_ge(got[a].sem, 16 * (TURNS + 1))

            @block.tensor
            def _(pe):
                w1, w2 = m["w1"], m["w2"]

                def turn_x(it, a, first=False):
                    pe.wait_ge(got[a % N].sem, got[a % N].at(it, 16 * (a // N + 1)))
                    if not first:
                        pe.wait_ge(xh_done.sem, xh_done.at(it, a))
                        pe.wait_ge(xl_done.sem, xl_done.at(it, a))
                    for k in range(KC):
                        ins = pe.transpose(ps_x[0][:, k * P:(k + 1) * P], xin[a % N][:, k * P:(k + 1) * P], m["ident"][:, :])
                    ins.then_inc(xt_ready.sem, 1)

                def hidden(it, a, e):
                    pe.wait_ge(xh_done.sem, xh_done.at(it, a + 1))
                    pe.wait_ge(xl_done.sem, xl_done.at(it, a + 1))
                    out = ps_h[a % 2][:, :]
                    pe.matmul(out, m["ones"][:, :], m["b1"][:, bass.ds(e * HID, HID)], start=True, stop=False)
                    for k in range(KC):
                        at = bass.ds(e * (KC * HID) + k * HID, HID)
                        ins = mm_split(pe, out, xh[a % 2][:, k, :], xl[a % 2][:, k, :], w1[0][:, at], w1[1][:, at], False, k == KC - 1)
                    ins.then_inc(h_ready.sem, 1)

                def turn_h(it, a):
                    pe.wait_ge(gelu_done.sem, gelu_done.at(it, a + 1))
                    for k in range(HC):
                        ins = pe.transpose(ps_t[a % 2][:, k * P:(k + 1) * P], hid[a % 2][:, k * P:(k + 1) * P], m["ident"][:, :])
                    ins.then_inc(ht_ready.sem, 1)

                def output(it, a, e):
                    pe.wait_ge(hth_done.sem, hth_done.at(it, a + 1))
                    pe.wait_ge(htl_done.sem, htl_done.at(it, a + 1))
                    pe.wait_ge(r_done.sem, r_done.at(it, a - 1))
                    out = ps_y[a % 2][:, 0:D]
                    pe.matmul(out, m["ones"][:, :], m["b2"][:, bass.ds(e * D, D)], start=True, stop=False)
                    for k in range(HC):
                        at = bass.ds(e * (HC * D) + k * D, D)
                        ins = mm_split(pe, out, hth[a % 2][:, k, :], htl[a % 2][:, k, :], w2[0][:, at], w2[1][:, at], False, k == HC - 1)
                    ins.then_inc(y_ready.sem, 1)

                turn_x(0, 0, True)
                turn_x(0, 1)
                hidden(0, 0, slot(pe, "expert", 0))
                with pe.Fori(0, TURNS) as it:
                    for a in range(N):
                        turn_h(it, a)
                        turn_x(it, a + 2)
                        hidden(it, a + 1, slot(pe, "expert", it * N + (a + 1)))
                        output(it, a, slot(pe, "expert", it * N + a))

            @block.scalar
            def _(act):
                def high_x(it, a):
                    act.wait_ge(xt_ready.sem, xt_ready.at(it, a + 1))
                    act.activation(xh[a % 2][:, :, :].rearrange("p c q -> p (c q)"), ps_x[0][:, 0:D], ACT.Copy).then_inc(xh_done.sem, 1)

                def gelu(it, a):
                    act.wait_ge(h_ready.sem, h_ready.at(it, a + 1))
                    act.activation(hid[a % 2][:, :], ps_h[a % 2][:, :], ACT.Gelu).then_inc(gelu_done.sem, 1)

                high_x(0, 0)
                high_x(0, 1)
                gelu(0, 0)
                with act.Fori(0, TURNS) as it:
                    for a in range(N):
                        act.wait_ge(ht_ready.sem, ht_ready.at(it, a + 1))
                        act.activation(hth[a % 2][:, :, :].rearrange("p c q -> p (c q)"), ps_t[a % 2][:, :], ACT.Copy).then_inc(hth_done.sem, 1)
                        high_x(it, a + 2)
                        gelu(it, a + 1)

            @block.vector
            def _(dve):
                def low_x(it, a):
                    dve.wait_ge(xh_done.sem, xh_done.at(it, a + 1))
                    dve.tensor_tensor(xl[a % 2][:, :, :].rearrange("p c q -> p (c q)"), ps_x[0][:, 0:D],
                                      f32(xh[a % 2][:, :, :].rearrange("p c q -> p (c q)")), SUB).then_inc(xl_done.sem, 1)

                def norm(it, a, at):
                    dve.wait_ge(rstd_done.sem, rstd_done.at(it, a + 1))
                    dve.tensor_scalar(x2[at][:, :], r[a % 2][:, :], mv[a % 2][:, 0:1], rstd[a % 2][:, :], SUB, MUL).then_inc(x2_done.sem, 1)

                def turn(it, peeled):
                    for a in range(N):
                        dve.wait_ge(hth_done.sem, hth_done.at(it, a + 1))
                        dve.tensor_tensor(htl[a % 2][:, :, :].rearrange("p c q -> p (c q)"), ps_t[a % 2][:, :],
                                          f32(hth[a % 2][:, :, :].rearrange("p c q -> p (c q)")), SUB).then_inc(htl_done.sem, 1)
                        if not (peeled and a == 0):
                            norm(it, a - 1, (a - 1) % N)
                        low_x(it, a + 2)
                        if not peeled:
                            dve.wait_ge(sent[a].sem, sent[a].at(it, 0))
                        dve.tensor_copy(ids[a][:, :], xin[a][:, D + 1:ROW])
                        dve.wait_ge(y_ready.sem, y_ready.at(it, a + 1))
                        dve.scalar_tensor_tensor(out=r[a % 2][:, :], in0=ps_y[a % 2][:, 0:D], scalar=xin[a % N][:, D:D + 1],
                                                 in1=xin[a % N][:, 0:D], op0=MUL, op1=ADD).then_inc(r_done.sem, 1)
                        dve.wait_ge(r_done.sem, r_done.at(it, a + 1))
                        dve.bn_stats(stats[:, :], r[a % 2][:, :]).then_inc(st_done.sem, 1)
                        dve.wait_ge(st_done.sem, st_done.at(it, a + 1))
                        dve.nop(nofuse=True)
                        dve.bn_aggr(mv[a % 2][:, :], stats[:, :]).then_inc(mv_done.sem, 1)

                low_x(0, 0)
                low_x(0, 1)
                turn(0, True)
                with dve.Fori(1, TURNS) as it:
                    turn(it, False)
                norm(TURNS, -1, N - 1)

            @block.gpsimd
            def _(pool):
                def send(it, a, at):
                    pool.wait_ge(x2_done.sem, x2_done.at(it, a + 1))
                    pool.nop(nofuse=True)
                    pool.indirect_dma_start(out=dr["x2"][:, :], out_offset=bass.IndirectOffsetOnAxis(ap=ids[at][:, :], axis=0),
                                            in_=x2[at][:, :], in_offset=None, bounds_check=T - 1, oob_is_err=False
                                            ).then_inc(sent[at].sem, 16)

                def turn(it, peeled):
                    for a in range(N):
                        pool.wait_ge(mv_done.sem, mv_done.at(it, a + 1))
                        pool.tensor_tensor(ve[:, :], mv[a % 2][:, 1:2], m["eps"][:, :], ADD).then_inc(ve_done.sem, 1)
                        pool.wait_ge(ve_done.sem, ve_done.at(it, a + 1))
                        pool.tensor_tensor(rstd[a % 2][:, :], ve[:, :], m["mhalf"][:, :], ALU.pow).then_inc(rstd_done.sem, 1)
                        if not (peeled and a == 0):
                            send(it, a - 1, (a - 1) % N)

                turn(0, True)
                with pool.Fori(1, TURNS) as it:
                    turn(it, False)
                send(TURNS, -1, N - 1)
                for i in range(N):
                    pool.wait_ge(sent[i].sem, 16 * TURNS)



FC = FF // P
GW = 4 * P
LIF_STEPS, BETA, THRESHOLD = 5, 0.9, 1.0


def quads(u):
    return u // 4 + 1


def quad_at(u, q):
    return sum(quads(v) for v in range(u)) + q


QUADS = quad_at(TILES, 0)

ORDER = [("prep", 0), ("first", 0), ("attend", 0), ("attend", 1), ("attend", 2)]
for _g in range(GROUPS - 1):
    ORDER += [("prep", _g + 1), ("attend", 4 * _g + 3), ("attend", 4 * _g + 4), ("attend", 4 * _g + 5), ("feed", _g), ("attend", 4 * _g + 6)]
ORDER += [("attend", TILES - 1), ("feed", GROUPS - 1)]
LIF_AT = {4 * g + 6 + k: (g, (k,)) for g in range(GROUPS - 2) for k in range(4)}
LIF_AT[TILES - 2] = (GROUPS - 2, (0, 1))
LIF_AT[TILES - 1] = (GROUPS - 2, (2, 3))


def setup_layer1(nc, ctx, dr, c):
    def keep(name, shape, dt):
        return ctx.enter_context(nc.sbuf_tensor("l_" + name, shape, dt))

    m = {}
    m["R"] = [keep("R" + x, [P, KC, D], F32R) for x in "hl"]
    m["fc"] = [keep("fc" + x, [P, KC, FF], F32R) for x in "hl"]
    m["pj"] = [keep("pj" + x, [P, FC, D], F32R) for x in "hl"]
    m["ident"], m["mhalf"], m["eps"] = c["ident"], c["mhalf"], c["eps"]
    m["ident_r"], m["mask"] = keep("ident_r", [P, P], F32R), keep("mask", [P, P], F32R)
    with ExitStack() as tmp:
        def stage(name, shape):
            return tmp.enter_context(nc.sbuf_tensor("v_" + name, shape, F32))

        rawR, rawf, rawp = stage("R", [P, KC, D]), stage("fc", [P, KC, FF]), stage("pj", [P, FC, D])
        parts = [(m["R"], rawR), (m["fc"], rawf), (m["pj"], rawp)]
        got = [nc.alloc_semaphore(f"v_got{i}") for i in range(3)]
        high = nc.alloc_semaphore("v_high")
        with nc.Block() as block:
            @block.sync
            def _(sp):
                sp.dma_start(rawR[:, :, :], dr["R"].rearrange("(k p) n -> p k n", p=P)).then_inc(got[0], 16)
                sp.dma_start(rawf[:, :, :], dr["fcT"].rearrange("(k p) n -> p k n", p=P)).then_inc(got[1], 16)
                sp.dma_start(rawp[:, :, :], dr["pjT"].rearrange("(k p) n -> p k n", p=P)).then_inc(got[2], 16)

            @block.scalar
            def _(act):
                for i, (pair, raw) in enumerate(parts):
                    act.wait_ge(got[i], 16)
                    act.activation(pair[0][:, :, :], raw[:, :, :], ACT.Copy).then_inc(high, 1)
                act.activation(m["ident_r"][:, :], c["ident"][:, :], ACT.Copy)
                act.activation(m["mask"][:, :], c["later"][:, :], ACT.Copy)

            @block.vector
            def _(dve):
                for i, (pair, raw) in enumerate(parts):
                    dve.wait_ge(high, i + 1)
                    dve.tensor_tensor(pair[1][:, :, :], raw[:, :, :], f32(pair[0][:, :, :]), SUB)
    return m


def layer1(nc, dr, m):
    ctx = ExitStack()

    def sb(name, shape, dt):
        return ctx.enter_context(nc.sbuf_tensor("c_" + name, shape, dt))

    with ctx:
        x2 = [sb(f"x2{i}", [P, 4, D], F32) for i in range(GROUPS)]
        xh, xl = sb("xh", [P, KC, S], F32R), sb("xl", [P, KC, S], F32R)
        vh, vl = sb("vh", [P, TILES, D], F16), sb("vl", [P, TILES, D], F16)
        eh, el = sb("eh", [P, KC, GW], F32R), sb("el", [P, KC, GW], F32R)
        nmax, ssum = [sb(f"nmax{i}", [P, 1], F32) for i in range(2)], [sb(f"ssum{i}", [P, 1], F32) for i in range(2)]
        rinv = sb("rinv", [P, 1], F32)
        prob = [sb(f"prob{i}", [P, S], F32) for i in range(2)]
        pth, ptl = [sb(f"pth{i}", [P, GW], F16) for i in range(2)], [sb(f"ptl{i}", [P, GW], F16) for i in range(2)]
        r = [sb(f"r{i}", [P, D], F32) for i in range(2)]
        stats, mv = sb("stats", [P, 6], F32), [sb(f"mv{i}", [P, 2], F32) for i in range(2)]
        ve, rstd = sb("ve", [P, 1], F32), [sb(f"rstd{i}", [P, 1], F32) for i in range(2)]
        x3 = [sb(f"x3{i}", [P, 4, D], F32) for i in range(3)]
        th, tl = sb("th", [P, 2, KC, 2 * P], F32R), sb("tl", [P, 2, KC, 2 * P], F32R)
        rl = [sb(f"rl{i}", [P, GW], F32) for i in range(2)]
        sq = [sb(f"sq{i}", [P, GW], F32) for i in range(2)]
        hh, hl = [sb(f"hh{i}", [P, GW], F32R) for i in range(2)], [sb(f"hl{i}", [P, GW], F32R) for i in range(2)]
        y, neg, drive, cnt = (sb(name, [P, 4 * D], F32) for name in ("y", "neg", "drive", "cnt"))
        fstats, fmv = sb("fstats", [P, 4, 6], F32), sb("fmv", [P, 4, 2], F32)
        fve, frstd = sb("fve", [P, 4], F32), sb("frstd", [P, 4], F32)
        fin = sb("fin", [P, 4, D], F32)

        ps_s = ctx.enter_context(nc.psum_tensor("c_ps_s", [P, S], F32))
        ps_t = [ctx.enter_context(nc.psum_tensor(f"c_ps_t{i}", [P, GW], F32)) for i in range(2)]
        ps_o = ctx.enter_context(nc.psum_tensor("c_ps_o", [P, GW], F32))
        ps_m = ctx.enter_context(nc.psum_tensor("c_ps_m", [P, GW], F32))

        def sig(name, per, credit=0):
            return Signal(nc, "c_" + name, per, credit)

        got = [sig(f"got{i}", 16) for i in range(GROUPS)]
        xt_ready, xh_done, xl_done = sig("xt_ready", 2 * GROUPS), sig("xh_done", 2 * GROUPS), sig("xl_done", 2 * GROUPS)
        vh_done, vl_done = sig("vh_done", GROUPS), sig("vl_done", GROUPS)
        e_ready, eh_done, el_done = sig("e_ready", 2 * GROUPS), sig("eh_done", 2 * GROUPS), sig("el_done", 2 * GROUPS)
        s_ready, max_done, exp_done = sig("s_ready", TILES), sig("max_done", TILES), sig("exp_done", TILES)
        t_ready, pth_done, ptl_done = sig("t_ready", QUADS), sig("pth_done", QUADS), sig("ptl_done", QUADS)
        o_ready, rinv_done, r_done = sig("o_ready", TILES), sig("rinv_done", TILES), sig("r_done", TILES, TILES)
        st_done, mv_done, ve_done, rstd_done, x3_done = (sig(n, TILES) for n in ("st_done", "mv_done", "ve_done", "rstd_done", "x3_done"))
        tt_ready, th_done, tl_done = sig("tt_ready", 2 * GROUPS), sig("th_done", 2 * GROUPS), sig("tl_done", 2 * GROUPS)
        h_ready, rl_done, sq_done = sig("h_ready", FC * GROUPS), sig("rl_done", FC * GROUPS), sig("sq_done", FC * GROUPS)
        hh_done, hl_done = sig("hh_done", FC * GROUPS), sig("hl_done", FC * GROUPS)
        y_ready, y_done = sig("y_ready", GROUPS), sig("y_done", 2 * GROUPS, 2)
        lif, lif_drive = sig("lif", (3 * LIF_STEPS - 2) * GROUPS), None
        r4_done, fst_done, fmv_done, fve_done, frstd_done, fin_done = (sig(n, GROUPS) for n in ("r4_done", "fst_done", "fmv_done", "fve_done", "frstd_done", "fin_done"))
        out_done = sig("out_done", 16 * GROUPS)

        with nc.Block() as block:
            @block.vector
            def _(dve):
                dve.sem_inc(r_done.sem, TILES)
                dve.sem_inc(y_done.sem, 2)

        with nc.Block() as block:
            @block.sync
            def _(sp):
                with sp.Fori(0, B) as b:
                    for g in range(GROUPS):
                        sp.wait_ge(r_done.sem, r_done.at(b, 4 * g + 4 - TILES))
                        sp.dma_start(x2[g][:, :, :], dr["x2"][bass.ds(b * S + g * GW, GW), :].rearrange("(j p) d -> p j d", p=P)
                                     ).then_inc(got[g].sem, 16)

            @block.gpsimd
            def _(pool):
                def deviation(b, u):
                    pool.wait_ge(mv_done.sem, mv_done.at(b, u + 1))
                    pool.tensor_tensor(ve[:, :], mv[u % 2][:, 1:2], m["eps"][:, :], ADD).then_inc(ve_done.sem, 1)
                    pool.wait_ge(ve_done.sem, ve_done.at(b, u + 1))
                    pool.tensor_tensor(rstd[u % 2][:, :], ve[:, :], m["mhalf"][:, :], ALU.pow).then_inc(rstd_done.sem, 1)

                def finish(b, g):
                    pool.wait_ge(fmv_done.sem, fmv_done.at(b, g + 1))
                    if g:
                        pool.wait_ge(out_done.sem, out_done.at(b, 16 * g))
                    pool.tensor_tensor(fve[:, :], fmv[:, :, 1:2].rearrange("p j a -> p (j a)"), m["eps"][:, :].broadcast_to([P, 4]), ADD).then_inc(fve_done.sem, 1)
                    pool.wait_ge(fve_done.sem, fve_done.at(b, g + 1))
                    pool.tensor_tensor(frstd[:, :], fve[:, :], m["mhalf"][:, :].broadcast_to([P, 4]), ALU.pow).then_inc(frstd_done.sem, 1)
                    pool.wait_ge(fin_done.sem, fin_done.at(b, g + 1))
                    pool.nop(nofuse=True)
                    pool.dma_start(dr["out"][bass.ds(b * S + g * GW, GW), :].rearrange("(j p) d -> p j d", p=P), fin[:, :, :]
                                   ).then_inc(out_done.sem, 16)

                with pool.Fori(0, B) as b:
                    for kind, i in ORDER:
                        if kind == "prep":
                            pool.wait_ge(got[i].sem, got[i].at(b, 16))
                            pool.wait_ge(xt_ready.sem, xt_ready.at(b, 2 * i + 1))
                            pool.nop(nofuse=True)
                            pool.tensor_copy(vh[:, 4 * i:4 * i + 4, :], x2[i][:, :, :]).then_inc(vh_done.sem, 1)
                            pool.wait_ge(vh_done.sem, vh_done.at(b, i + 1))
                            pool.tensor_tensor(vl[:, 4 * i:4 * i + 4, :], x2[i][:, :, :], vh[:, 4 * i:4 * i + 4, :], SUB).then_inc(vl_done.sem, 1)
                        if kind == "attend":
                            deviation(b, i)
                            if i in LIF_AT and LIF_AT[i][1][-1] == 3:
                                finish(b, LIF_AT[i][0])
                    finish(b, GROUPS - 1)
                    pool.wait_ge(out_done.sem, out_done.at(b, 16 * GROUPS))

            @block.scalar
            def _(act):
                with act.Fori(0, B) as b:
                    def high_p(u, q):
                        n = quad_at(u, q)
                        width = min(4, u + 1 - 4 * q) * P
                        act.wait_ge(t_ready.sem, t_ready.at(b, n + 1))
                        act.activation(pth[q % 2][:, 0:width], ps_t[q % 2][:, 0:width], ACT.Copy).then_inc(pth_done.sem, 1)

                    def exps(u):
                        act.wait_ge(max_done.sem, max_done.at(b, u + 1))
                        w = P * (u + 1)
                        act.activation(prob[u % 2][:, 0:w], ps_s[:, 0:w], ACT.Exp, bias=nmax[u % 2][:, :], accum_out=ssum[u % 2][:, :]
                                       ).then_inc(exp_done.sem, 1)

                    for kind, i in ORDER:
                        if kind == "prep":
                            for a in range(2):
                                act.wait_ge(xt_ready.sem, xt_ready.at(b, 2 * i + a + 1))
                                act.activation(xh[:, :, GW * i + 2 * P * a:GW * i + 2 * P * a + 2 * P],
                                               ps_t[a][:, :].rearrange("p (k q) -> p k q", k=KC), ACT.Copy).then_inc(xh_done.sem, 1)
                            for a in range(2):
                                act.wait_ge(e_ready.sem, e_ready.at(b, 2 * i + a + 1))
                                act.activation(eh[:, a, :], (ps_m if a == 0 else ps_t[0])[:, :], ACT.Copy).then_inc(eh_done.sem, 1)
                        if kind == "first":
                            exps(0)
                        if kind == "attend":
                            nq = quads(i)
                            for q in range(nq):
                                if q == nq - 1 and nq >= 3 and i + 1 < TILES:
                                    exps(i + 1)
                                high_p(i, q)
                            if nq < 3 and i + 1 < TILES:
                                exps(i + 1)
                        if kind == "feed":
                            for a in range(2):
                                act.wait_ge(tt_ready.sem, tt_ready.at(b, 2 * i + a + 1))
                                act.activation(th[:, a, :, :].rearrange("p k q -> p (k q)"), ps_t[a][:, :], ACT.Copy).then_inc(th_done.sem, 1)
                            for f in range(FC):
                                n = FC * i + f
                                act.wait_ge(h_ready.sem, h_ready.at(b, n + 1))
                                act.activation(rl[f % 2][:, :], ps_t[f % 2][:, :], ACT.Relu).then_inc(rl_done.sem, 1)
                                act.wait_ge(rl_done.sem, rl_done.at(b, n + 1))
                                if f >= 2:
                                    act.wait_ge(hl_done.sem, hl_done.at(b, n - 1))
                                act.activation(sq[f % 2][:, :], rl[f % 2][:, :], ACT.Square).then_inc(sq_done.sem, 1)
                                act.wait_ge(sq_done.sem, sq_done.at(b, n + 1))
                                act.activation(hh[f % 2][:, :], sq[f % 2][:, :], ACT.Copy).then_inc(hh_done.sem, 1)
                            act.wait_ge(y_ready.sem, y_ready.at(b, i + 1))
                            if i:
                                act.wait_ge(r4_done.sem, r4_done.at(b, i))
                            act.activation(y[:, 0:2 * D], ps_m[:, :], ACT.Copy).then_inc(y_done.sem, 1)
                            act.activation(y[:, 2 * D:4 * D], ps_o[:, :], ACT.Copy).then_inc(y_done.sem, 1)

            @block.tensor
            def _(pe):
                with pe.Fori(0, B) as b:
                    def scores(u):
                        g, tile = u // 4, slice(P * (u % 4), P * (u % 4) + P)
                        for c in range(g + 1):
                            w = GW if c < g else P * (u % 4 + 1)
                            out = ps_s[:, GW * c:GW * c + w]
                            for k in range(KC):
                                keys = slice(GW * c, GW * c + w)
                                ins = mm_split(pe, out, eh[:, k, tile], el[:, k, tile], xh[:, k, keys], xl[:, k, keys],
                                               k == 0, k == KC - 1 and c < g)
                        ins = pe.matmul(ps_s[:, P * u:P * u + P], m["ident_r"][:, :], m["mask"][:, :], start=False, stop=True)
                        ins.then_inc(s_ready.sem, 1)

                    def turn_p(u, q):
                        for j in range(min(4, u + 1 - 4 * q)):
                            at = P * (4 * q + j)
                            ins = pe.transpose(ps_t[q % 2][:, P * j:P * j + P], prob[u % 2][:, at:at + P], m["ident"][:, :])
                        ins.then_inc(t_ready.sem, 1)

                    def values(u, q):
                        n = quad_at(u, q)
                        pe.wait_ge(pth_done.sem, pth_done.at(b, n + 1))
                        pe.wait_ge(ptl_done.sem, ptl_done.at(b, n + 1))
                        if q == 0:
                            pe.wait_ge(r_done.sem, r_done.at(b, u))
                        for j in range(min(4, u + 1 - 4 * q)):
                            t, blk = 4 * q + j, slice(P * j, P * j + P)
                            out = ps_o[:, 0:D]
                            pe.matmul(out, pth[q % 2][:, blk], vh[:, t, :], start=t == 0, stop=False)
                            pe.matmul(out, pth[q % 2][:, blk], vl[:, t, :], start=False, stop=False)
                            ins = pe.matmul(out, ptl[q % 2][:, blk], vh[:, t, :], start=False, stop=t == u)
                        if q == quads(u) - 1:
                            ins.then_inc(o_ready.sem, 1)

                    fed = 0
                    for kind, i in ORDER:
                        if kind == "prep":
                            pe.wait_ge(got[i].sem, got[i].at(b, 16))
                            for a in range(2):
                                for j in range(2):
                                    for k in range(KC):
                                        ins = pe.transpose(ps_t[a][:, 2 * P * k + P * j:2 * P * k + P * j + P],
                                                           x2[i][:, 2 * a + j, P * k:P * k + P], m["ident"][:, :])
                                ins.then_inc(xt_ready.sem, 1)
                            pe.wait_ge(xh_done.sem, xh_done.at(b, 2 * i + 2))
                            pe.wait_ge(xl_done.sem, xl_done.at(b, 2 * i + 2))
                            pe.wait_ge(y_done.sem, y_done.at(b, 2 * fed))
                            for a in range(2):
                                for k in range(KC):
                                    keys = slice(GW * i, GW * i + GW)
                                    ins = mm_split(pe, (ps_m if a == 0 else ps_t[0])[:, :], m["R"][0][:, k, P * a:P * a + P],
                                                   m["R"][1][:, k, P * a:P * a + P], xh[:, k, keys], xl[:, k, keys], k == 0, k == KC - 1)
                                ins.then_inc(e_ready.sem, 1)
                        if kind == "first":
                            pe.wait_ge(eh_done.sem, eh_done.at(b, 2))
                            pe.wait_ge(el_done.sem, el_done.at(b, 2))
                            scores(0)
                        if kind == "attend":
                            u, nq = i, quads(i)
                            pe.wait_ge(exp_done.sem, exp_done.at(b, u + 1))
                            if u % 4 == 3 and u + 1 < TILES:
                                pe.wait_ge(eh_done.sem, eh_done.at(b, 2 * (u // 4) + 4))
                                pe.wait_ge(el_done.sem, el_done.at(b, 2 * (u // 4) + 4))
                            turn_p(u, 0)
                            if nq > 1:
                                turn_p(u, 1)
                            if u + 1 < TILES:
                                scores(u + 1)
                            if u % 4 == 0:
                                pe.wait_ge(vl_done.sem, vl_done.at(b, u // 4 + 1))
                            if fed:
                                pe.wait_ge(y_done.sem, y_done.at(b, 2 * fed))
                            else:
                                pe.wait_ge(y_done.sem, y_done.at(b, 0))
                            for q in range(nq):
                                values(u, q)
                                if q + 2 < nq:
                                    turn_p(u, q + 2)
                        if kind == "feed":
                            pe.wait_ge(x3_done.sem, x3_done.at(b, 4 * i + 4))
                            for a in range(2):
                                for j in range(2):
                                    for k in range(KC):
                                        ins = pe.transpose(ps_t[a][:, 2 * P * k + P * j:2 * P * k + P * j + P],
                                                           x3[i % 3][:, 2 * a + j, P * k:P * k + P], m["ident"][:, :])
                                ins.then_inc(tt_ready.sem, 1)
                            pe.wait_ge(th_done.sem, th_done.at(b, 2 * i + 2))
                            pe.wait_ge(tl_done.sem, tl_done.at(b, 2 * i + 2))
                            for f in range(FC + 1):
                                if f < FC:
                                    fs = slice(P * f, P * f + P)
                                    if f >= 2:
                                        pe.wait_ge(rl_done.sem, rl_done.at(b, FC * i + f - 1))
                                    for k in range(KC):
                                        ins = mm_split(pe, ps_t[f % 2][:, :], m["fc"][0][:, k, fs], m["fc"][1][:, k, fs],
                                                       th[:, :, k, :], tl[:, :, k, :], k == 0, k == KC - 1)
                                    ins.then_inc(h_ready.sem, 1)
                                if f == 1:
                                    last = {0: 5, 1: 9, 2: 13, 3: 15}[i]
                                    pe.wait_ge(r_done.sem, r_done.at(b, last + 1))
                                if f >= 1:
                                    n = FC * i + f
                                    pe.wait_ge(hh_done.sem, hh_done.at(b, n))
                                    pe.wait_ge(hl_done.sem, hl_done.at(b, n))
                                    for j in range(4):
                                        tok = slice(P * j, P * j + P)
                                        out = (ps_m if j < 2 else ps_o)[:, D * (j % 2):D * (j % 2) + D]
                                        h_, l_ = hh[(f - 1) % 2][:, tok], hl[(f - 1) % 2][:, tok]
                                        wh, wl = m["pj"][0][:, f - 1, :], m["pj"][1][:, f - 1, :]
                                        pe.matmul(out, h_, wh, start=f == 1 and j % 2 == 0, stop=False, skip_group_check=True)
                                        pe.matmul(out, h_, wl, start=False, stop=False, skip_group_check=True)
                                        ins = pe.matmul(out, l_, wh, start=False, stop=f == FC, skip_group_check=True)
                            ins.then_inc(y_ready.sem, 1)
                            fed = i + 1

            @block.vector
            def _(dve):
                with dve.Fori(0, B) as b:
                    def low_p(u, q):
                        n = quad_at(u, q)
                        width = min(4, u + 1 - 4 * q) * P
                        dve.wait_ge(pth_done.sem, pth_done.at(b, n + 1))
                        dve.tensor_tensor(ptl[q % 2][:, 0:width], ps_t[q % 2][:, 0:width], pth[q % 2][:, 0:width], SUB).then_inc(ptl_done.sem, 1)

                    def maximum(u):
                        dve.wait_ge(s_ready.sem, s_ready.at(b, u + 1))
                        dve.tensor_reduce(nmax[u % 2][:, :], ps_s[:, 0:P * (u + 1)], AX.X, MAXOP, negate=True).then_inc(max_done.sem, 1)

                    def normalise(u):
                        dve.wait_ge(rstd_done.sem, rstd_done.at(b, u + 1))
                        dve.tensor_scalar(x3[(u // 4) % 3][:, u % 4, :], r[u % 2][:, :], mv[u % 2][:, 0:1], rstd[u % 2][:, :], SUB, MUL
                                          ).then_inc(x3_done.sem, 1)

                    def lif_step(g, k):
                        at = (3 * LIF_STEPS - 2) * g + (1 + 3 * k if k else 0)
                        if k == 0:
                            dve.wait_ge(y_done.sem, y_done.at(b, 2 * g + 2))
                            dve.tensor_scalar(cnt[:, :], y[:, :], THRESHOLD, None, ALU.is_gt).then_inc(lif.sem, 1)
                            dve.scalar_tensor_tensor(out=drive[:, :], in0=y[:, :], scalar=-BETA, in1=y[:, :], op0=MUL, op1=SUB).then_inc(lif.sem, 1)
                            dve.wait_ge(lif.sem, lif.at(b, at + 2))
                            dve.scalar_tensor_tensor(out=neg[:, :], in0=y[:, :], scalar=THRESHOLD, in1=drive[:, :], op0=ALU.is_gt, op1=ADD).then_inc(lif.sem, 1)
                            at += 1
                        else:
                            dve.wait_ge(lif.sem, lif.at(b, at))
                            dve.scalar_tensor_tensor(out=drive[:, :], in0=neg[:, :], scalar=BETA, in1=y[:, :], op0=MUL, op1=SUB).then_inc(lif.sem, 1)
                            dve.wait_ge(lif.sem, lif.at(b, at + 1))
                            dve.scalar_tensor_tensor(out=neg[:, :], in0=neg[:, :], scalar=-THRESHOLD, in1=drive[:, :], op0=ALU.is_lt, op1=ADD).then_inc(lif.sem, 1)
                        dve.wait_ge(lif.sem, lif.at(b, at + 2))
                        dve.scalar_tensor_tensor(out=cnt[:, :], in0=neg[:, :], scalar=-THRESHOLD, in1=cnt[:, :], op0=ALU.is_lt, op1=ADD).then_inc(lif.sem, 1)

                    def finish(g):
                        dve.wait_ge(lif.sem, lif.at(b, (3 * LIF_STEPS - 2) * (g + 1)))
                        dve.scalar_tensor_tensor(out=neg[:, :], in0=cnt[:, :], scalar=1.0 / LIF_STEPS,
                                                 in1=x3[g % 3][:, :, :].rearrange("p j d -> p (j d)"), op0=MUL, op1=ADD).then_inc(r4_done.sem, 1)
                        dve.wait_ge(r4_done.sem, r4_done.at(b, g + 1))
                        for j in range(4):
                            ins = dve.bn_stats(fstats[:, j, :], neg[:, D * j:D * j + D])
                        ins.then_inc(fst_done.sem, 1)
                        dve.wait_ge(fst_done.sem, fst_done.at(b, g + 1))
                        dve.nop(nofuse=True)
                        for j in range(4):
                            ins = dve.bn_aggr(fmv[:, j, :], fstats[:, j, :])
                        ins.then_inc(fmv_done.sem, 1)

                    def result(g):
                        dve.wait_ge(frstd_done.sem, frstd_done.at(b, g + 1))
                        for j in range(4):
                            ins = dve.tensor_scalar(fin[:, j, :], neg[:, D * j:D * j + D], fmv[:, j, 0:1], frstd[:, j:j + 1], SUB, MUL)
                        ins.then_inc(fin_done.sem, 1)

                    for kind, i in ORDER:
                        if kind == "prep":
                            for a in range(2):
                                dve.wait_ge(xh_done.sem, xh_done.at(b, 2 * i + a + 1))
                                at = slice(GW * i + 2 * P * a, GW * i + 2 * P * a + 2 * P)
                                dve.tensor_tensor(xl[:, :, at], ps_t[a][:, :].rearrange("p (k q) -> p k q", k=KC), f32(xh[:, :, at]), SUB
                                                  ).then_inc(xl_done.sem, 1)
                            for a in range(2):
                                dve.wait_ge(eh_done.sem, eh_done.at(b, 2 * i + a + 1))
                                dve.tensor_tensor(el[:, a, :], (ps_m if a == 0 else ps_t[0])[:, :], f32(eh[:, a, :]), SUB).then_inc(el_done.sem, 1)
                        if kind == "first":
                            maximum(0)
                        if kind == "attend":
                            u, nq = i, quads(i)
                            low_p(u, 0)
                            if nq > 1:
                                low_p(u, 1)
                            if u + 1 < TILES:
                                maximum(u + 1)
                            for q in range(2, nq):
                                low_p(u, q)
                            steps = LIF_AT.get(u)
                            if steps:
                                for k in steps[1]:
                                    lif_step(steps[0], k)
                                if steps[1][-1] == 3:
                                    finish(steps[0])
                            dve.wait_ge(exp_done.sem, exp_done.at(b, u + 1))
                            dve.reciprocal(rinv[:, :], ssum[u % 2][:, :]).then_inc(rinv_done.sem, 1)
                            dve.wait_ge(rinv_done.sem, rinv_done.at(b, u + 1))
                            dve.wait_ge(o_ready.sem, o_ready.at(b, u + 1))
                            dve.scalar_tensor_tensor(out=r[u % 2][:, :], in0=ps_o[:, 0:D], scalar=rinv[:, :], in1=x2[u // 4][:, u % 4, :],
                                                     op0=MUL, op1=ADD).then_inc(r_done.sem, 1)
                            dve.wait_ge(r_done.sem, r_done.at(b, u + 1))
                            dve.bn_stats(stats[:, :], r[u % 2][:, :]).then_inc(st_done.sem, 1)
                            dve.wait_ge(st_done.sem, st_done.at(b, u + 1))
                            dve.nop(nofuse=True)
                            dve.bn_aggr(mv[u % 2][:, :], stats[:, :]).then_inc(mv_done.sem, 1)
                            normalise(u)
                            if steps and steps[1][-1] == 3:
                                result(steps[0])
                        if kind == "feed":
                            for a in range(2):
                                dve.wait_ge(th_done.sem, th_done.at(b, 2 * i + a + 1))
                                dve.tensor_tensor(tl[:, a, :, :].rearrange("p k q -> p (k q)"), ps_t[a][:, :],
                                                  f32(th[:, a, :, :].rearrange("p k q -> p (k q)")), SUB).then_inc(tl_done.sem, 1)
                            for f in range(FC):
                                n = FC * i + f
                                dve.wait_ge(hh_done.sem, hh_done.at(b, n + 1))
                                dve.tensor_tensor(hl[f % 2][:, :], sq[f % 2][:, :], f32(hh[f % 2][:, :]), SUB).then_inc(hl_done.sem, 1)
                            if i == GROUPS - 1:
                                for k in range(4):
                                    lif_step(i, k)
                                finish(i)
                                result(i)


def model(nc, dr, const_at):
    dr["routed"] = nc.dram_tensor("routed", [PAD_ROW + P, ROW], F32, kind="Internal").ap()
    dr["x2"] = nc.dram_tensor("x2", [T, D], F32, kind="Internal").ap()
    with ExitStack() as shared:
        with ExitStack() as ctx:
            c = setup_layer0(nc, shared, ctx, dr, const_at)
            layer0_attention(nc, dr, c)
        with ExitStack() as ctx:
            m = setup_experts(nc, ctx, dr, c)
            experts(nc, dr, m)
        with ExitStack() as ctx:
            m = setup_layer1(nc, ctx, dr, c)
            layer1(nc, dr, m)


def kernel(**inputs):
    import concourse.bacc as bacc
    from concourse.bass_utils import run_bass_kernel_spmd

    nc = bacc.Bacc("TRN2", target_bir_lowering=False, num_devices=1)
    table, const_at = const_table()
    x = np.asarray(inputs["L0_attn_hidden_states"]).reshape(T, D)
    arrays = {
        "x": x, "xT": x.T.reshape(KC, P, T).transpose(1, 0, 2), "table": table,
        "wq": inputs["L0_attn_Wq"], "wk": inputs["L0_attn_Wk"], "wv": inputs["L0_attn_Wv"], "wo": inputs["L0_attn_Wo"],
        "w1": inputs["L0_attn_W1"], "b1": inputs["L0_attn_b1"], "w2": inputs["L0_attn_W2"],
        "b2": np.asarray(inputs["L0_attn_b2"]).reshape(KC, P).T, "wg": inputs["L0_ffn_Wg"], "bg": inputs["L0_ffn_bg"],
        "mw1": inputs["L0_ffn_W1"], "mb1": inputs["L0_ffn_b1"], "mw2": inputs["L0_ffn_W2"], "mb2": inputs["L0_ffn_b2"],
        "R": inputs["L1_attn_R"], "fcT": np.asarray(inputs["L1_ffn_W_fc"]).T, "pjT": np.asarray(inputs["L1_ffn_W_proj"]).T,
    }
    arrays = {f"in_{name}_dram": np.ascontiguousarray(a) for name, a in arrays.items()}
    dr = {name[3:-5]: nc.dram_tensor(name, a.shape, F32, kind="ExternalInput").ap() for name, a in arrays.items()}
    out = nc.dram_tensor("out_0_dram", [B, S, D], F32, kind="ExternalOutput").ap()
    dr["out"] = out.rearrange("b s d -> (b s) d")
    model(nc, dr, const_at)
    got = run_bass_kernel_spmd(nc, [arrays], core_ids=[0])
    return got.results[0]["out_0_dram"]
```

```python
from contextlib import ExitStack

import numpy as np
import concourse.bass as bass
from concourse import mybir

F32 = mybir.dt.float32
F32R = mybir.dt.float32r
BF16 = mybir.dt.bfloat16
F16 = mybir.dt.float16
I32 = mybir.dt.int32
ALU = mybir.AluOpType
ACT = mybir.ActivationFunctionType
AX = mybir.AxisListType
SUB, ADD, MUL, MAXOP = ALU.subtract, ALU.add, ALU.mult, ALU.max

P = 128
D = 256
KC = D // P
B, S = 4, 2048
T = B * S
TILES = S // P
CTX = 256
POOL = 64
HEADS, HD = 16, 16
VW = HD + 1
EXPERTS, HID = 8, 512
EXPERT_W = KC * HID
FF = 1024
EPS = 1e-5
HIDDEN_NEG = -1.0e30
MASKED = -1.0e9

CAP = T + P
PAD_ROW = EXPERTS * CAP
ROW = D + 2
ROUTED_TILES = T // P + EXPERTS - 1
OFF_LIST = 2.0 * T


class Signal:

    def __init__(self, nc, name, per, credit=0):
        self.sem, self.per, self.credit = nc.alloc_semaphore(name), per, credit

    def at(self, b, k):
        return b * self.per + (k + self.credit)


def f32(ap):
    return ap.bitcast(F32)


def raw_and_low(nc, ctx, name, shape):
    at = -(-nc.sbuf_base // 32) * 32
    raw = ctx.enter_context(nc.sbuf_tensor("raw_" + name, shape, F32))
    return raw, nc.alloc_sbuf_tensor_at("low_" + name, shape, F32R, offset=at)


def mm_split(pe, out, lh, ll, rh, rl, first, last):
    pe.matmul(out, lh, rh, start=first, stop=False)
    pe.matmul(out, lh, rl, start=False, stop=False)
    return pe.matmul(out, ll, rh, start=False, stop=last)


INIT_UNITS = 8
UNITS = INIT_UNITS + TILES - 2
BLOCKS = TILES // 2
GROUPS = TILES // 4


def last_unit(t):
    return 4 * t + 3 if t < 2 else t + INIT_UNITS - 2


def tile_of(n):
    if n in (3, 7):
        return n // 4
    return n - INIT_UNITS + 2 if INIT_UNITS <= n < UNITS else None


def block_at(n):
    return (n - 3) // 2 if n >= 5 and n % 2 and (n - 3) // 2 < BLOCKS else None


def turned_early(n):
    return n < UNITS and block_at(n) is None


def group_done(n, lag):
    t = tile_of(n - lag)
    return t // 4 if t is not None and t % 4 == 3 else None


def layer0_attention(nc, dr, c, raw_w, raw_got):
    ctx = ExitStack()

    def sb(name, shape, dt):
        return ctx.enter_context(nc.sbuf_tensor(name, shape, dt))

    with ctx:
        raw = [sb(f"a_raw{i}", [P, KC, 256], F32) for i in range(2)]
        xh = [sb(f"a_xh{i}", [P, KC, 256], F32R) for i in range(2)]
        xl = [sb(f"a_xl{i}", [P, KC, 256], F32R) for i in range(2)]
        rows_in = [sb(f"a_rows{i}", [P, 4, D], F32) for i in range(2)]
        qh = [sb(f"a_qh{i}", [P, KC, 256], F32R) for i in range(2)]
        ql = [sb(f"a_ql{i}", [P, KC, 256], F32R) for i in range(2)]
        h1 = sb("a_h1", [P, CTX], F32)
        hp = sb("a_hp", [P, POOL], F32)
        hph, hpl = sb("a_hph", [P, POOL], F32R), sb("a_hpl", [P, POOL], F32R)
        comp = sb("a_comp", [P, KC, POOL], F32)
        ch, cl = sb("a_ch", [P, KC, 2, POOL], F32R), sb("a_cl", [P, KC, 2, POOL], F32R)
        kih, kil = sb("a_kih", [P, KC, 2, CTX], F32R), sb("a_kil", [P, KC, 2, CTX], F32R)
        kcl = sb("a_kcl", [P, KC, POOL], F32)
        kchr = sb("a_kchr", [P, KC, POOL], F32R)
        kmh, kml = sb("a_kmh", [P, KC, 8, POOL], F32R), sb("a_kml", [P, KC, 8, POOL], F32R)
        vi = [sb(f"a_vi{i}", [P, 2, HEADS, VW], BF16) for i in range(3)]
        vir = [sb(f"a_vir{i}", [P, 2, D], F32) for i in range(2)]
        vc = [sb(f"a_vc{i}", [P, HEADS, VW], BF16) for i in range(3)]
        vcr = [sb(f"a_vcr{i}", [P, D], F32) for i in range(2)]
        mx = [sb(f"a_mx{i}", [P, HEADS], F32) for i in range(2)]
        mts = [sb(f"a_mts{i}", [HEADS, P], F32R) for i in range(2)]
        prob = [sb(f"a_prob{i}", [P, 1024], F32) for i in range(2)]
        pth, ptl = sb("a_pth", [P, 1024], F16), sb("a_ptl", [P, 1024], F16)
        rs = sb("a_rs", [P, HEADS], F32)
        o = [sb(f"a_o{i}", [P, HEADS, HD], F32) for i in range(2)]
        oth, otl = sb("a_oth", [P, KC, P], F32R), sb("a_otl", [P, KC, P], F32R)
        r = [sb(f"a_r{i}", [P, D], F32) for i in range(2)]
        stats, mv = sb("a_stats", [P, 6], F32), [sb(f"a_mv{i}", [P, 2], F32) for i in range(2)]
        ve = sb("a_ve", [P, 1], F32)
        rstd = [sb(f"a_rstd{i}", [P, 1], F32) for i in range(2)]
        rows = [sb(f"a_out{i}", [P, 4, ROW], F32) for i in range(2)]
        x1h = [sb(f"a_x1h{i}", [P, KC, P], F32R) for i in range(2)]
        x1l = [sb(f"a_x1l{i}", [P, KC, P], F32R) for i in range(2)]
        lga, lg = sb("a_lga", [P, 4, EXPERTS], F32), sb("a_lg", [P, 4, EXPERTS], F32)
        lmax, mkey = sb("a_lmax", [P, 4], F32), sb("a_mkey", [P, 4], F32)
        ld, lex = sb("a_ld", [P, 4, EXPERTS], F32), sb("a_lex", [P, 4, EXPERTS], F32)
        key = sb("a_key", [P, 4, EXPERTS], F32)
        key2 = sb("a_key2", [P, 4, EXPERTS], F32)
        oh = sb("a_oh", [P, 4, EXPERTS], BF16)
        lsum = sb("a_lsum", [P, 4], F32)
        pf, pf2 = sb("a_pf", [P, 4, EXPERTS], F32), sb("a_pf2", [P, 4, EXPERTS], F32)
        pos = [sb(f"a_pos{i}", [P, 4], I32) for i in range(2)]

        ps_s = [ctx.enter_context(nc.psum_tensor(f"a_ps_s{i}", [P, 1024], F32)) for i in range(2)]
        ps_t = [ctx.enter_context(nc.psum_tensor(f"a_ps_t{i}", [P, 512], F32)) for i in range(2)]
        ps_o = ctx.enter_context(nc.psum_tensor("a_ps_o", [P, 512], F32))
        ps_m = ctx.enter_context(nc.psum_tensor("a_ps_m", [P, 512], F32))
        OUT = ps_o[:, 0:HEADS * VW]
        MT = ps_m[:, 0:128]
        LG = ps_m[:, 128:192].rearrange("p (j a e) -> p j a e", j=4, a=2)
        PF = ps_m[:, 192:224]
        TOT = ps_m[:, 224:232]
        TURN = ps_t[1][:, 256:512]
        PROJ = ps_t[0][:, 0:256]
        X1T = ps_t[1][:, 0:256]
        KI, VI = ps_s[0][:, 0:512], ps_s[0][:, 512:1024]
        H1, CM = ps_s[1][:, 0:256], ps_s[1][:, 256:384]
        KCP, VCP = ps_s[1][:, 512:640], ps_s[1][:, 640:896]

        n_ = {}

        def sig(name, per, credit=0):
            n_[name] = Signal(nc, "a_" + name, per, credit)
            return n_[name]

        xt_in = [sig(f"xt_in{i}", 8 * BLOCKS) for i in range(2)]
        rows_got = [sig(f"rows_got{i}", 8 * GROUPS) for i in range(2)]
        xh_done, xl_done = sig("xh_done", BLOCKS), sig("xl_done", BLOCKS, 2)
        h1_ready, h1_done = sig("h1_ready", 1), sig("h1_done", 1)
        hp_sum, hp_done, hph_done, hpl_done = sig("hp_sum", 1), sig("hp_done", 1), sig("hph_done", 1), sig("hpl_done", 1)
        comp_ready, comp_done, ch_done, cl_done = sig("comp_ready", 1), sig("comp_done", 1), sig("ch_done", 1), sig("cl_done", 1)
        ki_ready, kih_done, kil_done = sig("ki_ready", 1), sig("kih_done", 1), sig("kil_done", 1)
        vi_ready, vi_hi, vi_mid = sig("vi_ready", 1), sig("vi_hi", 3), sig("vi_mid", 2)
        kc_ready, kch_done, kcl_done, kmh_done, kml_done = sig("kc_ready", 1), sig("kch_done", 1), sig("kcl_done", 1), sig("kmh_done", 1), sig("kml_done", 1)
        vc_hi, vc_mid = sig("vc_hi", 3), sig("vc_mid", 3)
        q_ready, qh_done, ql_done = sig("q_ready", BLOCKS), sig("qh_done", BLOCKS), sig("ql_done", BLOCKS)
        s_ready, max_done = sig("s_ready", UNITS), sig("max_done", UNITS)
        mt_ready, mts_done = sig("mt_ready", UNITS), sig("mts_done", UNITS)
        sh_ready, exp_done = sig("sh_ready", UNITS), sig("exp_done", UNITS)
        t_ready, pth_done, ptl_done = sig("t_ready", 2 * UNITS), sig("pth_done", 2 * UNITS), sig("ptl_done", 2 * UNITS)
        pv_ready, rs_done, o_done = sig("pv_ready", UNITS), sig("rs_done", UNITS), sig("o_done", UNITS, 1)
        ot_ready, oth_done, otl_done = sig("ot_ready", TILES), sig("oth_done", TILES), sig("otl_done", TILES)
        wo_ready, r_done, st_done, mv_done = sig("wo_ready", TILES), sig("r_done", TILES, 1), sig("st_done", TILES), sig("mv_done", TILES)
        ve_done, rstd_done, x1_done = sig("ve_done", TILES), sig("rstd_done", TILES), sig("x1_done", TILES)
        xt_ready, x1h_done, x1l_done = sig("xt_ready", TILES), sig("x1h_done", TILES), sig("x1l_done", TILES, 1)
        lg_ready, lga_done, lg_done = sig("lg_ready", TILES), sig("lga_done", GROUPS), sig("lg_done", GROUPS, 1)
        lm_done, ld_done, ex_done = sig("lm_done", GROUPS), sig("ld_done", GROUPS), sig("ex_done", GROUPS)
        key_done, oh_done = sig("key_done", 3 * GROUPS), sig("oh_done", GROUPS)
        pf_ready, base_read, base_done, pos_done = sig("pf_ready", GROUPS), sig("base_read", GROUPS), sig("base_done", GROUPS), sig("pos_done", GROUPS, 1)
        sel_done, lsum_done, row_done = sig("sel_done", GROUPS), sig("lsum_done", GROUPS), sig("row_done", 2 * GROUPS)
        ids_done = sig("ids_done", 1, 1)
        scattered = [sig(f"scattered{i}", 8 * TILES) for i in range(2)]

        credits = nc.Block()
        with credits as block:
            @block.vector
            def _(dve):
                dve.sem_inc(xl_done.sem, 2)
                dve.sem_inc(o_done.sem, 1)
                dve.sem_inc(r_done.sem, 1)
                dve.sem_inc(x1l_done.sem, 1)
                dve.sem_inc(lg_done.sem, 1)
                dve.sem_inc(pos_done.sem, 1)
                dve.sem_inc(ids_done.sem, 1)
                for i in range(3):
                    dve.memset(vi[i][:, :, :, HD:VW], 1.0 if i == 0 else 0.0)
                    if i:
                        dve.memset(vc[i][:, :, HD:VW], 0.0)
                dve.tensor_copy(vc[0][:, :, HD:VW], c["half"][:, :].rearrange("p (h a) -> p h a", a=1))

        with nc.Block() as block:

            @block.sync
            def _(sp):
                with sp.Fori(0, B) as b:
                    def rows_load(g):
                        if g >= 2:
                            sp.wait_ge(r_done.sem, r_done.at(b, 4 * (g - 1)))
                        else:
                            sp.wait_ge(r_done.sem, r_done.at(b, 0))
                        sp.dma_start(rows_in[g % 2][:, :, :],
                                     dr["x"][bass.ds(b * S + g * 512, 512), :].rearrange("(j p) d -> p j d", p=P)
                                     ).then_inc(rows_got[g % 2].sem, 16)

                    for k in range(BLOCKS):
                        sp.wait_ge(xl_done.sem, xl_done.at(b, k - 1))
                        if k >= 2:
                            sp.wait_ge(xh_done.sem, xh_done.at(b, k - 1))
                        sp.dma_start(raw[k % 2][:, :, :],
                                     dr["xT"][:, :, bass.ds(b * S + k * 256, 256)]).then_inc(xt_in[k % 2].sem, 16)
                        if k % 2:
                            rows_load(k // 2)
                            w, e = raw_w[k // 2 % 2][0], b * (EXPERTS // B) + k // 4
                            src = dr[("mw1", "mw2")[k // 2 % 2]][bass.ds(e, 1), :, :].rearrange("e (c p) n -> p (e c) n", p=P)
                            sp.dma_start(w[:, bass.ds(e * EXPERT_W, EXPERT_W)].rearrange("p (c n) -> p c n", c=src.shape[1]), src
                                         ).then_inc(raw_got, 16)

            @block.gpsimd
            def _(pool):
                with pool.Fori(0, B) as b:
                    def split_x(k):
                        pool.wait_ge(xh_done.sem, xh_done.at(b, k + 1))
                        pool.tensor_tensor(xl[k % 2][:, :, :], raw[k % 2][:, :, :], f32(xh[k % 2][:, :, :]), SUB).then_inc(xl_done.sem, 1)

                    split_x(0)
                    pool.wait_ge(kcl_done.sem, kcl_done.at(b, 1))
                    pool.tensor_tensor(kml[:, :, :, :],
                                       kcl[:, :, :].unsqueeze(2).broadcast_to([P, KC, 8, POOL]),
                                       c["head"][:, :].unsqueeze(1).unsqueeze(3).broadcast_to([P, KC, 8, POOL]),
                                       MUL).then_inc(kml_done.sem, 1)
                    for n in range(0, UNITS + 5):
                        t = tile_of(n - 2)
                        if t is not None:
                            pool.wait_ge(mv_done.sem, mv_done.at(b, t + 1))
                            pool.tensor_tensor(ve[:, :], mv[t % 2][:, 1:2], c["eps"][:, :], ADD).then_inc(ve_done.sem, 1)
                            pool.wait_ge(ve_done.sem, ve_done.at(b, t + 1))
                            pool.tensor_tensor(rstd[t % 2][:, :], ve[:, :], c["mhalf"][:, :], ALU.pow).then_inc(rstd_done.sem, 1)
                            g = t // 4
                            if t % 4 == 0 and g >= 2:
                                pool.wait_ge(scattered[g % 2].sem, scattered[g % 2].at(b, 64 * (g // 2)))
                            pool.wait_ge(rstd_done.sem, rstd_done.at(b, t + 1))
                            pool.nop(nofuse=True)
                            pool.tensor_scalar(rows[g % 2][:, t % 4, 0:D], r[t % 2][:, :], mv[t % 2][:, 0:1], rstd[t % 2][:, :], SUB, MUL
                                               ).then_inc(x1_done.sem, 1)
                        k = block_at(n + 2)
                        if k is not None:
                            split_x(k)
                        g = group_done(n, 5)
                        if g is not None:
                            pool.wait_ge(pos_done.sem, pos_done.at(b, g + 1))
                            pool.wait_ge(row_done.sem, row_done.at(b, 2 * g + 2))
                            pool.nop(nofuse=True)
                            for j in range(4):
                                pool.indirect_dma_start(
                                    out=dr["routed"][:, :],
                                    out_offset=bass.IndirectOffsetOnAxis(ap=pos[g % 2][:, j:j + 1], axis=0),
                                    in_=rows[g % 2][:, j, :], in_offset=None).then_inc(scattered[g % 2].sem, 16)
                    for i in range(2):
                        pool.wait_ge(scattered[i].sem, scattered[i].at(b, 8 * TILES))

            @block.scalar
            def _(act):
                with act.Fori(0, B) as b:
                    def split_x(k):
                        act.wait_ge(xt_in[k % 2].sem, xt_in[k % 2].at(b, 16 * (k // 2 + 1)))
                        if k >= 2:
                            act.wait_ge(q_ready.sem, q_ready.at(b, k - 1))
                            act.wait_ge(vi_ready.sem, vi_ready.at(b, 1))
                        act.activation(xh[k % 2][:, :, :], raw[k % 2][:, :, :], ACT.Copy).then_inc(xh_done.sem, 1)

                    def project_q(k):
                        act.wait_ge(q_ready.sem, q_ready.at(b, k + 1))
                        act.activation(qh[k % 2][:, :, :].rearrange("p c q -> p (c q)"), ps_t[1][:, :], ACT.Copy).then_inc(qh_done.sem, 1)

                    split_x(0)
                    act.wait_ge(ki_ready.sem, ki_ready.at(b, 1))
                    for a in range(2):
                        ins = act.activation(kih[:, :, a, :], KI.rearrange("p (c k) -> p c k", c=KC), ACT.Copy, scale=c["pair"][:, a:a + 1])
                    ins.then_inc(kih_done.sem, 1)
                    project_q(0)
                    act.wait_ge(h1_ready.sem, h1_ready.at(b, 1))
                    act.activation(h1[:, :], H1, ACT.Relu, bias=c["b1"][:, :]).then_inc(h1_done.sem, 1)
                    act.wait_ge(vi_ready.sem, vi_ready.at(b, 1))
                    act.activation(vi[0][:, :, :, 0:HD], VI.rearrange("p (k h d) -> p k h d", k=2, h=HEADS), ACT.Copy).then_inc(vi_hi.sem, 1)
                    act.wait_ge(hp_done.sem, hp_done.at(b, 1))
                    act.activation(hph[:, :], hp[:, :], ACT.Copy).then_inc(hph_done.sem, 1)
                    act.wait_ge(comp_ready.sem, comp_ready.at(b, 1))
                    for k in range(KC):
                        ins = act.activation(comp[:, k, :], CM[:, k * POOL:(k + 1) * POOL], ACT.Identity, bias=c["b2"][:, k:k + 1])
                    ins.then_inc(comp_done.sem, 1)
                    act.wait_ge(comp_done.sem, comp_done.at(b, 1))
                    act.activation(ch[:, :, :, :], comp[:, :, :].unsqueeze(2).broadcast_to([P, KC, 2, POOL]), ACT.Copy).then_inc(ch_done.sem, 1)
                    act.wait_ge(kc_ready.sem, kc_ready.at(b, 1))
                    act.activation(kchr[:, :, :].rearrange("p c k -> p (c k)"), KCP, ACT.Copy).then_inc(kch_done.sem, 1)
                    act.wait_ge(vi_mid.sem, vi_mid.at(b, 1))
                    act.activation(vi[1][:, :, :, 0:HD], vir[0][:, :, :].rearrange("p k (h d) -> p k h d", h=HEADS), ACT.Copy).then_inc(vi_hi.sem, 1)
                    act.wait_ge(vi_mid.sem, vi_mid.at(b, 2))
                    act.activation(vi[2][:, :, :, 0:HD], vir[1][:, :, :].rearrange("p k (h d) -> p k h d", h=HEADS), ACT.Copy).then_inc(vi_hi.sem, 1)
                    for i in range(3):
                        act.wait_ge(vc_mid.sem, vc_mid.at(b, i + 1))
                        act.activation(vc[i][:, :, 0:HD], vcr[i % 2][:, :].rearrange("p (h d) -> p h d", h=HEADS), ACT.Copy).then_inc(vc_hi.sem, 1)

                    for n in range(-1, UNITS + 5):
                        u = n + 1
                        if u < UNITS:
                            heads = 4 if u < INIT_UNITS else HEADS
                            act.wait_ge(mt_ready.sem, mt_ready.at(b, u + 1))
                            act.activation(mts[u % 2][0:heads, :], MT[0:heads, :], ACT.Copy, scale=-1.0).then_inc(mts_done.sem, 1)
                        if 0 <= n < UNITS:
                            for i in range(2):
                                act.wait_ge(t_ready.sem, t_ready.at(b, 2 * n + i + 1))
                                act.activation(pth[:, 512 * i:512 * i + 512], ps_t[i][:, :], ACT.Copy).then_inc(pth_done.sem, 1)
                        if u < UNITS:
                            act.wait_ge(sh_ready.sem, sh_ready.at(b, u + 1))
                            act.activation(prob[u % 2][:, :], ps_s[u % 2][:, :], ACT.Exp, scale=float(HD) ** -0.5).then_inc(exp_done.sem, 1)
                        k = block_at(n)
                        if k is not None:
                            project_q(k)
                        t = tile_of(n - 3)
                        if t is not None:
                            act.wait_ge(xt_ready.sem, xt_ready.at(b, t + 1))
                            if tile_of(n - 1) is not None:
                                act.wait_ge(ot_ready.sem, ot_ready.at(b, tile_of(n - 1) + 1))
                            act.activation(x1h[t % 2][:, :, :].rearrange("p c q -> p (c q)"), X1T, ACT.Copy).then_inc(x1h_done.sem, 1)
                        t = tile_of(n - 1)
                        if t is not None:
                            act.wait_ge(ot_ready.sem, ot_ready.at(b, t + 1))
                            act.activation(oth[:, :, :].rearrange("p c q -> p (c q)"), TURN, ACT.Copy).then_inc(oth_done.sem, 1)
                        k = block_at(n + 2)
                        if k is not None:
                            split_x(k)
                        g = group_done(n, 4)
                        if g is not None:
                            act.wait_ge(ld_done.sem, ld_done.at(b, g + 1))
                            act.activation(lex[:, :, :], ld[:, :, :], ACT.Exp).then_inc(ex_done.sem, 1)

            @block.tensor
            def _(pe):
                wq, wk, wv, wo = c["wq"], c["wk"], c["wv"], c["wo"]
                with pe.Fori(0, B) as b:
                    def x_split(k):
                        pe.wait_ge(xh_done.sem, xh_done.at(b, k + 1))
                        pe.wait_ge(xl_done.sem, xl_done.at(b, k + 1))

                    def project_q(k):
                        x_split(k)
                        for m in range(KC):
                            for kk in range(KC):
                                ins = mm_split(pe, ps_t[1][:, m * 256:(m + 1) * 256],
                                               wq[0][:, kk, m * P:(m + 1) * P], wq[1][:, kk, m * P:(m + 1) * P],
                                               xh[k % 2][:, kk, :], xl[k % 2][:, kk, :], kk == 0, kk == KC - 1)
                        ins.then_inc(q_ready.sem, 1)

                    def scores(u):
                        out = ps_s[u % 2]
                        if u < INIT_UNITS:
                            t, g = u // 4, u % 4
                            q = slice(P * t, P * t + P)
                            for i in range(2):
                                pair = 2 * g + i
                                m, rr = pair // 4, slice(32 * (pair % 4), 32 * (pair % 4) + 32)
                                o_ = out[:, 512 * i:512 * i + 512]
                                kh = kih[rr, m, :, :].rearrange("p a k -> p (a k)")
                                kl = kil[rr, m, :, :].rearrange("p a k -> p (a k)")
                                mm_split(pe, o_, qh[0][rr, m, q], ql[0][rr, m, q], kh, kl, True, False)
                            for i in range(2):
                                ins = pe.matmul(out[:, 512 * i:512 * i + 512], c["ident_r"][:, :], c["causal"][t][:, :],
                                                start=False, stop=True)
                        else:
                            t = u - INIT_UNITS + 2
                            k, q = t // 2, slice(P * (t % 2), P * (t % 2) + P)
                            for m in range(KC):
                                o_ = out[:, 512 * m:512 * m + 512]
                                kh = kmh[:, m, :, :].rearrange("p h k -> p (h k)")
                                kl = kml[:, m, :, :].rearrange("p h k -> p (h k)")
                                ins = mm_split(pe, o_, qh[k % 2][:, m, q], ql[k % 2][:, m, q], kh, kl, True, True)
                        ins.then_inc(s_ready.sem, 1)

                    x_split(0)
                    for m in range(KC):
                        for kk in range(KC):
                            ins = mm_split(pe, KI[:, m * 256:(m + 1) * 256],
                                           wk[0][:, kk, m * P:(m + 1) * P], wk[1][:, kk, m * P:(m + 1) * P],
                                           xh[0][:, kk, :], xl[0][:, kk, :], kk == 0, kk == KC - 1)
                    ins.then_inc(ki_ready.sem, 1)
                    for kk in range(KC):
                        ins = mm_split(pe, H1, c["w1"][0][:, kk, :], c["w1"][1][:, kk, :],
                                       xh[0][:, kk, :], xl[0][:, kk, :], kk == 0, kk == KC - 1)
                    ins.then_inc(h1_ready.sem, 1)
                    project_q(0)
                    for m in range(2):
                        for kk in range(KC):
                            ins = mm_split(pe, VI[:, m * 256:(m + 1) * 256],
                                           xh[0][:, kk, m * P:(m + 1) * P], xl[0][:, kk, m * P:(m + 1) * P],
                                           wv[0][:, kk, :], wv[1][:, kk, :], kk == 0, kk == KC - 1)
                    ins.then_inc(vi_ready.sem, 1)
                    pe.wait_ge(hph_done.sem, hph_done.at(b, 1))
                    pe.wait_ge(hpl_done.sem, hpl_done.at(b, 1))
                    for m in range(KC):
                        ins = mm_split(pe, CM[:, m * POOL:(m + 1) * POOL],
                                       c["w2"][0][:, m * P:(m + 1) * P], c["w2"][1][:, m * P:(m + 1) * P],
                                       hph[:, :], hpl[:, :], True, True)
                    ins.then_inc(comp_ready.sem, 1)
                    pe.wait_ge(ch_done.sem, ch_done.at(b, 1))
                    pe.wait_ge(cl_done.sem, cl_done.at(b, 1))
                    for m in range(KC):
                        for kk in range(KC):
                            ins = mm_split(pe, KCP[:, m * POOL:(m + 1) * POOL],
                                           wk[0][:, kk, m * P:(m + 1) * P], wk[1][:, kk, m * P:(m + 1) * P],
                                           ch[:, kk, 0, :], cl[:, kk, 0, :], kk == 0, kk == KC - 1)
                    for kk in range(KC):
                        ins = mm_split(pe, VCP,
                                       ch[:, kk, :, :].rearrange("p a k -> p (a k)"), cl[:, kk, :, :].rearrange("p a k -> p (a k)"),
                                       wv[0][:, kk, :], wv[1][:, kk, :], kk == 0, kk == KC - 1)
                    ins.then_inc(kc_ready.sem, 1)
                    pe.wait_ge(kih_done.sem, kih_done.at(b, 1))
                    pe.wait_ge(kil_done.sem, kil_done.at(b, 1))
                    pe.wait_ge(vi_hi.sem, vi_hi.at(b, 1))
                    pe.wait_ge(vi_mid.sem, vi_mid.at(b, 1))
                    pe.wait_ge(qh_done.sem, qh_done.at(b, 1))
                    pe.wait_ge(ql_done.sem, ql_done.at(b, 1))

                    def turn_rows(n):
                        t = tile_of(n - 3)
                        if t is not None:
                            pe.wait_ge(x1_done.sem, x1_done.at(b, t + 1))
                        t1, t3 = tile_of(n - 1), tile_of(n - 3)
                        if t1 is not None or t3 is not None:
                            k = block_at(n)
                            if k is not None:
                                pe.wait_ge(qh_done.sem, qh_done.at(b, k + 1))
                                pe.wait_ge(ql_done.sem, ql_done.at(b, k + 1))
                            if turned_early(n):
                                pe.wait_ge(pth_done.sem, pth_done.at(b, 2 * n + 2))
                                pe.wait_ge(ptl_done.sem, ptl_done.at(b, 2 * n + 2))
                            if n >= UNITS:
                                pe.wait_ge(x1l_done.sem, x1l_done.at(b, t3))
                                pe.wait_ge(otl_done.sem, otl_done.at(b, min(n - UNITS, 1) + TILES - 1))
                        if t3 is not None:
                            for m in range(KC):
                                ins = pe.transpose(X1T[:, m * P:(m + 1) * P],
                                                   rows[(t3 // 4) % 2][:, t3 % 4, m * P:(m + 1) * P], c["ident"][:, :])
                            ins.then_inc(xt_ready.sem, 1)
                        if t1 is not None:
                            pe.wait_ge(o_done.sem, o_done.at(b, last_unit(t1) + 1))
                            for m in range(KC):
                                ins = pe.transpose(TURN[:, m * P:(m + 1) * P],
                                                   o[t1 % 2][:, 8 * m:8 * m + 8, :].rearrange("p h d -> p (h d)"), c["ident"][:, :])
                            ins.then_inc(ot_ready.sem, 1)

                    def routed_read(n):
                        if group_done(n, 4) is not None:
                            pe.wait_ge(lg_done.sem, lg_done.at(b, group_done(n, 4) + 1))
                        if group_done(n, 5) is not None:
                            pe.wait_ge(base_done.sem, base_done.at(b, group_done(n, 5) + 1))

                    def turn_probs(n, i):
                        t = tile_of(n - 4)
                        if i and t is not None:
                            pe.wait_ge(x1h_done.sem, x1h_done.at(b, t + 1))
                            pe.wait_ge(x1l_done.sem, x1l_done.at(b, t + 1))
                        t = tile_of(n - 2)
                        if i and t is not None:
                            pe.wait_ge(oth_done.sem, oth_done.at(b, t + 1))
                            pe.wait_ge(otl_done.sem, otl_done.at(b, t + 1))
                        for j in range(4):
                            ins = pe.transpose(ps_t[i][:, P * j:P * j + P],
                                               prob[n % 2][:, 512 * i + P * j:512 * i + P * j + P], c["ident"][:, :])
                        ins.then_inc(t_ready.sem, 1)

                    for n in range(-2, UNITS + 5):
                        u = n + 1
                        k = block_at(n - 1)
                        if k is not None:
                            pe.wait_ge(qh_done.sem, qh_done.at(b, k + 1))
                            pe.wait_ge(ql_done.sem, ql_done.at(b, k + 1))
                        if 0 <= n < UNITS:
                            pe.wait_ge(exp_done.sem, exp_done.at(b, n + 1))
                        if 0 <= n < UNITS:
                            t = tile_of(n - 3)
                            if t is not None:
                                pe.wait_ge(r_done.sem, r_done.at(b, t + 1))
                            turn_probs(n, 0)
                        if 0 <= u < UNITS:
                            heads = 4 if u < INIT_UNITS else HEADS
                            pe.wait_ge(max_done.sem, max_done.at(b, u + 1))
                            routed_read(n - 1)
                            pe.transpose(MT[0:heads, :], mx[u % 2][:, 0:heads], c["ident"][:, :]).then_inc(mt_ready.sem, 1)
                        if 0 <= n < UNITS:
                            turn_probs(n, 1)
                        if 0 <= u < UNITS:
                            pe.wait_ge(mts_done.sem, mts_done.at(b, u + 1))
                            sel = c["sel4"] if u < INIT_UNITS else c["sel16"]
                            for i in range(2):
                                ins = pe.matmul(ps_s[u % 2][:, 512 * i:512 * i + 512], mts[u % 2][0:heads, :],
                                                sel[0:heads, 512 * i:512 * i + 512], start=False, stop=True,
                                                skip_group_check=True)
                            ins.then_inc(sh_ready.sem, 1)
                        if n + 2 < UNITS:
                            if n + 2 == 1:
                                pe.wait_ge(kcl_done.sem, kcl_done.at(b, 1))
                                pe.wait_ge(vc_mid.sem, vc_mid.at(b, 1))
                            if n + 2 == INIT_UNITS:
                                pe.wait_ge(kmh_done.sem, kmh_done.at(b, 1))
                                pe.wait_ge(kml_done.sem, kml_done.at(b, 1))
                            scores(n + 2)
                        k = block_at(n)
                        if k is not None:
                            pe.wait_ge(pth_done.sem, pth_done.at(b, 2 * n + 2))
                            pe.wait_ge(ptl_done.sem, ptl_done.at(b, 2 * n + 2))
                            project_q(k)
                        t = tile_of(n - 2)
                        if t is not None:
                            pe.wait_ge(oth_done.sem, oth_done.at(b, t + 1))
                            pe.wait_ge(otl_done.sem, otl_done.at(b, t + 1))
                            if n < UNITS:
                                pe.wait_ge(pth_done.sem, pth_done.at(b, 2 * n + 1))
                                pe.wait_ge(ptl_done.sem, ptl_done.at(b, 2 * n + 1))
                            else:
                                pe.wait_ge(r_done.sem, r_done.at(b, t))
                            for kk in range(KC):
                                ins = mm_split(pe, PROJ, oth[:, kk, :], otl[:, kk, :], wo[0][:, kk, :], wo[1][:, kk, :],
                                               kk == 0, kk == KC - 1)
                            ins.then_inc(wo_ready.sem, 1)
                        if turned_early(n):
                            turn_rows(n)
                        g = group_done(n, 5)
                        t = tile_of(n - 4)
                        if (g is not None or t is not None) and not 0 <= u < UNITS:
                            routed_read(n - 1)
                        if t is not None:
                            pe.wait_ge(x1h_done.sem, x1h_done.at(b, t + 1))
                            pe.wait_ge(x1l_done.sem, x1l_done.at(b, t + 1))
                            if t % 4 == 0:
                                pe.wait_ge(lg_done.sem, lg_done.at(b, t // 4))
                            for kk in range(KC):
                                pe.matmul(LG[:, t % 4, :, :].rearrange("p a e -> p (a e)"), x1h[t % 2][:, kk, :], c["wg"][:, kk, :],
                                          start=kk == 0, stop=False)
                                ins = pe.matmul(LG[:, t % 4, 0, :], x1l[t % 2][:, kk, :], c["wg"][:, kk, 0:EXPERTS],
                                                start=False, stop=kk == KC - 1)
                            ins.then_inc(lg_ready.sem, 1)
                        if g is not None:
                            pe.wait_ge(oh_done.sem, oh_done.at(b, g + 1))
                            pe.wait_ge(lg_done.sem, lg_done.at(b, g + 1))
                            for j in range(4):
                                pe.matmul(PF[:, 8 * j:8 * j + 8], c["before"][:, :], oh[:, j, :], start=True, stop=j == 0)
                                for i in range(j):
                                    pe.matmul(PF[:, 8 * j:8 * j + 8], c["all"][:, :], oh[:, i, :], start=False, stop=i == j - 1)
                            for j in range(4):
                                ins = pe.matmul(TOT, c["all"][:, :], oh[:, j, :], start=j == 0, stop=j == 3)
                            ins.then_inc(pf_ready.sem, 1)
                        if 0 <= n < UNITS:
                            pe.wait_ge(pth_done.sem, pth_done.at(b, 2 * n + 2))
                            pe.wait_ge(ptl_done.sem, ptl_done.at(b, 2 * n + 2))
                            pe.wait_ge(o_done.sem, o_done.at(b, n))
                            if n == 0:
                                pe.wait_ge(vi_hi.sem, vi_hi.at(b, 3))
                            if n == INIT_UNITS:
                                pe.wait_ge(vc_hi.sem, vc_hi.at(b, 3))
                            for j in range(8):
                                blk = slice(P * j, P * j + P)
                                if n < INIT_UNITS:
                                    h = 4 * (n % 4) + j // 2
                                    out, val = OUT[:, VW * h:VW * h + VW], [v[:, j % 2, h, :] for v in vi]
                                    first, last = j % 2 == 0, j % 2 == 1
                                else:
                                    out = OUT[:, 2 * VW * j:2 * VW * j + 2 * VW]
                                    val = [v[:, 2 * j:2 * j + 2, :].rearrange("p h d -> p (h d)") for v in vc]
                                    first = last = True
                                pe.matmul(out, pth[:, blk], val[0], start=first, stop=False)
                                pe.matmul(out, pth[:, blk], val[1], start=False, stop=False)
                                pe.matmul(out, pth[:, blk], val[2], start=False, stop=False)
                                pe.matmul(out, ptl[:, blk], val[0], start=False, stop=False)
                                ins = pe.matmul(out, ptl[:, blk], val[1], start=False, stop=last)
                            ins.then_inc(pv_ready.sem, 1)
                        if not turned_early(n):
                            turn_rows(n)

            @block.vector
            def _(dve):
                with dve.Fori(0, B) as b:
                    def project_q(k):
                        dve.wait_ge(qh_done.sem, qh_done.at(b, k + 1))
                        dve.tensor_tensor(ql[k % 2][:, :, :].rearrange("p c q -> p (c q)"), ps_t[1][:, :],
                                          f32(qh[k % 2][:, :, :].rearrange("p c q -> p (c q)")), SUB).then_inc(ql_done.sem, 1)

                    dve.wait_ge(kih_done.sem, kih_done.at(b, 1))
                    for a in range(2):
                        ins = dve.scalar_tensor_tensor(out=kil[:, :, a, :], in0=KI.rearrange("p (c k) -> p c k", c=KC),
                                                       scalar=c["pair"][:, a:a + 1], in1=f32(kih[:, :, a, :]), op0=MUL, op1=SUB)
                    ins.then_inc(kil_done.sem, 1)
                    project_q(0)
                    dve.wait_ge(h1_done.sem, h1_done.at(b, 1))
                    dve.tensor_reduce(hp[:, :], h1[:, :].rearrange("p (k a) -> p k a", a=CTX // POOL), AX.X, ADD).then_inc(hp_sum.sem, 1)
                    dve.wait_ge(hp_sum.sem, hp_sum.at(b, 1))
                    dve.tensor_scalar(hp[:, :], hp[:, :], float(POOL) / CTX, None, MUL).then_inc(hp_done.sem, 1)
                    dve.wait_ge(hph_done.sem, hph_done.at(b, 1))
                    dve.wait_ge(hp_done.sem, hp_done.at(b, 1))
                    dve.tensor_tensor(hpl[:, :], hp[:, :], f32(hph[:, :]), SUB).then_inc(hpl_done.sem, 1)
                    dve.wait_ge(vi_hi.sem, vi_hi.at(b, 1))
                    dve.tensor_tensor(vir[0][:, :, :].rearrange("p k (h d) -> p (k h) d", h=HEADS),
                                      VI.rearrange("p (k d) -> p k d", d=HD),
                                      vi[0][:, :, :, 0:HD].rearrange("p k h d -> p (k h) d"), SUB).then_inc(vi_mid.sem, 1)
                    dve.wait_ge(ch_done.sem, ch_done.at(b, 1))
                    dve.tensor_tensor(cl[:, :, :, :], comp[:, :, :].unsqueeze(2).broadcast_to([P, KC, 2, POOL]),
                                      f32(ch[:, :, :, :]), SUB).then_inc(cl_done.sem, 1)
                    dve.wait_ge(kch_done.sem, kch_done.at(b, 1))
                    dve.tensor_tensor(kcl[:, :, :].rearrange("p c k -> p (c k)"), KCP,
                                      f32(kchr[:, :, :].rearrange("p c k -> p (c k)")), SUB).then_inc(kcl_done.sem, 1)
                    dve.tensor_tensor(kmh[:, :, :, :], f32(kchr[:, :, :]).unsqueeze(2).broadcast_to([P, KC, 8, POOL]),
                                      c["head"][:, :].unsqueeze(1).unsqueeze(3).broadcast_to([P, KC, 8, POOL]), MUL
                                      ).then_inc(kmh_done.sem, 1)
                    dve.wait_ge(vi_hi.sem, vi_hi.at(b, 2))
                    dve.wait_ge(vi_mid.sem, vi_mid.at(b, 1))
                    dve.tensor_tensor(vir[1][:, :, :].rearrange("p k (h d) -> p (k h) d", h=HEADS),
                                      vir[0][:, :, :].rearrange("p k (h d) -> p (k h) d", h=HEADS),
                                      vi[1][:, :, :, 0:HD].rearrange("p k h d -> p (k h) d"), SUB).then_inc(vi_mid.sem, 1)
                    dve.wait_ge(kcl_done.sem, kcl_done.at(b, 1))
                    dve.tensor_tensor(vcr[0][:, :].rearrange("p (h d) -> p h d", h=HEADS), VCP.rearrange("p (h d) -> p h d", h=HEADS),
                                      c["half"][:, :].unsqueeze(2).broadcast_to([P, HEADS, HD]), MUL).then_inc(vc_mid.sem, 1)
                    for i in range(2):
                        dve.wait_ge(vc_hi.sem, vc_hi.at(b, i + 1))
                        dve.wait_ge(vc_mid.sem, vc_mid.at(b, i + 1))
                        dve.tensor_tensor(vcr[(i + 1) % 2][:, :].rearrange("p (h d) -> p h d", h=HEADS),
                                          vcr[i][:, :].rearrange("p (h d) -> p h d", h=HEADS), vc[i][:, :, 0:HD], SUB
                                          ).then_inc(vc_mid.sem, 1)

                    def low_rows(n):
                        t = tile_of(n - 3)
                        if t is not None:
                            dve.wait_ge(x1h_done.sem, x1h_done.at(b, t + 1))
                            if tile_of(n - 1) is not None:
                                dve.wait_ge(oth_done.sem, oth_done.at(b, tile_of(n - 1) + 1))
                            dve.tensor_tensor(x1l[t % 2][:, :, :].rearrange("p c q -> p (c q)"), X1T,
                                              f32(x1h[t % 2][:, :, :].rearrange("p c q -> p (c q)")), SUB).then_inc(x1l_done.sem, 1)
                        t = tile_of(n - 1)
                        if t is not None:
                            dve.wait_ge(oth_done.sem, oth_done.at(b, t + 1))
                            dve.tensor_tensor(otl[:, :, :].rearrange("p c q -> p (c q)"), TURN,
                                              f32(oth[:, :, :].rearrange("p c q -> p (c q)")), SUB).then_inc(otl_done.sem, 1)

                    for n in range(-2, UNITS + 5):
                        if 0 <= n < UNITS:
                            for i in range(2):
                                dve.wait_ge(pth_done.sem, pth_done.at(b, 2 * n + i + 1))
                                dve.tensor_tensor(ptl[:, 512 * i:512 * i + 512], ps_t[i][:, :], pth[:, 512 * i:512 * i + 512], SUB
                                                  ).then_inc(ptl_done.sem, 1)
                        u = n + 2
                        if u < UNITS:
                            heads, keys = (4, CTX) if u < INIT_UNITS else (HEADS, POOL)
                            dve.wait_ge(s_ready.sem, s_ready.at(b, u + 1))
                            dve.tensor_reduce(mx[u % 2][:, 0:heads], ps_s[u % 2][:, :].rearrange("p (h k) -> p h k", k=keys), AX.X, MAXOP
                                              ).then_inc(max_done.sem, 1)
                        g = group_done(n, 4)
                        if g is not None:
                            dve.wait_ge(lg_ready.sem, lg_ready.at(b, 4 * g + 4))
                            dve.tensor_tensor(lga[:, :, :], LG[:, :, 0, :], c["bg"][:, :].unsqueeze(1).broadcast_to([P, 4, EXPERTS]), ADD
                                              ).then_inc(lga_done.sem, 1)
                            dve.wait_ge(lga_done.sem, lga_done.at(b, g + 1))
                            dve.tensor_tensor(lg[:, :, :], LG[:, :, 1, :], lga[:, :, :], ADD).then_inc(lg_done.sem, 1)
                        g = group_done(n, 5)
                        if g is not None:
                            full = [P, 4, EXPERTS]
                            dve.wait_ge(ids_done.sem, ids_done.at(b, 0))
                            if g:
                                dve.wait_ge(base_done.sem, base_done.at(b, g))
                            dve.wait_ge(oh_done.sem, oh_done.at(b, g + 1))
                            dve.wait_ge(pf_ready.sem, pf_ready.at(b, g + 1))
                            dve.tensor_tensor(pf[:, :, :], PF.rearrange("p (j e) -> p j e", j=4),
                                              c["base"][:, :].unsqueeze(1).broadcast_to(full), ADD).then_inc(base_read.sem, 1)
                            dve.wait_ge(base_read.sem, base_read.at(b, g + 1))
                            dve.tensor_tensor(c["base"][:, :], c["base"][:, :], TOT, ADD).then_inc(base_done.sem, 1)
                        k = block_at(n)
                        if k is not None:
                            project_q(k)
                        t = tile_of(n - 2)
                        if t is not None:
                            dve.wait_ge(wo_ready.sem, wo_ready.at(b, t + 1))
                            if t % 4 == 0:
                                dve.wait_ge(rows_got[t // 4 % 2].sem, rows_got[t // 4 % 2].at(b, 16 * (t // 8 + 1)))
                            dve.tensor_tensor(r[t % 2][:, :], PROJ, rows_in[(t // 4) % 2][:, t % 4, :], ADD).then_inc(r_done.sem, 1)
                        if turned_early(n):
                            low_rows(n)
                        t = tile_of(n - 2)
                        if t is not None:
                            dve.wait_ge(r_done.sem, r_done.at(b, t + 1))
                            dve.bn_stats(stats[:, :], r[t % 2][:, :]).then_inc(st_done.sem, 1)
                            dve.wait_ge(st_done.sem, st_done.at(b, t + 1))
                            dve.nop(nofuse=True)
                            dve.bn_aggr(mv[t % 2][:, :], stats[:, :]).then_inc(mv_done.sem, 1)
                        if 0 <= n < UNITS:
                            hs = slice(4 * (n % 4), 4 * (n % 4) + 4) if n < INIT_UNITS else slice(0, HEADS)
                            heads = hs.stop - hs.start
                            out = OUT.rearrange("p (h d) -> p h d", d=VW)
                            dve.wait_ge(pv_ready.sem, pv_ready.at(b, n + 1))
                            dve.wait_ge(o_done.sem, o_done.at(b, n))
                            dve.reciprocal(rs[:, hs], out[:, hs, HD:VW].rearrange("p h a -> p (h a)")).then_inc(rs_done.sem, 1)
                            dve.wait_ge(rs_done.sem, rs_done.at(b, n + 1))
                            tt = n // 4 if n < INIT_UNITS else n - INIT_UNITS + 2
                            if tt >= 2:
                                dve.wait_ge(ot_ready.sem, ot_ready.at(b, tt - 1))
                            dve.tensor_tensor(o[tt % 2][:, hs, :], out[:, hs, 0:HD], rs[:, hs].unsqueeze(2).broadcast_to([P, heads, HD]), MUL
                                              ).then_inc(o_done.sem, 1)
                        if not turned_early(n):
                            low_rows(n)
                        g = group_done(n, 4)
                        if g is not None:
                            full = [P, 4, EXPERTS]
                            dve.wait_ge(lg_done.sem, lg_done.at(b, g + 1))
                            dve.tensor_reduce(lmax[:, :], lg[:, :, :], AX.X, MAXOP).then_inc(lm_done.sem, 1)
                            dve.wait_ge(lm_done.sem, lm_done.at(b, g + 1))
                            dve.tensor_tensor(ld[:, :, :], lg[:, :, :], lmax[:, :].unsqueeze(2).broadcast_to(full), SUB).then_inc(ld_done.sem, 1)
                            dve.tensor_tensor(key[:, :, :], lg[:, :, :], lmax[:, :].unsqueeze(2).broadcast_to(full), ALU.is_equal
                                              ).then_inc(key_done.sem, 1)
                            dve.wait_ge(key_done.sem, key_done.at(b, 3 * g + 1))
                            dve.tensor_tensor(key2[:, :, :], key[:, :, :], c["order"][:, :].unsqueeze(1).broadcast_to(full), MUL
                                              ).then_inc(key_done.sem, 1)
                            dve.wait_ge(key_done.sem, key_done.at(b, 3 * g + 2))
                            dve.tensor_reduce(mkey[:, :], key2[:, :, :], AX.X, MAXOP).then_inc(key_done.sem, 1)
                            dve.wait_ge(key_done.sem, key_done.at(b, 3 * g + 3))
                            dve.tensor_tensor(oh[:, :, :], key2[:, :, :], mkey[:, :].unsqueeze(2).broadcast_to(full), ALU.is_equal
                                              ).then_inc(oh_done.sem, 1)
                        g = group_done(n, 5)
                        if g is not None:
                            dve.tensor_tensor(pf2[:, :, :], pf[:, :, :], oh[:, :, :], MUL).then_inc(sel_done.sem, 1)
                            dve.wait_ge(ex_done.sem, ex_done.at(b, g + 1))
                            dve.tensor_reduce(lsum[:, :], lex[:, :, :], AX.X, ADD).then_inc(lsum_done.sem, 1)
                            dve.wait_ge(sel_done.sem, sel_done.at(b, g + 1))
                            with nc.allow_low_precision(reason="whole numbers below 2**24"):
                                dve.tensor_reduce(pos[g % 2][:, :], pf2[:, :, :], AX.X, ADD).then_inc(pos_done.sem, 1)
                            dve.wait_ge(lsum_done.sem, lsum_done.at(b, g + 1))
                            dve.reciprocal(rows[g % 2][:, :, D:D + 1].rearrange("p j a -> p (j a)"), lsum[:, :]).then_inc(row_done.sem, 1)
                            dve.tensor_copy(rows[g % 2][:, :, D + 1:D + 2].rearrange("p j a -> p (j a)"), c["ids"][:, 4 * g:4 * g + 4]
                                            ).then_inc(row_done.sem, 1)
                    dve.wait_ge(row_done.sem, row_done.at(b, 2 * GROUPS))
                    dve.tensor_scalar(c["ids"][:, :], c["ids"][:, :], float(S), None, ADD).then_inc(ids_done.sem, 1)


def const_table():
    p = np.arange(P)
    k = {}
    k["ident"] = np.eye(P)
    k["before"] = (p[:, None] < p[None, :]) * 1.0
    for t in range(2):
        hidden = (np.arange(CTX)[None, :] > (p + P * t)[:, None]) * HIDDEN_NEG
        k[f"causal{t}"] = np.concatenate([hidden, hidden], 1)
    k["sel4"] = (p[:, None] == (np.arange(1024) // CTX)[None, :]) * 1.0
    k["sel16"] = (p[:, None] == (np.arange(1024) // POOL)[None, :]) * 1.0
    k["half"] = ((p // 64)[:, None] == (np.arange(HEADS) % 2)[None, :]) * 1.0
    k["head"] = ((p // HD)[:, None] == np.arange(8)[None, :]) * 1.0
    k["pair"] = ((p // HD % 2)[:, None] == np.arange(2)[None, :]) * 1.0
    k["order"] = np.broadcast_to(EXPERTS - np.arange(EXPERTS), (P, EXPERTS))
    k["ids"] = p[:, None] + P * np.arange(TILES)[None, :]
    k["base"] = np.broadcast_to(CAP * np.arange(EXPERTS), (P, EXPERTS))
    k["lane"] = p[:, None]
    k["rowsel"] = (p[:, None] == np.arange(2)[None, :]) * 1.0
    k["mhalf"] = np.full((P, 1), -0.5)
    k["eps"] = np.full((P, 1), EPS)
    k["later"] = (p[None, :] > p[:, None]) * MASKED
    k["slots"] = np.broadcast_to(np.arange(TABLE), (P, TABLE))
    k["caps"] = np.broadcast_to(CAP * np.arange(EXPERTS), (P, EXPERTS))
    at, n = {}, 0
    for name, v in k.items():
        at[name] = (n, v.shape[1])
        n += v.shape[1]
    return np.ascontiguousarray(np.concatenate([v.astype(np.float32) for v in k.values()], 1)), at


PLAIN = ("half", "head", "pair", "order", "ids")
SHARED = ("base", "mhalf", "eps", "ident", "lane", "rowsel", "slots", "caps", "later")
TABLE = 80


def setup_layer0(nc, ctx, dr, c, const_at):
    def keep(name, shape, dt):
        return ctx.enter_context(nc.sbuf_tensor("k_" + name, shape, dt))

    names = ["wq", "wk", "wv", "wo"]
    for w in names:
        c[w] = [keep(w + x, [P, KC, D], F32R) for x in "hl"]
    c["w1"] = [keep("w1" + x, [P, KC, P], F32R) for x in "hl"]
    c["w2"] = [keep("w2" + x, [P, D], F32R) for x in "hl"]
    c["wg"] = keep("wg", [P, KC, 2 * EXPERTS], F32R)
    c["b1"], c["b2"], c["bg"] = keep("b1", [P, 1], F32), keep("b2", [P, KC], F32), keep("bg", [P, EXPERTS], F32)
    for name in PLAIN:
        c[name] = keep(name, [P, const_at[name][1]], F32)
    c["ident_r"] = keep("ident_r", [P, P], F32R)
    c["causal"] = [keep(f"causal{t}", [P, 2 * CTX], F32R) for t in range(2)]
    c["sel4"], c["sel16"] = keep("sel4", [4, 1024], F32R), keep("sel16", [HEADS, 1024], F32R)
    c["before"], c["all"] = keep("before", [P, P], BF16), keep("all", [P, P], BF16)
    loaded = nc.alloc_semaphore("w_loaded")
    high = nc.alloc_semaphore("w_high")

    with ExitStack() as tmp:
        def stage(name, shape):
            return tmp.enter_context(nc.sbuf_tensor("s_" + name, shape, F32))

        ncol = sum(v[1] for v in const_at.values())
        table = stage("table", [P, ncol])
        raws = [(c[w], stage(w, [P, KC, D]), dr[w].rearrange("(c p) n -> p c n", p=P)) for w in names]
        raws.append((c["w1"], stage("w1", [P, KC, P]), dr["w1"].rearrange("(c p) n -> p c n", p=P)))
        raws.append((c["w2"], stage("w2", [P, D]), dr["w2"]))
        wg = stage("wg", [P, KC, EXPERTS])

        def col(name):
            a, w = const_at[name]
            return table[:, a:a + w]

        with nc.Block() as block:
            @block.sync
            def _(sp):
                sp.dma_start(table[:, :], dr["table"]).then_inc(loaded, 16)
                for _, raw, src in raws:
                    full = raw[:, :, :] if len(raw.shape) == 3 else raw[:, :]
                    sp.dma_start(full, src).then_inc(loaded, 16)
                sp.dma_start(wg[:, :, :], dr["wg"].rearrange("(c p) e -> p c e", p=P)).then_inc(loaded, 16)
                sp.dma_start(c["b1"][:, :], dr["b1"].rearrange("(p a) -> p a", a=1)).then_inc(loaded, 16)
                sp.dma_start(c["b2"][:, :], dr["b2"]).then_inc(loaded, 16)
                sp.dma_start(c["bg"][:, :], dr["bg"].rearrange("(a e) -> a e", a=1).broadcast_to([P, EXPERTS])).then_inc(loaded, 16)

            all_loaded = 16 * (len(raws) + 5)

            @block.scalar
            def _(act):
                act.wait_ge(loaded, all_loaded)
                for pair, raw, _ in raws:
                    ix = (slice(None),) * len(raw.shape)
                    act.activation(pair[0][ix], raw[ix], ACT.Copy).then_inc(high, 1)
                act.activation(c["wg"][:, :, 0:EXPERTS], wg[:, :, :], ACT.Copy).then_inc(high, 1)
                act.activation(c["ident_r"][:, :], col("ident"), ACT.Copy)
                for t in range(2):
                    act.activation(c["causal"][t][:, :], col(f"causal{t}"), ACT.Copy)
                act.activation(c["sel4"][:, :], col("sel4")[0:4, :], ACT.Copy)
                act.activation(c["sel16"][:, :], col("sel16")[0:HEADS, :], ACT.Copy)

            @block.vector
            def _(dve):
                dve.memset(c["all"][:, :], 1.0)
                dve.wait_ge(loaded, all_loaded)
                dve.tensor_copy(c["before"][:, :], col("before"))
                for name in PLAIN + SHARED:
                    dve.tensor_copy(c[name][:, :], col(name))
                for i, (pair, raw, _) in enumerate(raws):
                    ix = (slice(None),) * len(raw.shape)
                    dve.wait_ge(high, i + 1)
                    dve.tensor_tensor(pair[1][ix], raw[ix], f32(pair[0][ix]), SUB)
                dve.wait_ge(high, len(raws) + 1)
                dve.tensor_tensor(c["wg"][:, :, EXPERTS:], wg[:, :, :], f32(c["wg"][:, :, 0:EXPERTS]), SUB)



HC = HID // P
STEPS = 72
AHEAD = 4
DVE_SHARE = 5
TURN_OF = 4


def setup_experts(nc, ctx, dr, c, raw_w, raw_got):
    def keep(name, shape, dt):
        return ctx.enter_context(nc.sbuf_tensor("m_" + name, shape, dt))

    m = {}
    m["w1"], m["w2"] = [[keep(f"w{i + 1}h", [P, EXPERTS * EXPERT_W], F32R), raw_w[i][1]] for i in range(2)]
    m["b1"] = keep("b1", [2, EXPERTS * HID], F32R)
    m["b2"] = keep("b2", [2, EXPERTS * D], F32R)
    m["ones"] = keep("ones", [2, P], F32R)
    m["table"] = keep("table", [P, 2, TABLE], I32)
    m["ident"], m["mhalf"], m["eps"] = c["ident"], c["mhalf"], c["eps"]
    biases = [(m["b1"], dr["mb1"], EXPERTS * HID), (m["b2"], dr["mb2"], EXPERTS * D)]
    weights = [(raw_w[i][0], m[f"w{i + 1}"], slice(e * EXPERT_W, (e + 1) * EXPERT_W)) for i in range(2) for e in range(EXPERTS)]
    m["later"] = weights[EXPERTS:]
    with ExitStack() as tmp:
        def stage(name, shape, dt=F32):
            return tmp.enter_context(nc.sbuf_tensor("t_" + name, shape, dt))

        def sem(name):
            return nc.alloc_semaphore("t_" + name)

        raw = [stage(f"raw{i}", [P, n // P]) for i, (_, _, n) in enumerate(biases)]
        parts = [[stage(f"part{x}{i}", [P, n // P], F32R) for x in "hl"] for i, (_, _, n) in enumerate(biases)]
        pad = stage("pad", [P, ROW])
        tail = stage("tail", [P, EXPERTS], I32)
        fill, tiles, tiles_x = stage("fill", [P, EXPERTS]), stage("tiles", [P, EXPERTS], I32), stage("tiles_x", [P, EXPERTS])
        tiles_f, ones8, cum = stage("tiles_f", [P, EXPERTS]), stage("ones8", [P, EXPERTS]), stage("cum", [P, EXPERTS])
        ind, ind2 = stage("ind", [P, TABLE, EXPERTS]), stage("ind2", [P, TABLE, EXPERTS])
        e_of, start = stage("e_of", [P, TABLE]), stage("start", [P, TABLE])
        row, row2 = stage("row", [P, TABLE]), stage("row2", [P, TABLE])
        got, high = sem("got"), sem("high")
        bias_parts = sem("bias_parts")
        pads, step, padded = sem("pads"), sem("table_step"), sem("padded")

        with nc.Block() as block:
            @block.sync
            def _(sp):
                for (_, src, n), given in zip(biases, raw):
                    sp.dma_start(given[:, :], src.rearrange("e (a n) -> (e a) n", n=n // P)).then_inc(got, 16)

            @block.scalar
            def _(act):
                act.wait_ge(raw_got, 16 * len(weights))
                for given, w, at in weights[:AHEAD]:
                    act.activation(w[0][:, at], given[:, at], ACT.Copy).then_inc(high, 1)
                act.wait_ge(got, 32)
                for given, pair in zip(raw, parts):
                    act.activation(pair[0][:, :], given[:, :], ACT.Copy).then_inc(high, 1)
                for given, w, at in weights[AHEAD:]:
                    act.activation(w[0][:, at], given[:, at], ACT.Copy).then_inc(high, 1)

            @block.gpsimd
            def _(pool):
                pool.wait_ge(pads, 3)
                for e in range(EXPERTS):
                    pool.indirect_dma_start(out=dr["routed"][:, :],
                                            out_offset=bass.IndirectOffsetOnAxis(ap=tail[:, e:e + 1], axis=0),
                                            in_=pad[:, :], in_offset=None).then_inc(padded, 16)
                pool.dma_start(dr["routed"][PAD_ROW:PAD_ROW + P, :], pad[:, :]).then_inc(padded, 16)
                pool.wait_ge(bias_parts, 2)
                for (w, _, n), pair in zip(biases, parts):
                    for i in range(2):
                        pool.dma_start(w[i:i + 1, :].rearrange("o (a n) -> o a n", n=n // P), pair[i][:, :]).then_inc(padded, 16)
                pool.wait_ge(padded, 16 * (EXPERTS + 1 + 4))

            @block.vector
            def _(dve):
                count = [0]

                def link(ins):
                    count[0] += 1
                    ins.then_inc(step, 1)
                    dve.wait_ge(step, count[0])

                dve.memset(pad[:, 0:D + 1], 0.0).then_inc(pads, 1)
                dve.memset(pad[:, D + 1:ROW], OFF_LIST).then_inc(pads, 1)
                link(dve.memset(ones8[:, :], 1.0))
                dve.tensor_scalar(m["ones"][:, :], c["ident"][0:2, :], 0.0, 1.0, MUL, ADD)
                dve.tensor_tensor(tail[:, :], c["base"][:, :], c["lane"][:, :].broadcast_to([P, EXPERTS]), ADD).then_inc(pads, 1)
                link(dve.tensor_tensor(fill[:, :], c["base"][:, :], c["caps"][:, :], SUB))
                link(dve.tensor_scalar(tiles_x[:, :], fill[:, :], 1.0 / P, (P - 1.0) / P - 0.5 + 0.5 / P, MUL, ADD))
                link(dve.tensor_copy(tiles[:, :], tiles_x[:, :]))
                link(dve.tensor_copy(tiles_f[:, :], tiles[:, :]))
                link(dve.tensor_tensor_scan(cum[:, :], ones8[:, :], tiles_f[:, :], 0.0, MUL, ADD))
                full = [P, TABLE, EXPERTS]
                link(dve.tensor_tensor(ind[:, :, :], c["slots"][:, :].unsqueeze(2).broadcast_to(full),
                                       cum[:, :].unsqueeze(1).broadcast_to(full), ALU.is_ge))
                link(dve.tensor_tensor(ind2[:, :, :], ind[:, :, :], tiles_f[:, :].unsqueeze(1).broadcast_to(full), MUL))
                link(dve.tensor_reduce(e_of[:, :], ind[:, :, :], AX.X, ADD))
                link(dve.tensor_reduce(start[:, :], ind2[:, :, :], AX.X, ADD))
                link(dve.tensor_tensor(row[:, :], c["slots"][:, :], start[:, :], SUB))
                link(dve.tensor_scalar(row2[:, :], row[:, :], float(P), None, MUL))
                link(dve.scalar_tensor_tensor(out=row[:, :], in0=e_of[:, :], scalar=float(CAP), in1=row2[:, :], op0=MUL, op1=ADD))
                dve.tensor_scalar(m["table"][:, 0, :], row[:, :], float(PAD_ROW), None, ALU.min)
                dve.tensor_scalar(m["table"][:, 1, :], e_of[:, :], float(EXPERTS - 1), None, ALU.min)
                dve.wait_ge(high, AHEAD + 2)
                for given, pair in zip(raw, parts):
                    dve.tensor_tensor(pair[1][:, :], given[:, :], f32(pair[0][:, :]), SUB).then_inc(bias_parts, 1)
                for i, (given, w, at) in enumerate(weights[:EXPERTS]):
                    if i >= AHEAD:
                        dve.wait_ge(high, i + 3)
                    dve.tensor_tensor(w[1][:, at], given[:, at], f32(w[0][:, at]), SUB)
    return m


def experts(nc, dr, m, raw_l1, raw_l1_got):
    N = TURN_OF
    TURNS = STEPS // N
    ctx = ExitStack()

    def sb(name, shape, dt):
        return ctx.enter_context(nc.sbuf_tensor("b_" + name, shape, dt))

    with ctx:
        xin = [sb(f"xin{i}", [P, ROW], F32) for i in range(N)]
        xh = [sb(f"xh{i}", [P, KC, P], F32R) for i in range(2)]
        xl = [sb(f"xl{i}", [P, KC, P], F32R) for i in range(2)]
        hid = [sb(f"hid{i}", [P, HID], F32) for i in range(2)]
        hth = [sb(f"hth{i}", [P, HC, P], F32R) for i in range(2)]
        htl = [sb(f"htl{i}", [P, HC, P], F32R) for i in range(2)]
        r = [sb(f"r{i}", [P, D], F32) for i in range(2)]
        stats, ve = sb("stats", [P, 6], F32), sb("ve", [P, 1], F32)
        mv = [sb(f"mv{i}", [P, 2], F32) for i in range(2)]
        rstd = [sb(f"rstd{i}", [P, 1], F32) for i in range(2)]
        x2 = [sb(f"x2{i}", [P, D], F32) for i in range(N)]
        ids = [sb(f"ids{i}", [P, 1], I32) for i in range(N)]
        ps_x = [ctx.enter_context(nc.psum_tensor(f"b_ps_x{i}", [P, 512], F32)) for i in range(1)]
        ps_h = [ctx.enter_context(nc.psum_tensor(f"b_ps_h{i}", [P, HID], F32)) for i in range(2)]
        ps_t = [ctx.enter_context(nc.psum_tensor(f"b_ps_t{i}", [P, HID], F32)) for i in range(2)]
        ps_y = [ctx.enter_context(nc.psum_tensor(f"b_ps_y{i}", [P, 512], F32)) for i in range(2)]

        def sig(name, per=N, credit=0):
            return Signal(nc, "b_" + name, per, credit)

        got = [sig(f"got{i}", 16) for i in range(N)]
        xt_ready, xh_done, xl_done = sig("xt_ready"), sig("xh_done"), sig("xl_done")
        h_ready, gelu_done = sig("h_ready"), sig("gelu_done")
        ht_ready, hth_done, htl_done = sig("ht_ready"), sig("hth_done"), sig("htl_done")
        y_ready, r_done, st_done, mv_done = sig("y_ready"), sig("r_done", N, 4), sig("st_done"), sig("mv_done")
        ve_done, rstd_done = sig("ve_done"), sig("rstd_done")
        x2_done = sig("x2_done")
        w2_low = nc.alloc_semaphore("b_w2_low")
        sent = [sig(f"sent{i}", 16) for i in range(N)]

        def low_w2(eng, chunks):
            for given, w, at in chunks:
                eng.tensor_tensor(w[1][:, at], given[:, at], f32(w[0][:, at]), SUB).then_inc(w2_low, 1)

        def slot(eng, name, j):
            k = 0 if name == "row" else 1
            return eng.value_load(m["table"][0:1, k, bass.ds(j, 1)], min_val=0, max_val=PAD_ROW if k == 0 else EXPERTS - 1)

        with nc.Block() as block:
            @block.vector
            def _(dve):
                dve.sem_inc(r_done.sem, 4)

        with nc.Block() as block:
            @block.sync
            def _(sp):
                def load(it, a, j):
                    sp.wait_ge(r_done.sem, r_done.at(it, a - N + 1))
                    row = slot(sp, "row", j)
                    sp.dma_start(xin[a % N][:, :], dr["routed"][bass.ds(row, P), :]).then_inc(got[a % N].sem, 16)

                for a in range(3):
                    load(0, a, a)
                for name, w in raw_l1.items():
                    sp.dma_start(w[0][:, :, :], dr[name].rearrange("(k p) n -> p k n", p=P)).then_inc(raw_l1_got, 16)
                with sp.Fori(0, TURNS) as it:
                    for a in range(3, 3 + N):
                        load(it, a, it * N + a)
                for a in range(3):
                    sp.wait_ge(got[a].sem, 16 * (TURNS + 1))

            @block.tensor
            def _(pe):
                w1, w2 = m["w1"], m["w2"]

                def turn_x(it, a, first=False):
                    pe.wait_ge(got[a % N].sem, got[a % N].at(it, 16 * (a // N + 1)))
                    if not first:
                        pe.wait_ge(xh_done.sem, xh_done.at(it, a))
                        pe.wait_ge(xl_done.sem, xl_done.at(it, a))
                    for k in range(KC):
                        ins = pe.transpose(ps_x[0][:, k * P:(k + 1) * P], xin[a % N][:, k * P:(k + 1) * P], m["ident"][:, :])
                    ins.then_inc(xt_ready.sem, 1)

                def hidden(it, a, e):
                    pe.wait_ge(xh_done.sem, xh_done.at(it, a + 1))
                    pe.wait_ge(xl_done.sem, xl_done.at(it, a + 1))
                    out = ps_h[a % 2][:, :]
                    pe.matmul(out, m["ones"][:, :], m["b1"][:, bass.ds(e * HID, HID)], start=True, stop=False)
                    for k in range(KC):
                        at = bass.ds(e * (KC * HID) + k * HID, HID)
                        ins = mm_split(pe, out, xh[a % 2][:, k, :], xl[a % 2][:, k, :], w1[0][:, at], w1[1][:, at], False, k == KC - 1)
                    ins.then_inc(h_ready.sem, 1)

                def turn_h(it, a):
                    pe.wait_ge(gelu_done.sem, gelu_done.at(it, a + 1))
                    for k in range(HC):
                        ins = pe.transpose(ps_t[a % 2][:, k * P:(k + 1) * P], hid[a % 2][:, k * P:(k + 1) * P], m["ident"][:, :])
                    ins.then_inc(ht_ready.sem, 1)

                def output(it, a, e):
                    pe.wait_ge(hth_done.sem, hth_done.at(it, a + 1))
                    pe.wait_ge(htl_done.sem, htl_done.at(it, a + 1))
                    pe.wait_ge(r_done.sem, r_done.at(it, a - 1))
                    out = ps_y[a % 2][:, 0:D]
                    pe.matmul(out, m["ones"][:, :], m["b2"][:, bass.ds(e * D, D)], start=True, stop=False)
                    for k in range(HC):
                        at = bass.ds(e * (HC * D) + k * D, D)
                        ins = mm_split(pe, out, hth[a % 2][:, k, :], htl[a % 2][:, k, :], w2[0][:, at], w2[1][:, at], False, k == HC - 1)
                    ins.then_inc(y_ready.sem, 1)

                turn_x(0, 0, True)
                turn_x(0, 1)
                hidden(0, 0, slot(pe, "expert", 0))
                pe.wait_ge(w2_low, EXPERTS)
                with pe.Fori(0, TURNS) as it:
                    for a in range(N):
                        turn_h(it, a)
                        turn_x(it, a + 2)
                        hidden(it, a + 1, slot(pe, "expert", it * N + (a + 1)))
                        output(it, a, slot(pe, "expert", it * N + a))

            @block.scalar
            def _(act):
                def high_x(it, a):
                    act.wait_ge(xt_ready.sem, xt_ready.at(it, a + 1))
                    act.activation(xh[a % 2][:, :, :].rearrange("p c q -> p (c q)"), ps_x[0][:, 0:D], ACT.Copy).then_inc(xh_done.sem, 1)

                def gelu(it, a):
                    act.wait_ge(h_ready.sem, h_ready.at(it, a + 1))
                    act.activation(hid[a % 2][:, :], ps_h[a % 2][:, :], ACT.Gelu).then_inc(gelu_done.sem, 1)

                high_x(0, 0)
                high_x(0, 1)
                gelu(0, 0)
                with act.Fori(0, TURNS) as it:
                    for a in range(N):
                        act.wait_ge(ht_ready.sem, ht_ready.at(it, a + 1))
                        act.activation(hth[a % 2][:, :, :].rearrange("p c q -> p (c q)"), ps_t[a % 2][:, :], ACT.Copy).then_inc(hth_done.sem, 1)
                        high_x(it, a + 2)
                        gelu(it, a + 1)

            @block.vector
            def _(dve):
                def low_x(it, a):
                    dve.wait_ge(xh_done.sem, xh_done.at(it, a + 1))
                    dve.tensor_tensor(xl[a % 2][:, :, :].rearrange("p c q -> p (c q)"), ps_x[0][:, 0:D],
                                      f32(xh[a % 2][:, :, :].rearrange("p c q -> p (c q)")), SUB).then_inc(xl_done.sem, 1)

                def norm(it, a, at):
                    dve.wait_ge(rstd_done.sem, rstd_done.at(it, a + 1))
                    dve.tensor_scalar(x2[at][:, :], r[a % 2][:, :], mv[a % 2][:, 0:1], rstd[a % 2][:, :], SUB, MUL).then_inc(x2_done.sem, 1)

                def turn(it, peeled):
                    for a in range(N):
                        dve.wait_ge(hth_done.sem, hth_done.at(it, a + 1))
                        dve.tensor_tensor(htl[a % 2][:, :, :].rearrange("p c q -> p (c q)"), ps_t[a % 2][:, :],
                                          f32(hth[a % 2][:, :, :].rearrange("p c q -> p (c q)")), SUB).then_inc(htl_done.sem, 1)
                        if not (peeled and a == 0):
                            norm(it, a - 1, (a - 1) % N)
                        low_x(it, a + 2)
                        if not peeled:
                            dve.wait_ge(sent[a].sem, sent[a].at(it, 0))
                        dve.tensor_copy(ids[a][:, :], xin[a][:, D + 1:ROW])
                        dve.wait_ge(y_ready.sem, y_ready.at(it, a + 1))
                        dve.scalar_tensor_tensor(out=r[a % 2][:, :], in0=ps_y[a % 2][:, 0:D], scalar=xin[a % N][:, D:D + 1],
                                                 in1=xin[a % N][:, 0:D], op0=MUL, op1=ADD).then_inc(r_done.sem, 1)
                        dve.wait_ge(r_done.sem, r_done.at(it, a + 1))
                        dve.bn_stats(stats[:, :], r[a % 2][:, :]).then_inc(st_done.sem, 1)
                        dve.wait_ge(st_done.sem, st_done.at(it, a + 1))
                        dve.nop(nofuse=True)
                        dve.bn_aggr(mv[a % 2][:, :], stats[:, :]).then_inc(mv_done.sem, 1)

                low_w2(dve, m["later"][0:2])
                low_x(0, 0)
                low_w2(dve, m["later"][2:3])
                low_x(0, 1)
                low_w2(dve, m["later"][3:DVE_SHARE])
                turn(0, True)
                with dve.Fori(1, TURNS) as it:
                    turn(it, False)
                norm(TURNS, -1, N - 1)

            @block.gpsimd
            def _(pool):
                def send(it, a, at):
                    pool.wait_ge(x2_done.sem, x2_done.at(it, a + 1))
                    pool.nop(nofuse=True)
                    pool.indirect_dma_start(out=dr["x2"][:, :], out_offset=bass.IndirectOffsetOnAxis(ap=ids[at][:, :], axis=0),
                                            in_=x2[at][:, :], in_offset=None, bounds_check=T - 1, oob_is_err=False
                                            ).then_inc(sent[at].sem, 16)

                def turn(it, peeled):
                    for a in range(N):
                        pool.wait_ge(mv_done.sem, mv_done.at(it, a + 1))
                        pool.tensor_tensor(ve[:, :], mv[a % 2][:, 1:2], m["eps"][:, :], ADD).then_inc(ve_done.sem, 1)
                        pool.wait_ge(ve_done.sem, ve_done.at(it, a + 1))
                        pool.tensor_tensor(rstd[a % 2][:, :], ve[:, :], m["mhalf"][:, :], ALU.pow).then_inc(rstd_done.sem, 1)
                        if not (peeled and a == 0):
                            send(it, a - 1, (a - 1) % N)

                low_w2(pool, m["later"][DVE_SHARE:])
                turn(0, True)
                with pool.Fori(1, TURNS) as it:
                    turn(it, False)
                send(TURNS, -1, N - 1)
                for i in range(N):
                    pool.wait_ge(sent[i].sem, 16 * TURNS)



FC = FF // P
GW = 4 * P
LIF_STEPS, BETA, THRESHOLD = 5, 0.9, 1.0


def quads(u):
    return u // 4 + 1


def quad_at(u, q):
    return sum(quads(v) for v in range(u)) + q


QUADS = quad_at(TILES, 0)

ORDER = [("attend", 0), ("attend", 1), ("attend", 2)]
for _g in range(GROUPS - 1):
    ORDER += [("prep", _g + 1), ("attend", 4 * _g + 3), ("attend", 4 * _g + 4), ("attend", 4 * _g + 5), ("feed", _g), ("attend", 4 * _g + 6)]
ORDER += [("attend", TILES - 1), ("prep", GROUPS), ("feed", GROUPS - 1)]
LAST_ORDER = [part for part in ORDER if part != ("prep", GROUPS)]
TURNED_IN = {ORDER[n][1]: ORDER[n + 1] for n in range(len(ORDER) - 1) if ORDER[n][0] == "attend" and ORDER[n + 1][0] != "attend"}
EXPS_IN_FEED = {part[1]: u for u, part in TURNED_IN.items() if part[0] == "feed"}
EXPS_BEHIND = 1
FED_BY = {u: sum(kind == "feed" for kind, _ in ORDER[:ORDER.index(("attend", u))]) for u in range(TILES)}
LIF_BESIDE = {3: (-1, [1]), 4: (-1, [2]), 7: (0, [1]), 8: (0, [2]), 11: (1, [1]), 12: (1, [2]), 14: (2, [1]), 15: (2, [2])}
LIF_BEHIND = {0: ("step", 3), 2: ("step", 4), 5: ("sum", 0), 6: ("moments", 0), 7: ("result", 0)}


def setup_layer1(nc, ctx, dr, c, raw_l1, raw_l1_got):
    def keep(name, shape, dt):
        return ctx.enter_context(nc.sbuf_tensor("l_" + name, shape, dt))

    m = {}
    for name, w in raw_l1.items():
        m[name] = [keep(name, list(w[0].shape), F32R), w[1]]
    m["ident"], m["mhalf"], m["eps"] = c["ident"], c["mhalf"], c["eps"]
    m["ident_r"], m["mask"] = keep("ident_r", [P, P], F32R), keep("mask", [P, P], F32R)
    m["R"] = [keep("R" + x, [P, KC, D], F32R) for x in "hl"]
    given = {**{name: w[0] for name, w in raw_l1.items()}, "R": keep("rawR", [P, KC, D], F32)}
    high = nc.alloc_semaphore("v_high")
    with nc.Block() as block:
        @block.sync
        def _(sp):
            sp.wait_ge(raw_l1_got, 16 * len(raw_l1))
            sp.dma_start(given["R"][:, :, :], dr["R"].rearrange("(k p) n -> p k n", p=P)).then_inc(raw_l1_got, 16)

        @block.scalar
        def _(act):
            act.wait_ge(raw_l1_got, 16 * len(raw_l1))
            for name in given:
                if name == "R":
                    act.wait_ge(raw_l1_got, 16 * (len(raw_l1) + 1))
                act.activation(m[name][0][:, :, :], given[name][:, :, :], ACT.Copy).then_inc(high, 1)
            act.activation(m["ident_r"][:, :], c["ident"][:, :], ACT.Copy)
            act.activation(m["mask"][:, :], c["later"][:, :], ACT.Copy)

        @block.vector
        def _(dve):
            for i, name in enumerate(given):
                dve.wait_ge(high, i + 1)
                dve.tensor_tensor(m[name][1][:, :, :], given[name][:, :, :], f32(m[name][0][:, :, :]), SUB)
    return m


def layer1(nc, dr, m):
    ctx = ExitStack()

    def sb(name, shape, dt):
        return ctx.enter_context(nc.sbuf_tensor("c_" + name, shape, dt))

    with ctx:
        x2 = [sb(f"x2{i}", [P, 4, D], F32) for i in range(GROUPS)]
        xh, xl = sb("xh", [P, KC, S], F32R), sb("xl", [P, KC, S], F32R)
        vh, vl = sb("vh", [P, TILES, D], F16), sb("vl", [P, TILES, D], F16)
        eh, el = sb("eh", [P, KC, GW], F32R), sb("el", [P, KC, GW], F32R)
        nmax, ssum = [sb(f"nmax{i}", [P, 1], F32) for i in range(2)], [sb(f"ssum{i}", [P, 1], F32) for i in range(2)]
        rinv = sb("rinv", [P, 1], F32)
        prob = [sb(f"prob{i}", [P, S], F32) for i in range(2)]
        pth, ptl = [sb(f"pth{i}", [P, GW], F16) for i in range(2)], [sb(f"ptl{i}", [P, GW], F16) for i in range(2)]
        r = [sb(f"r{i}", [P, D], F32) for i in range(2)]
        stats, mv = sb("stats", [P, 6], F32), [sb(f"mv{i}", [P, 2], F32) for i in range(2)]
        ve, rstd = sb("ve", [P, 1], F32), [sb(f"rstd{i}", [P, 1], F32) for i in range(2)]
        x3 = [sb(f"x3{i}", [P, 4, D], F32) for i in range(GROUPS)]
        th, tl = sb("th", [P, 2, KC, 2 * P], F32R), sb("tl", [P, 2, KC, 2 * P], F32R)
        rl = [sb(f"rl{i}", [P, GW], F32) for i in range(2)]
        sq = [sb(f"sq{i}", [P, GW], F32) for i in range(2)]
        hh, hl = [sb(f"hh{i}", [P, GW], F32R) for i in range(3)], [sb(f"hl{i}", [P, GW], F32R) for i in range(3)]
        y, drive, r4 = (sb(name, [P, 4 * D], F32) for name in ("y", "drive", "r4"))
        spk, cnt = sb("spk", [P, 4 * D], BF16), sb("cnt", [P, 4 * D], BF16)
        neg = [sb(f"neg{i}", [P, 4 * D], F32) for i in range(2)]
        fstats, fmv = sb("fstats", [P, 4, 6], F32), sb("fmv", [P, 4, 2], F32)
        fve, frstd = sb("fve", [P, 4], F32), sb("frstd", [P, 4], F32)
        fin = sb("fin", [P, 4, D], F32)

        ps_s = ctx.enter_context(nc.psum_tensor("c_ps_s", [P, S], F32))
        ps_t = [ctx.enter_context(nc.psum_tensor(f"c_ps_t{i}", [P, GW], F32)) for i in range(2)]
        ps_o = ctx.enter_context(nc.psum_tensor("c_ps_o", [P, GW], F32))
        ps_m = ctx.enter_context(nc.psum_tensor("c_ps_m", [P, GW], F32))

        def sig(name, per, credit=0):
            return Signal(nc, "c_" + name, per, credit)

        got = [sig(f"got{i}", 16) for i in range(GROUPS)]
        xt_ready, xh_done, xl_done = sig("xt_ready", 2 * GROUPS), sig("xh_done", 2 * GROUPS), sig("xl_done", 2 * GROUPS)
        vh_done, vl_done = sig("vh_done", GROUPS), sig("vl_done", GROUPS)
        e_ready, eh_done, el_done = sig("e_ready", 2 * GROUPS), sig("eh_done", 2 * GROUPS), sig("el_done", 2 * GROUPS)
        s_ready, max_done, exp_done = sig("s_ready", TILES), sig("max_done", TILES), sig("exp_done", TILES)
        t_ready, pth_done, ptl_done = sig("t_ready", QUADS), sig("pth_done", QUADS), sig("ptl_done", QUADS)
        o_ready, rinv_done, r_done = sig("o_ready", TILES), sig("rinv_done", TILES), sig("r_done", TILES, TILES)
        st_done, mv_done, ve_done, rstd_done, x3_done = (sig(n, TILES) for n in ("st_done", "mv_done", "ve_done", "rstd_done", "x3_done"))
        tt_ready, th_done, tl_done = sig("tt_ready", 2 * GROUPS), sig("th_done", 2 * GROUPS), sig("tl_done", 2 * GROUPS)
        h_ready, rl_done, sq_done = sig("h_ready", FC * GROUPS), sig("rl_done", FC * GROUPS), sig("sq_done", FC * GROUPS)
        hh_done, hl_done = sig("hh_done", FC * GROUPS), sig("hl_done", FC * GROUPS)
        y_ready, y_done = sig("y_ready", GROUPS), sig("y_done", 2 * GROUPS, 2)
        drive_done, neg_done = sig("drive_done", LIF_STEPS * GROUPS), sig("neg_done", 4 * GROUPS)
        spk_done, cnt_done = sig("spk_done", 3 * GROUPS), sig("cnt_done", 4 * GROUPS)
        r4_done, fst_done, fmv_done, fve_done, frstd_done, fin_done = (sig(n, GROUPS) for n in ("r4_done", "fst_done", "fmv_done", "fve_done", "frstd_done", "fin_done"))
        out_done = sig("out_done", 16 * GROUPS)

        with nc.Block() as block:
            @block.vector
            def _(dve):
                dve.sem_inc(r_done.sem, TILES)
                dve.sem_inc(y_done.sem, 2)

        def bank(name):
            return {"m": ps_m, "t0": ps_t[0], "t1": ps_t[1]}[name]

        def turn_banks(kind, i):
            if (kind, i) == ("feed", GROUPS - 1):
                return "t0", "t1"
            if (kind, i) == ("prep", 0):
                return "m", "t1"
            u = next(t for t, part in TURNED_IN.items() if part == (kind, i))
            return "m", f"t{quads(u) % 2}"

        def batches(eng, turn):
            turn(0, True, False)
            with eng.Fori(1, B - 1) as b:
                turn(b, False, False)
            turn(B - 1, False, True)

        E_BANKS = ("t1", "m")

        with nc.Block() as block:
            @block.sync
            def _(sp):
                with sp.Fori(0, B) as b:
                    for g in range(GROUPS):
                        sp.wait_ge(r_done.sem, r_done.at(b, 4 * g + 4 - TILES))
                        sp.dma_start(x2[g][:, :, :], dr["x2"][bass.ds(b * S + g * GW, GW), :].rearrange("(j p) d -> p j d", p=P)
                                     ).then_inc(got[g].sem, 16)

            @block.gpsimd
            def _(pool):
                def deviation(b, u):
                    pool.wait_ge(mv_done.sem, mv_done.at(b, u + 1))
                    pool.tensor_tensor(ve[:, :], mv[u % 2][:, 1:2], m["eps"][:, :], ADD).then_inc(ve_done.sem, 1)
                    pool.wait_ge(ve_done.sem, ve_done.at(b, u + 1))
                    pool.tensor_tensor(rstd[u % 2][:, :], ve[:, :], m["mhalf"][:, :], ALU.pow).then_inc(rstd_done.sem, 1)

                def split_values(b, i):
                    x = x2[i % GROUPS]
                    at = slice(4 * (i % GROUPS), 4 * (i % GROUPS) + 4)
                    pool.wait_ge(got[i % GROUPS].sem, got[i % GROUPS].at(b, 16 * (i // GROUPS + 1)))
                    pool.wait_ge(xt_ready.sem, xt_ready.at(b, 2 * i + 1))
                    pool.nop(nofuse=True)
                    pool.tensor_copy(vh[:, at, :], x[:, :, :]).then_inc(vh_done.sem, 1)
                    pool.wait_ge(vh_done.sem, vh_done.at(b, i + 1))
                    pool.tensor_tensor(vl[:, at, :], x[:, :, :], vh[:, at, :], SUB).then_inc(vl_done.sem, 1)

                def spikes(b, g, k):
                    if k == 0:
                        pool.wait_ge(y_done.sem, y_done.at(b, 2 * g + 2))
                        pool.nop(nofuse=True)
                        pool.tensor_scalar(cnt[:, :], y[:, :], THRESHOLD, None, ALU.is_gt).then_inc(cnt_done.sem, 1)
                    else:
                        pool.wait_ge(neg_done.sem, neg_done.at(b, 4 * g + k))
                        pool.wait_ge(cnt_done.sem, cnt_done.at(b, 4 * g + k))
                        pool.nop(nofuse=True)
                        pool.tensor_scalar(spk[:, :], neg[k % 2][:, :], -THRESHOLD, None, ALU.is_lt).then_inc(spk_done.sem, 1)
                        pool.wait_ge(spk_done.sem, spk_done.at(b, 3 * g + k))
                        pool.tensor_tensor(cnt[:, :], cnt[:, :], spk[:, :], ADD).then_inc(cnt_done.sem, 1)

                def finish(b, g, first):
                    pool.wait_ge(fmv_done.sem, fmv_done.at(b, g + 1))
                    if not first:
                        pool.wait_ge(out_done.sem, out_done.at(b, 16 * g))
                    pool.tensor_tensor(fve[:, :], fmv[:, :, 1:2].rearrange("p j a -> p (j a)"), m["eps"][:, :].broadcast_to([P, 4]), ADD
                                       ).then_inc(fve_done.sem, 1)
                    pool.wait_ge(fve_done.sem, fve_done.at(b, g + 1))
                    pool.tensor_tensor(frstd[:, :], fve[:, :], m["mhalf"][:, :].broadcast_to([P, 4]), ALU.pow).then_inc(frstd_done.sem, 1)
                    pool.wait_ge(fin_done.sem, fin_done.at(b, g + 1))
                    pool.nop(nofuse=True)
                    pool.dma_start(dr["out"][bass.ds(b * S + g * GW, GW), :].rearrange("(j p) d -> p j d", p=P), fin[:, :, :]
                                   ).then_inc(out_done.sem, 16)

                def turn(b, first, last):
                    for kind, i in (LAST_ORDER if last else ORDER):
                        if kind == "attend":
                            part, group = TURNED_IN.get(i, (None, 0))
                            if part == "prep" and not (last and i == TILES - 1):
                                split_values(b, group)
                            deviation(b, i)
                            g, steps = LIF_BESIDE.get(i, (0, []))
                            if not (first and g < 0):
                                for k in steps:
                                    spikes(b, g, k - 1)
                        if kind == "feed" and not (first and i == 0):
                            spikes(b, i - 1, 2)
                            spikes(b, i - 1, 3)
                            finish(b, i - 1, first and i == 1)

                split_values(0, 0)
                batches(pool, turn)
                for k in range(4):
                    spikes(B - 1, GROUPS - 1, k)
                finish(B - 1, GROUPS - 1, False)
                pool.wait_ge(out_done.sem, 16 * GROUPS * B)

            @block.scalar
            def _(act):
                def high_p(b, u, q):
                    width = min(4, u + 1 - 4 * q) * P
                    act.wait_ge(t_ready.sem, t_ready.at(b, quad_at(u, q) + 1))
                    act.activation(pth[q % 2][:, 0:width], ps_t[q % 2][:, 0:width], ACT.Copy).then_inc(pth_done.sem, 1)

                def exps(b, u):
                    act.wait_ge(max_done.sem, max_done.at(b, u + 1))
                    w = P * (u % TILES + 1)
                    act.activation(prob[u % 2][:, 0:w], ps_s[:, 0:w], ACT.Exp, bias=nmax[u % 2][:, :], accum_out=ssum[u % 2][:, :]
                                   ).then_inc(exp_done.sem, 1)

                def high_turned(b, kind, i):
                    for a, name in enumerate(turn_banks(kind, i)):
                        if kind == "prep":
                            at = GW * (i % GROUPS) + 2 * P * a
                            act.wait_ge(xt_ready.sem, xt_ready.at(b, 2 * i + a + 1))
                            act.activation(xh[:, :, at:at + 2 * P], bank(name)[:, :].rearrange("p (k q) -> p k q", k=KC), ACT.Copy
                                           ).then_inc(xh_done.sem, 1)
                        else:
                            act.wait_ge(tt_ready.sem, tt_ready.at(b, 2 * i + a + 1))
                            act.activation(th[:, a, :, :].rearrange("p k q -> p (k q)"), bank(name)[:, :], ACT.Copy).then_inc(th_done.sem, 1)

                def high_e(b, i):
                    for a in range(2):
                        act.wait_ge(e_ready.sem, e_ready.at(b, 2 * i + a + 1))
                        act.activation(eh[:, a, :], bank(E_BANKS[a])[:, :], ACT.Copy).then_inc(eh_done.sem, 1)

                def turn(b, first, last):
                    for kind, i in (LAST_ORDER if last else ORDER):
                        if kind == "attend":
                            nq = quads(i)
                            turned = i in TURNED_IN and not (last and i == TILES - 1)
                            for q in range(nq):
                                if q == nq - 1 and nq >= 3 and i + 1 < TILES and not turned:
                                    exps(b, i + 1)
                                high_p(b, i, q)
                            if turned:
                                high_turned(b, *TURNED_IN[i])
                            if i + 1 < TILES and (turned or nq < 3) and i not in EXPS_IN_FEED.values():
                                exps(b, i + 1)
                        if kind == "prep":
                            high_e(b, i)
                        if kind == "feed":
                            if i == GROUPS - 1:
                                high_turned(b, "feed", i)
                                if not last:
                                    exps(b, TILES)
                            for f in range(FC):
                                n = FC * i + f
                                act.wait_ge(h_ready.sem, h_ready.at(b, n + 1))
                                act.activation(rl[f % 2][:, :], ps_t[f % 2][:, :], ACT.Relu).then_inc(rl_done.sem, 1)
                                act.wait_ge(rl_done.sem, rl_done.at(b, n + 1))
                                if f >= 2:
                                    act.wait_ge(hl_done.sem, hl_done.at(b, n - 1))
                                act.activation(sq[f % 2][:, :], rl[f % 2][:, :], ACT.Square).then_inc(sq_done.sem, 1)
                                act.wait_ge(sq_done.sem, sq_done.at(b, n + 1))
                                act.activation(hh[f % 3][:, :], sq[f % 2][:, :], ACT.Copy).then_inc(hh_done.sem, 1)
                                if f == EXPS_BEHIND and i in EXPS_IN_FEED:
                                    exps(b, EXPS_IN_FEED[i] + 1)
                            act.wait_ge(y_ready.sem, y_ready.at(b, i + 1))
                            if not (first and i == 0):
                                act.wait_ge(r4_done.sem, r4_done.at(b, i))
                            act.activation(y[:, 0:2 * D], ps_m[:, :], ACT.Copy).then_inc(y_done.sem, 1)
                            act.activation(y[:, 2 * D:4 * D], ps_o[:, :], ACT.Copy).then_inc(y_done.sem, 1)

                high_turned(0, "prep", 0)
                high_e(0, 0)
                exps(0, 0)
                batches(act, turn)

            @block.tensor
            def _(pe):
                def scores(b, u):
                    t = u % TILES
                    g, tile = t // 4, slice(P * (t % 4), P * (t % 4) + P)
                    for c in range(g + 1):
                        w = GW if c < g else P * (t % 4 + 1)
                        out = ps_s[:, GW * c:GW * c + w]
                        for k in range(KC):
                            keys = slice(GW * c, GW * c + w)
                            mm_split(pe, out, eh[:, k, tile], el[:, k, tile], xh[:, k, keys], xl[:, k, keys], k == 0, k == KC - 1 and c < g)
                    pe.matmul(ps_s[:, P * t:P * t + P], m["ident_r"][:, :], m["mask"][:, :], start=False, stop=True).then_inc(s_ready.sem, 1)

                def turn_p(b, u, q):
                    for j in range(min(4, u + 1 - 4 * q)):
                        at = P * (4 * q + j)
                        ins = pe.transpose(ps_t[q % 2][:, P * j:P * j + P], prob[u % 2][:, at:at + P], m["ident"][:, :])
                    ins.then_inc(t_ready.sem, 1)

                def values(b, u, q):
                    n = quad_at(u, q)
                    pe.wait_ge(pth_done.sem, pth_done.at(b, n + 1))
                    pe.wait_ge(ptl_done.sem, ptl_done.at(b, n + 1))
                    if q == 0:
                        pe.wait_ge(r_done.sem, r_done.at(b, u))
                        pe.wait_ge(y_done.sem, y_done.at(b, 2 * FED_BY[u]))
                    for j in range(min(4, u + 1 - 4 * q)):
                        t, blk = 4 * q + j, slice(P * j, P * j + P)
                        out = ps_o[:, 0:D]
                        pe.matmul(out, pth[q % 2][:, blk], vh[:, t, :], start=t == 0, stop=False)
                        pe.matmul(out, pth[q % 2][:, blk], vl[:, t, :], start=False, stop=False)
                        ins = pe.matmul(out, ptl[q % 2][:, blk], vh[:, t, :], start=False, stop=t == u)
                    if q == quads(u) - 1:
                        ins.then_inc(o_ready.sem, 1)

                def turn_inputs(kind, i, a, b):
                    src, ready = (x2[i % GROUPS], xt_ready) if kind == "prep" else (x3[i], tt_ready)
                    if kind == "prep" and a == 0:
                        pe.wait_ge(got[i % GROUPS].sem, got[i % GROUPS].at(b, 16 * (i // GROUPS + 1)))
                    if kind == "feed" and a == 0:
                        pe.wait_ge(x3_done.sem, x3_done.at(b, 4 * i + 4))
                    for j in range(2):
                        for k in range(KC):
                            ins = pe.transpose(bank(turn_banks(kind, i)[a])[:, 2 * P * k + P * j:2 * P * k + P * j + P],
                                               src[:, 2 * a + j, P * k:P * k + P], m["ident"][:, :])
                    ins.then_inc(ready.sem, 1)

                def project(b, i):
                    pe.wait_ge(xh_done.sem, xh_done.at(b, 2 * i + 2))
                    pe.wait_ge(xl_done.sem, xl_done.at(b, 2 * i + 2))
                    keys = slice(GW * (i % GROUPS), GW * (i % GROUPS) + GW)
                    for a in range(2):
                        for k in range(KC):
                            ins = mm_split(pe, bank(E_BANKS[a])[:, :], m["R"][0][:, k, P * a:P * a + P],
                                           m["R"][1][:, k, P * a:P * a + P], xh[:, k, keys], xl[:, k, keys], k == 0, k == KC - 1)
                        ins.then_inc(e_ready.sem, 1)

                def projected(b, i, a):
                    pe.wait_ge(eh_done.sem, eh_done.at(b, 2 * i + a + 1))
                    pe.wait_ge(el_done.sem, el_done.at(b, 2 * i + a + 1))

                def attend(b, u, last):
                    nq = quads(u)
                    behind_prep = u % 4 == 3
                    part = TURNED_IN.get(u) if not (last and u == TILES - 1) else None
                    pe.wait_ge(exp_done.sem, exp_done.at(b, u + 1))
                    turn_p(b, u, 0)
                    if nq > 1:
                        if behind_prep and u + 1 < TILES:
                            projected(b, (u + 1) // 4, 0)
                        turn_p(b, u, 1)
                    if behind_prep and u + 1 < TILES:
                        projected(b, (u + 1) // 4, 1)
                    if u + 1 < TILES:
                        scores(b, u + 1)
                    if u % 4 == 0:
                        pe.wait_ge(vl_done.sem, vl_done.at(b, u // 4 + 1))
                    for q in range(nq):
                        if part and q == max(nq - 2, 0):
                            pe.wait_ge(y_done.sem, y_done.at(b, 2 * FED_BY[u]))
                            turn_inputs(*part, 0, b)
                        if part and q == nq - 1:
                            turn_inputs(*part, 1, b)
                        values(b, u, q)
                        if q + 2 < nq:
                            turn_p(b, u, q + 2)

                def feed(b, i, last):
                    if i == GROUPS - 1:
                        turn_inputs("feed", i, 0, b)
                        if not last:
                            projected(b, GROUPS, 1)
                            scores(b, TILES)
                        turn_inputs("feed", i, 1, b)
                    pe.wait_ge(th_done.sem, th_done.at(b, 2 * i + 2))
                    pe.wait_ge(tl_done.sem, tl_done.at(b, 2 * i + 2))
                    for f in range(FC + 2):
                        if f < FC:
                            fs = slice(P * f, P * f + P)
                            if f >= 2:
                                pe.wait_ge(rl_done.sem, rl_done.at(b, FC * i + f - 1))
                            for k in range(KC):
                                ins = mm_split(pe, ps_t[f % 2][:, :], m["fcT"][0][:, k, fs], m["fcT"][1][:, k, fs],
                                               th[:, :, k, :], tl[:, :, k, :], k == 0, k == KC - 1)
                            ins.then_inc(h_ready.sem, 1)
                        if f == 2:
                            pe.wait_ge(r_done.sem, r_done.at(b, min(4 * i + 6, TILES)))
                        if f >= 2:
                            h, n = f - 2, FC * i + f - 1
                            pe.wait_ge(hh_done.sem, hh_done.at(b, n))
                            pe.wait_ge(hl_done.sem, hl_done.at(b, n))
                            for j in range(4):
                                tok = slice(P * j, P * j + P)
                                out = (ps_m if j < 2 else ps_o)[:, D * (j % 2):D * (j % 2) + D]
                                h_, l_ = hh[h % 3][:, tok], hl[h % 3][:, tok]
                                wh, wl = m["pjT"][0][:, h, :], m["pjT"][1][:, h, :]
                                pe.matmul(out, h_, wh, start=h == 0 and j % 2 == 0, stop=False, skip_group_check=True)
                                pe.matmul(out, h_, wl, start=False, stop=False, skip_group_check=True)
                                ins = pe.matmul(out, l_, wh, start=False, stop=h == FC - 1, skip_group_check=True)
                    ins.then_inc(y_ready.sem, 1)

                def turn(b, first, last):
                    for kind, i in (LAST_ORDER if last else ORDER):
                        if kind == "attend":
                            attend(b, i, last)
                        if kind == "prep":
                            if i == GROUPS:
                                pe.wait_ge(ptl_done.sem, ptl_done.at(b, QUADS))
                            project(b, i)
                            if i == GROUPS:
                                projected(b, i, 0)
                        if kind == "feed":
                            feed(b, i, last)

                turn_inputs("prep", 0, 0, 0)
                turn_inputs("prep", 0, 1, 0)
                project(0, 0)
                projected(0, 0, 1)
                scores(0, 0)
                batches(pe, turn)

            @block.vector
            def _(dve):
                def low_p(b, u, q):
                    n = quad_at(u, q)
                    width = min(4, u + 1 - 4 * q) * P
                    dve.wait_ge(pth_done.sem, pth_done.at(b, n + 1))
                    dve.tensor_tensor(ptl[q % 2][:, 0:width], ps_t[q % 2][:, 0:width], pth[q % 2][:, 0:width], SUB).then_inc(ptl_done.sem, 1)

                def maximum(b, u):
                    dve.wait_ge(s_ready.sem, s_ready.at(b, u + 1))
                    dve.tensor_reduce(nmax[u % 2][:, :], ps_s[:, 0:P * (u % TILES + 1)], AX.X, MAXOP, negate=True).then_inc(max_done.sem, 1)

                def low_turned(b, kind, i):
                    for a, name in enumerate(turn_banks(kind, i)):
                        if kind == "prep":
                            at = GW * (i % GROUPS) + 2 * P * a
                            dve.wait_ge(xh_done.sem, xh_done.at(b, 2 * i + a + 1))
                            dve.tensor_tensor(xl[:, :, at:at + 2 * P], bank(name)[:, :].rearrange("p (k q) -> p k q", k=KC),
                                              f32(xh[:, :, at:at + 2 * P]), SUB).then_inc(xl_done.sem, 1)
                        else:
                            dve.wait_ge(th_done.sem, th_done.at(b, 2 * i + a + 1))
                            dve.tensor_tensor(tl[:, a, :, :].rearrange("p k q -> p (k q)"), bank(name)[:, :],
                                              f32(th[:, a, :, :].rearrange("p k q -> p (k q)")), SUB).then_inc(tl_done.sem, 1)

                def low_e(b, i):
                    for a in range(2):
                        dve.wait_ge(eh_done.sem, eh_done.at(b, 2 * i + a + 1))
                        dve.tensor_tensor(el[:, a, :], bank(E_BANKS[a])[:, :], f32(eh[:, a, :]), SUB).then_inc(el_done.sem, 1)

                def normalise(b, u):
                    dve.wait_ge(rstd_done.sem, rstd_done.at(b, u + 1))
                    dve.tensor_scalar(x3[u // 4][:, u % 4, :], r[u % 2][:, :], mv[u % 2][:, 0:1], rstd[u % 2][:, :], SUB, MUL
                                      ).then_inc(x3_done.sem, 1)

                def lif(b, g, what, k):
                    if what == "step":
                        n = 4 * g + k
                        if k == 1:
                            dve.wait_ge(y_done.sem, y_done.at(b, 2 * g + 2))
                            dve.scalar_tensor_tensor(out=drive[:, :], in0=y[:, :], scalar=-BETA, in1=y[:, :], op0=MUL, op1=SUB
                                                     ).then_inc(drive_done.sem, 1)
                        else:
                            dve.wait_ge(neg_done.sem, neg_done.at(b, n - 1))
                            dve.scalar_tensor_tensor(out=drive[:, :], in0=neg[(k - 1) % 2][:, :], scalar=BETA, in1=y[:, :], op0=MUL, op1=SUB
                                                     ).then_inc(drive_done.sem, 1)
                        dve.wait_ge(drive_done.sem, drive_done.at(b, LIF_STEPS * g + k))
                        if k > 2:
                            dve.wait_ge(spk_done.sem, spk_done.at(b, 3 * g + k - 2))
                        if k == 1:
                            dve.scalar_tensor_tensor(out=neg[k % 2][:, :], in0=y[:, :], scalar=THRESHOLD, in1=drive[:, :], op0=ALU.is_gt, op1=ADD
                                                     ).then_inc(neg_done.sem, 1)
                        else:
                            dve.scalar_tensor_tensor(out=neg[k % 2][:, :], in0=neg[(k - 1) % 2][:, :], scalar=-THRESHOLD, in1=drive[:, :],
                                                     op0=ALU.is_lt, op1=ADD).then_inc(neg_done.sem, 1)
                    if what == "sum":
                        dve.wait_ge(neg_done.sem, neg_done.at(b, 4 * g + 4))
                        dve.wait_ge(cnt_done.sem, cnt_done.at(b, 4 * g + 4))
                        dve.scalar_tensor_tensor(out=drive[:, :], in0=neg[0][:, :], scalar=-THRESHOLD, in1=cnt[:, :], op0=ALU.is_lt, op1=ADD
                                                 ).then_inc(drive_done.sem, 1)
                        dve.wait_ge(drive_done.sem, drive_done.at(b, LIF_STEPS * (g + 1)))
                        dve.scalar_tensor_tensor(out=r4[:, :], in0=drive[:, :], scalar=1.0 / LIF_STEPS,
                                                 in1=x3[g % GROUPS][:, :, :].rearrange("p j d -> p (j d)"), op0=MUL, op1=ADD).then_inc(r4_done.sem, 1)
                    if what == "moments":
                        dve.wait_ge(r4_done.sem, r4_done.at(b, g + 1))
                        for j in range(4):
                            ins = dve.bn_stats(fstats[:, j, :], r4[:, D * j:D * j + D])
                        ins.then_inc(fst_done.sem, 1)
                        dve.wait_ge(fst_done.sem, fst_done.at(b, g + 1))
                        dve.nop(nofuse=True)
                        for j in range(4):
                            ins = dve.bn_aggr(fmv[:, j, :], fstats[:, j, :])
                        ins.then_inc(fmv_done.sem, 1)
                    if what == "result":
                        dve.wait_ge(frstd_done.sem, frstd_done.at(b, g + 1))
                        for j in range(4):
                            ins = dve.tensor_scalar(fin[:, j, :], r4[:, D * j:D * j + D], fmv[:, j, 0:1], frstd[:, j:j + 1], SUB, MUL)
                        ins.then_inc(fin_done.sem, 1)

                def output(b, u):
                    dve.wait_ge(exp_done.sem, exp_done.at(b, u + 1))
                    dve.reciprocal(rinv[:, :], ssum[u % 2][:, :]).then_inc(rinv_done.sem, 1)
                    dve.wait_ge(rinv_done.sem, rinv_done.at(b, u + 1))
                    dve.wait_ge(o_ready.sem, o_ready.at(b, u + 1))
                    dve.scalar_tensor_tensor(out=r[u % 2][:, :], in0=ps_o[:, 0:D], scalar=rinv[:, :], in1=x2[u // 4][:, u % 4, :],
                                             op0=MUL, op1=ADD).then_inc(r_done.sem, 1)
                    dve.wait_ge(r_done.sem, r_done.at(b, u + 1))
                    dve.bn_stats(stats[:, :], r[u % 2][:, :]).then_inc(st_done.sem, 1)
                    dve.wait_ge(st_done.sem, st_done.at(b, u + 1))
                    dve.nop(nofuse=True)
                    dve.bn_aggr(mv[u % 2][:, :], stats[:, :]).then_inc(mv_done.sem, 1)

                def turn(b, first, last):
                    for kind, i in (LAST_ORDER if last else ORDER):
                        if kind == "attend":
                            u, nq = i, quads(i)
                            turned = i in TURNED_IN and not (last and i == TILES - 1)
                            low_p(b, u, 0)
                            if nq > 1:
                                low_p(b, u, 1)
                            if u + 1 < TILES and not turned:
                                maximum(b, u + 1)
                            for q in range(2, nq):
                                low_p(b, u, q)
                            if turned:
                                low_turned(b, *TURNED_IN[i])
                                if u + 1 < TILES:
                                    maximum(b, u + 1)
                            g, steps = LIF_BESIDE.get(u, (0, []))
                            if not (first and g < 0):
                                for k in steps:
                                    lif(b, g, "step", k)
                            output(b, u)
                            normalise(b, u)
                        if kind == "prep":
                            low_e(b, i)
                        if kind == "feed":
                            if i == GROUPS - 1:
                                low_turned(b, "feed", i)
                                if not last:
                                    maximum(b, TILES)
                            for f in range(FC):
                                n = FC * i + f
                                dve.wait_ge(hh_done.sem, hh_done.at(b, n + 1))
                                dve.tensor_tensor(hl[f % 3][:, :], sq[f % 2][:, :], f32(hh[f % 3][:, :]), SUB).then_inc(hl_done.sem, 1)
                                if f in LIF_BEHIND and not (first and i == 0):
                                    lif(b, i - 1, *LIF_BEHIND[f])

                low_turned(0, "prep", 0)
                low_e(0, 0)
                maximum(0, 0)
                batches(dve, turn)
                for what, k in [("step", 1), ("step", 2), *LIF_BEHIND.values()]:
                    lif(B - 1, GROUPS - 1, what, k)


def model(nc, dr, const_at):
    dr["routed"] = nc.dram_tensor("routed", [PAD_ROW + P, ROW], F32, kind="Internal").ap()
    dr["x2"] = nc.dram_tensor("x2", [T, D], F32, kind="Internal").ap()
    c = {}
    raw_got, raw_l1_got = nc.alloc_semaphore("raw_got"), nc.alloc_semaphore("raw_l1_got")
    with ExitStack() as shared:
        raw_l1 = {name: raw_and_low(nc, shared, name, shape)
                  for name, shape in (("fcT", [P, KC, FF]), ("pjT", [P, FC, D]))}
        for name in SHARED:
            c[name] = shared.enter_context(nc.sbuf_tensor("g_" + name, [P, const_at[name][1]], F32))
        with ExitStack() as moe:
            raw_w = [raw_and_low(nc, moe, f"w{i + 1}", [P, EXPERTS * EXPERT_W]) for i in range(2)]
            with ExitStack() as ctx:
                setup_layer0(nc, ctx, dr, c, const_at)
                layer0_attention(nc, dr, c, raw_w, raw_got)
            with ExitStack() as ctx:
                m = setup_experts(nc, ctx, dr, c, raw_w, raw_got)
                experts(nc, dr, m, raw_l1, raw_l1_got)
        with ExitStack() as ctx:
            m = setup_layer1(nc, ctx, dr, c, raw_l1, raw_l1_got)
            layer1(nc, dr, m)


def kernel(**inputs):
    import concourse.bacc as bacc
    from concourse.bass_utils import run_bass_kernel_spmd

    nc = bacc.Bacc("TRN2", target_bir_lowering=False, num_devices=1)
    table, const_at = const_table()
    x = np.asarray(inputs["L0_attn_hidden_states"]).reshape(T, D)
    arrays = {
        "x": x, "xT": x.T.reshape(KC, P, T).transpose(1, 0, 2), "table": table,
        "wq": inputs["L0_attn_Wq"], "wk": inputs["L0_attn_Wk"], "wv": inputs["L0_attn_Wv"], "wo": inputs["L0_attn_Wo"],
        "w1": inputs["L0_attn_W1"], "b1": inputs["L0_attn_b1"], "w2": inputs["L0_attn_W2"],
        "b2": np.asarray(inputs["L0_attn_b2"]).reshape(KC, P).T, "wg": inputs["L0_ffn_Wg"], "bg": inputs["L0_ffn_bg"],
        "mw1": inputs["L0_ffn_W1"], "mb1": inputs["L0_ffn_b1"], "mw2": inputs["L0_ffn_W2"], "mb2": inputs["L0_ffn_b2"],
        "R": inputs["L1_attn_R"], "fcT": np.asarray(inputs["L1_ffn_W_fc"]).T, "pjT": np.asarray(inputs["L1_ffn_W_proj"]).T,
    }
    arrays = {f"in_{name}_dram": np.ascontiguousarray(a) for name, a in arrays.items()}
    dr = {name[3:-5]: nc.dram_tensor(name, a.shape, F32, kind="ExternalInput").ap() for name, a in arrays.items()}
    out = nc.dram_tensor("out_0_dram", [B, S, D], F32, kind="ExternalOutput").ap()
    dr["out"] = out.rearrange("b s d -> (b s) d")
    model(nc, dr, const_at)
    got = run_bass_kernel_spmd(nc, [arrays], core_ids=[0])
    return got.results[0]["out_0_dram"]
```
